# Optimizing a Trainium2 kernel written in Bass

```python
import numpy as np
import jax
import jax.numpy as jnp

def _softmax(x, axis=-1):
    return jax.nn.softmax(x, axis=axis)

def _gelu(x):
    return jax.nn.gelu(x, approximate=True)

def _silu(x):
    return jax.nn.silu(x)

def _sigmoid(x):
    return jax.nn.sigmoid(x)

def _layernorm(x, axis=-1, eps=1e-05):
    m = jnp.mean(x, axis=axis, keepdims=True)
    v = jnp.var(x, axis=axis, keepdims=True)
    return (x - m) / jnp.sqrt(v + eps)

def _scatter_add(tgt, idx, src, axis=0):
    return tgt.at[idx].add(src)

def _segment_sum(src, seg, n):
    return jax.ops.segment_sum(src, seg, n)
kernel_name = 'mk_flamingo_gated_d4_seqx_r8_c995bf'

def setup_inputs(seed: int=0):
    np.random.seed(seed)
    _w = jnp.asarray

    def _rec_inputs():
        import jax
        import jax.numpy as jnp
        _rk = jax.random.key(seed)
        x = 0.002226 + 0.9996 * jax.random.normal(jax.random.fold_in(_rk, 1), (8, 100, 128), jnp.float32)
        _lenS = 100 - jax.random.randint(jax.random.fold_in(_rk, 7), (8,), 0, max(1, 100 // 4) + 1, jnp.int32)
        _lenS2 = 1444 - jax.random.randint(jax.random.fold_in(_rk, 8), (8,), 0, max(1, 1444 // 4) + 1, jnp.int32)
        _ctx_1024P = jax.random.normal(jax.random.fold_in(_rk, 11), (8, 16, 128), jnp.float32)
        _ctx_1024c = jax.random.dirichlet(jax.random.fold_in(_rk, 511), 0.3 * jnp.ones((16,), jnp.float32), (8, 1444))
        _ctx_1024t = jnp.einsum('bsk,bkd->bsd', _ctx_1024c, _ctx_1024P)
        _ctx_1024t = _ctx_1024t * jax.lax.rsqrt(jnp.mean(jnp.square(_ctx_1024t)) + 1e-12) * 0.953939
        ctx_1024 = -0.000125008 + 0.999885 * (_ctx_1024t + 0.3 * jax.random.normal(jax.random.fold_in(_rk, 611), (8, 1444, 128), jnp.float32))
        fside_BxSxS2_0 = jax.random.uniform(jax.random.fold_in(_rk, 13), (8, 100, 1444), jnp.float32, 0.0, 1)
        fside_Bx16xSxS2_0 = 9.80324e-06 + 0.100009 * jax.random.normal(jax.random.fold_in(_rk, 15), (8, 16, 100, 1444), jnp.float32)
        fside_SxS2_0 = -2.64403e-05 + 0.100002 * jax.random.normal(jax.random.fold_in(_rk, 17), (100, 1444), jnp.float32)
        _validS = jnp.arange(100)[None, :] < _lenS[:, None]
        _validS2 = jnp.arange(1444)[None, :] < _lenS2[:, None]
        _causal = jnp.tril(jnp.ones((100, 100), dtype=bool))
        mask_BxS2_bk0 = jnp.logical_not(jnp.broadcast_to(_validS2[:, :], (8, 1444)))
        mask_BxSxS2_ik1 = jnp.where(jnp.broadcast_to(_validS2[:, None, :], (8, 100, 1444)), 1, 0).astype(jnp.int32)
        mask_BxS2_bf0 = jnp.logical_not(jnp.ones((8, 1444), dtype=bool))
        _g = jax.random.normal(jax.random.fold_in(_rk, 9001), (2, 4), jnp.float32)
        _g = jnp.sign(_g) * jnp.maximum(jnp.abs(_g), 1.0) + (_g == 0) * 1.0
        g_xattn = _g[0]
        g_ffn = _g[1]
        return (x, ctx_1024, fside_BxSxS2_0, fside_Bx16xSxS2_0, fside_SxS2_0, mask_BxS2_bk0, mask_BxSxS2_ik1, mask_BxS2_bf0, g_xattn, g_ffn)
    x, ctx_1024, fside_BxSxS2_0, fside_Bx16xSxS2_0, fside_SxS2_0, mask_BxS2_bk0, mask_BxSxS2_ik1, mask_BxS2_bf0, g_xattn, g_ffn = _rec_inputs()

    def _L0_xattn_setup():
        import jax, jax.numpy as jnp
        import numpy as np
        EPS = 1e-05

        def layer_norm(x, g, b):
            mu = jnp.mean(x, axis=-1, keepdims=True)
            var = jnp.mean((x - mu) ** 2, axis=-1, keepdims=True)
            return (x - mu) * jax.lax.rsqrt(var + EPS) * g + b
        key = jax.random.key(seed)
        ks = jax.random.split(key, 8)
        b, n, l, D = (8, 512, 64, 128)
        heads, dim_head = (16, 64)
        inner = heads * dim_head
        x = jax.random.normal(ks[0], (b, n, D), dtype=jnp.float32)
        latents = jax.random.normal(ks[1], (b, l, D), dtype=jnp.float32)
        mask = jax.random.randint(ks[2], (b, n), 0, 2) > 0
        Wq = jax.random.normal(ks[3], (D, inner), dtype=jnp.float32) * D ** (-0.5)
        Wkv = jax.random.normal(ks[4], (D, 2 * inner), dtype=jnp.float32) * D ** (-0.5)
        Wout = jax.random.normal(ks[5], (inner, D), dtype=jnp.float32) * inner ** (-0.5)
        g1 = jnp.ones((D,), jnp.float32)
        b1 = jnp.zeros((D,), jnp.float32)
        g2 = jnp.ones((D,), jnp.float32)
        b2 = jnp.zeros((D,), jnp.float32)
        return {'x': x, 'latents': latents, 'mask': mask, 'g1': g1, 'b1': b1, 'g2': g2, 'b2': b2, 'Wq': Wq, 'Wkv': Wkv, 'Wout': Wout}
    _L0_xattn_all = _L0_xattn_setup()
    _L0_xattn_in = {k: v for k, v in _L0_xattn_all.items() if k in ('g1', 'b1', 'g2', 'b2', 'Wq', 'Wkv', 'Wout')}
    del _L0_xattn_all

    def _L0_ffn_setup():
        import jax, jax.numpy as jnp
        import numpy as np
        D_MODEL = 128
        EXPERT_DIM = 64
        N_EXPERTS = 8
        TOP_K = 2

        def _sq_relu(h):
            return jnp.square(jax.nn.relu(h))
        key = jax.random.key(seed)
        ks = jax.random.split(key, 6)
        s = 0.02
        x = jax.random.normal(ks[0], (2, 256, D_MODEL), dtype=jnp.float32)
        Ws1 = jax.random.normal(ks[1], (D_MODEL, EXPERT_DIM), dtype=jnp.float32) * s
        Ws2 = jax.random.normal(ks[2], (EXPERT_DIM, D_MODEL), dtype=jnp.float32) * s
        W1 = jax.random.normal(ks[3], (N_EXPERTS, D_MODEL, EXPERT_DIM), dtype=jnp.float32) * s
        W2 = jax.random.normal(ks[4], (N_EXPERTS, EXPERT_DIM, D_MODEL), dtype=jnp.float32) * s
        Wr = jax.random.normal(ks[5], (D_MODEL, N_EXPERTS), dtype=jnp.float32) * s
        return {'x': x, 'Ws1': Ws1, 'Ws2': Ws2, 'W1': W1, 'W2': W2, 'Wr': Wr}
    _L0_ffn_all = _L0_ffn_setup()
    _L0_ffn_in = {k: v for k, v in _L0_ffn_all.items() if k in ('Ws1', 'Ws2', 'W1', 'W2', 'Wr')}
    del _L0_ffn_all

    def _L1_xattn_setup():
        import jax, jax.numpy as jnp
        import numpy as np
        NUM_HEADS = 16
        HIDDEN = 128
        B, S = (2, 256)

        def _split_heads(x, H):
            b, s, d = x.shape
            return x.reshape(b, s, H, d // H).transpose(0, 2, 1, 3)
        key = jax.random.key(seed)
        ks = jax.random.split(key, 14)
        D = HIDDEN
        scale = 1.0 / np.sqrt(D)
        inp = {'query': jax.random.normal(ks[0], (B, S, D), jnp.float32), 'key_in': jax.random.normal(ks[1], (B, S, D), jnp.float32), 'value': jax.random.normal(ks[2], (B, S, D), jnp.float32), 'group_prob': jax.random.uniform(ks[3], (B, S, S), jnp.float32), 'mask': jax.random.randint(ks[4], (B, S, S), 0, 2, jnp.int32), 'wq_k': jax.random.normal(ks[5], (D, D), jnp.float32) * scale, 'wq_b': jnp.zeros((D,), jnp.float32), 'wk_k': jax.random.normal(ks[6], (D, D), jnp.float32) * scale, 'wk_b': jnp.zeros((D,), jnp.float32), 'wv_k': jax.random.normal(ks[7], (D, D), jnp.float32) * scale, 'wv_b': jnp.zeros((D,), jnp.float32), 'wo_k': jax.random.normal(ks[8], (D, D), jnp.float32) * scale, 'wo_b': jnp.zeros((D,), jnp.float32)}
        return inp
    _L1_xattn_all = _L1_xattn_setup()
    _L1_xattn_in = {k: v for k, v in _L1_xattn_all.items() if k in ('wq_k', 'wq_b', 'wk_k', 'wk_b', 'wv_k', 'wv_b', 'wo_k', 'wo_b')}
    del _L1_xattn_all

    def _L1_ffn_setup():
        import jax, jax.numpy as jnp
        import numpy as np
        BLOCK = 16
        _GRID = jnp.array([0.0, 0.5, 1.0, 1.5, 2.0, 3.0, 4.0, 6.0], dtype=jnp.float32)
        _MID = jnp.array([0.25, 0.75, 1.25, 1.75, 2.5, 3.5, 5.0], dtype=jnp.float32)

        def fp4_quant_dequant(x):
            shape = x.shape
            xb = x.reshape(shape[:-1] + (shape[-1] // BLOCK, BLOCK))
            scale = jnp.max(jnp.abs(xb), axis=-1, keepdims=True) / 6.0
            scale = jnp.maximum(scale, jnp.float32(1e-12))
            xn = xb / scale
            idx = jnp.searchsorted(_MID, jnp.abs(xn))
            q = _GRID[idx] * jnp.sign(xn) * scale
            return q.reshape(shape)

        def fp4_linear(x, w):
            xq = fp4_quant_dequant(x)
            wq = fp4_quant_dequant(w)
            return jnp.einsum('bsk,nk->bsn', xq, wq)
        key = jax.random.key(seed)
        k1, k2, k3, k4 = jax.random.split(key, 4)
        H, I = (128, 352)
        x = jax.random.normal(k1, (4, 512, H), dtype=jnp.float32)
        w_gate = jax.random.normal(k2, (I, H), dtype=jnp.float32) * 0.02
        w_up = jax.random.normal(k3, (I, H), dtype=jnp.float32) * 0.02
        w_down = jax.random.normal(k4, (H, I), dtype=jnp.float32) * 0.02
        return {'x': x, 'w_gate': w_gate, 'w_up': w_up, 'w_down': w_down}
    _L1_ffn_all = _L1_ffn_setup()
    _L1_ffn_in = {k: v for k, v in _L1_ffn_all.items() if k in ('w_gate', 'w_up', 'w_down')}
    del _L1_ffn_all

    def _L2_xattn_setup():
        import jax, jax.numpy as jnp
        import numpy as np
        E = 128
        H = 16
        D = E // H
        key = jax.random.key(seed)
        ks = jax.random.split(key, 12)
        B, T, S = (2, 256, 256)
        inp = {'query': jax.random.normal(ks[0], (B, T, E), jnp.float32), 'key': jax.random.normal(ks[1], (B, S, E), jnp.float32), 'value': jax.random.normal(ks[2], (B, S, E), jnp.float32), 'spatial_bias': jax.random.normal(ks[3], (B, H, T, S), jnp.float32) * 0.1, 'directional_bias': jax.random.normal(ks[4], (B, H, T, S), jnp.float32) * 0.1, 'key_padding_mask': jnp.zeros((B, S), dtype=bool), 'attn_mask': jax.random.normal(ks[5], (T, S), jnp.float32) * 0.1, 'Wq': jax.random.normal(ks[6], (E, E), jnp.float32) / np.sqrt(E), 'bq': jnp.zeros((E,), jnp.float32), 'Wk': jax.random.normal(ks[7], (E, E), jnp.float32) / np.sqrt(E), 'bk': jnp.zeros((E,), jnp.float32), 'Wv': jax.random.normal(ks[8], (E, E), jnp.float32) / np.sqrt(E), 'bv': jnp.zeros((E,), jnp.float32), 'Wo': jax.random.normal(ks[9], (E, E), jnp.float32) / np.sqrt(E), 'bo': jnp.zeros((E,), jnp.float32)}
        return inp
    _L2_xattn_all = _L2_xattn_setup()
    _L2_xattn_in = {k: v for k, v in _L2_xattn_all.items() if k in ('Wq', 'bq', 'Wk', 'bk', 'Wv', 'bv', 'Wo', 'bo')}
    del _L2_xattn_all

    def _L2_ffn_setup():
        import jax, jax.numpy as jnp
        import numpy as np
        N_EXPERTS = 32
        TOP_K = 8
        N_GROUP = 4
        TOPK_GROUP = 2
        ROUTED_SCALING = 2.5

        def _gate(x, gate_w, gate_bias):
            T, E = (x.shape[0], gate_w.shape[0])
            logits = jnp.einsum('th,eh->te', x, gate_w)
            scores = jax.nn.sigmoid(logits)
            scores_choice = scores + gate_bias[None, :]
            grp = scores_choice.reshape(T, N_GROUP, E // N_GROUP)
            top2, _ = jax.lax.top_k(grp, 2)
            group_scores = top2.sum(-1)
            _, grp_idx = jax.lax.top_k(group_scores, TOPK_GROUP)
            group_mask = jax.nn.one_hot(grp_idx, N_GROUP, dtype=scores.dtype).sum(1)
            expert_mask = jnp.repeat(group_mask, E // N_GROUP, axis=1)
            masked = jnp.where(expert_mask > 0, scores_choice, 0.0)
            _, topk_idx = jax.lax.top_k(masked, TOP_K)
            topk_w = jnp.take_along_axis(scores, topk_idx, axis=1)
            topk_w = topk_w / (topk_w.sum(-1, keepdims=True) + 1e-20)
            topk_w = topk_w * ROUTED_SCALING
            return (topk_idx, topk_w)

        def _mlp(x, wg, wu, wd):
            return jnp.einsum('...i,hi->...h', jax.nn.silu(jnp.einsum('...h,ih->...i', x, wg)) * jnp.einsum('...h,ih->...i', x, wu), wd)
        key = jax.random.key(seed)
        ks = jax.random.split(key, 9)
        B, S, H, I = (2, 64, 128, 64)
        w = 0.02
        return {'hidden_states': jax.random.normal(ks[0], (B, S, H), jnp.float32), 'gate_w': jax.random.normal(ks[1], (N_EXPERTS, H), jnp.float32) * w, 'gate_bias': jax.random.normal(ks[2], (N_EXPERTS,), jnp.float32) * w, 'expert_gate': jax.random.normal(ks[3], (N_EXPERTS, I, H), jnp.float32) * w, 'expert_up': jax.random.normal(ks[4], (N_EXPERTS, I, H), jnp.float32) * w, 'expert_down': jax.random.normal(ks[5], (N_EXPERTS, H, I), jnp.float32) * w, 'shared_gate': jax.random.normal(ks[6], (2 * I, H), jnp.float32) * w, 'shared_up': jax.random.normal(ks[7], (2 * I, H), jnp.float32) * w, 'shared_down': jax.random.normal(ks[8], (H, 2 * I), jnp.float32) * w}
    _L2_ffn_all = _L2_ffn_setup()
    _L2_ffn_in = {k: v for k, v in _L2_ffn_all.items() if k in ('gate_w', 'gate_bias', 'expert_gate', 'expert_up', 'expert_down', 'shared_gate', 'shared_up', 'shared_down')}
    del _L2_ffn_all

    def _L3_xattn_setup():
        import jax, jax.numpy as jnp
        import numpy as np
        D_MODEL = 128
        B, S = (4, 256)
        key = jax.random.key(seed)
        ks = jax.random.split(key, 10)
        s = 1.0 / np.sqrt(D_MODEL)
        return {'k': jax.random.normal(ks[0], (B, S, D_MODEL), jnp.float32), 'v': jax.random.normal(ks[1], (B, S, D_MODEL), jnp.float32), 'q': jax.random.normal(ks[2], (B, S, D_MODEL), jnp.float32), 'Wk': jax.random.normal(ks[3], (D_MODEL, D_MODEL), jnp.float32) * s, 'Wv': jax.random.normal(ks[4], (D_MODEL, D_MODEL), jnp.float32) * s, 'bv': jnp.zeros((D_MODEL,), jnp.float32), 'Wq': jax.random.normal(ks[5], (D_MODEL, D_MODEL), jnp.float32) * s, 'bq': jnp.zeros((D_MODEL,), jnp.float32), 'Wo': jax.random.normal(ks[6], (D_MODEL, D_MODEL), jnp.float32) * s, 'bo': jnp.zeros((D_MODEL,), jnp.float32)}
    _L3_xattn_all = _L3_xattn_setup()
    _L3_xattn_in = {k: v for k, v in _L3_xattn_all.items() if k in ('Wk', 'Wv', 'bv', 'Wq', 'bq', 'Wo', 'bo')}
    del _L3_xattn_all

    def _L3_ffn_setup():
        import jax, jax.numpy as jnp
        import numpy as np
        N_EMBD = 128
        N_EXP = 8
        TOP_K = 2
        CAPACITY = 512
        D_FF = 3 * N_EMBD
        key = jax.random.key(seed)
        k1, k2, k3, k4 = jax.random.split(key, 4)
        x = jax.random.normal(k1, (8, 256, N_EMBD), dtype=jnp.float32)
        w_gate = jax.random.normal(k2, (N_EMBD, N_EXP), dtype=jnp.float32) * 0.02
        c_fc = jax.random.normal(k3, (N_EXP, N_EMBD, D_FF), dtype=jnp.float32) * 0.02
        c_proj = jax.random.normal(k4, (N_EXP, D_FF // 2, N_EMBD), dtype=jnp.float32) * 0.02
        return {'x': x, 'w_gate': w_gate, 'c_fc': c_fc, 'c_proj': c_proj}
    _L3_ffn_all = _L3_ffn_setup()
    _L3_ffn_in = {k: v for k, v in _L3_ffn_all.items() if k in ('w_gate', 'c_fc', 'c_proj')}
    del _L3_ffn_all
    return {'x': x, 'ctx_1024': ctx_1024, 'fside_BxSxS2_0': fside_BxSxS2_0, 'fside_Bx16xSxS2_0': fside_Bx16xSxS2_0, 'fside_SxS2_0': fside_SxS2_0, 'mask_BxS2_bk0': mask_BxS2_bk0, 'mask_BxSxS2_ik1': mask_BxSxS2_ik1, 'mask_BxS2_bf0': mask_BxS2_bf0, 'g_xattn': g_xattn, 'g_ffn': g_ffn, 'L0_xattn_g1': _L0_xattn_in['g1'], 'L0_xattn_b1': _L0_xattn_in['b1'], 'L0_xattn_g2': _L0_xattn_in['g2'], 'L0_xattn_b2': _L0_xattn_in['b2'], 'L0_xattn_Wq': _L0_xattn_in['Wq'], 'L0_xattn_Wkv': _L0_xattn_in['Wkv'], 'L0_xattn_Wout': _L0_xattn_in['Wout'], 'L0_ffn_Ws1': _L0_ffn_in['Ws1'], 'L0_ffn_Ws2': _L0_ffn_in['Ws2'], 'L0_ffn_W1': _L0_ffn_in['W1'], 'L0_ffn_W2': _L0_ffn_in['W2'], 'L0_ffn_Wr': _L0_ffn_in['Wr'], 'L1_xattn_wq_k': _L1_xattn_in['wq_k'], 'L1_xattn_wq_b': _L1_xattn_in['wq_b'], 'L1_xattn_wk_k': _L1_xattn_in['wk_k'], 'L1_xattn_wk_b': _L1_xattn_in['wk_b'], 'L1_xattn_wv_k': _L1_xattn_in['wv_k'], 'L1_xattn_wv_b': _L1_xattn_in['wv_b'], 'L1_xattn_wo_k': _L1_xattn_in['wo_k'], 'L1_xattn_wo_b': _L1_xattn_in['wo_b'], 'L1_ffn_w_gate': _L1_ffn_in['w_gate'], 'L1_ffn_w_up': _L1_ffn_in['w_up'], 'L1_ffn_w_down': _L1_ffn_in['w_down'], 'L2_xattn_Wq': _L2_xattn_in['Wq'], 'L2_xattn_bq': _L2_xattn_in['bq'], 'L2_xattn_Wk': _L2_xattn_in['Wk'], 'L2_xattn_bk': _L2_xattn_in['bk'], 'L2_xattn_Wv': _L2_xattn_in['Wv'], 'L2_xattn_bv': _L2_xattn_in['bv'], 'L2_xattn_Wo': _L2_xattn_in['Wo'], 'L2_xattn_bo': _L2_xattn_in['bo'], 'L2_ffn_gate_w': _L2_ffn_in['gate_w'], 'L2_ffn_gate_bias': _L2_ffn_in['gate_bias'], 'L2_ffn_expert_gate': _L2_ffn_in['expert_gate'], 'L2_ffn_expert_up': _L2_ffn_in['expert_up'], 'L2_ffn_expert_down': _L2_ffn_in['expert_down'], 'L2_ffn_shared_gate': _L2_ffn_in['shared_gate'], 'L2_ffn_shared_up': _L2_ffn_in['shared_up'], 'L2_ffn_shared_down': _L2_ffn_in['shared_down'], 'L3_xattn_Wk': _L3_xattn_in['Wk'], 'L3_xattn_Wv': _L3_xattn_in['Wv'], 'L3_xattn_bv': _L3_xattn_in['bv'], 'L3_xattn_Wq': _L3_xattn_in['Wq'], 'L3_xattn_bq': _L3_xattn_in['bq'], 'L3_xattn_Wo': _L3_xattn_in['Wo'], 'L3_xattn_bo': _L3_xattn_in['bo'], 'L3_ffn_w_gate': _L3_ffn_in['w_gate'], 'L3_ffn_c_fc': _L3_ffn_in['c_fc'], 'L3_ffn_c_proj': _L3_ffn_in['c_proj']}

def reference(x, ctx_1024, fside_BxSxS2_0, fside_Bx16xSxS2_0, fside_SxS2_0, mask_BxS2_bk0, mask_BxSxS2_ik1, mask_BxS2_bf0, g_xattn, g_ffn, L0_xattn_g1, L0_xattn_b1, L0_xattn_g2, L0_xattn_b2, L0_xattn_Wq, L0_xattn_Wkv, L0_xattn_Wout, L0_ffn_Ws1, L0_ffn_Ws2, L0_ffn_W1, L0_ffn_W2, L0_ffn_Wr, L1_xattn_wq_k, L1_xattn_wq_b, L1_xattn_wk_k, L1_xattn_wk_b, L1_xattn_wv_k, L1_xattn_wv_b, L1_xattn_wo_k, L1_xattn_wo_b, L1_ffn_w_gate, L1_ffn_w_up, L1_ffn_w_down, L2_xattn_Wq, L2_xattn_bq, L2_xattn_Wk, L2_xattn_bk, L2_xattn_Wv, L2_xattn_bv, L2_xattn_Wo, L2_xattn_bo, L2_ffn_gate_w, L2_ffn_gate_bias, L2_ffn_expert_gate, L2_ffn_expert_up, L2_ffn_expert_down, L2_ffn_shared_gate, L2_ffn_shared_up, L2_ffn_shared_down, L3_xattn_Wk, L3_xattn_Wv, L3_xattn_bv, L3_xattn_Wq, L3_xattn_bq, L3_xattn_Wo, L3_xattn_bo, L3_ffn_w_gate, L3_ffn_c_fc, L3_ffn_c_proj):
    import jax
    import jax.numpy as jnp

    def _L0_xattn_ref(x, latents, mask, g1, b1, g2, b2, Wq, Wkv, Wout):
        import jax, jax.numpy as jnp
        import numpy as np
        EPS = 1e-05

        def layer_norm(x, g, b):
            mu = jnp.mean(x, axis=-1, keepdims=True)
            var = jnp.mean((x - mu) ** 2, axis=-1, keepdims=True)
            return (x - mu) * jax.lax.rsqrt(var + EPS) * g + b
        heads, dim_head = (16, 64)
        b, n, D = x.shape
        l = latents.shape[1]
        xn = layer_norm(x, g1, b1)
        ln_lat = layer_norm(latents, g2, b2)
        q = ln_lat @ Wq
        kv = jnp.concatenate([xn, ln_lat], axis=1) @ Wkv
        k, v = jnp.split(kv, 2, axis=-1)

        def to_heads(t):
            return t.reshape(t.shape[0], t.shape[1], heads, dim_head).transpose(0, 2, 1, 3)
        q, k, v = (to_heads(q), to_heads(k), to_heads(v))
        scale = 1.0 / np.sqrt(np.sqrt(dim_head)).astype(np.float32)
        weight = jnp.einsum('bhld,bhnd->bhln', q * scale, k * scale)
        full_mask = jnp.concatenate([mask, jnp.ones((b, l), dtype=bool)], axis=1)
        neg = -jnp.finfo(weight.dtype).max
        weight = jnp.where(full_mask[:, None, None, :], weight, neg)
        weight = jax.nn.softmax(weight.astype(jnp.float32), axis=-1).astype(q.dtype)
        out = jnp.einsum('bhln,bhnd->bhld', weight, v)
        out = out.transpose(0, 2, 1, 3).reshape(b, l, heads * dim_head)
        return out @ Wout

    def _L0_ffn_ref(x, Ws1, Ws2, W1, W2, Wr):
        import jax, jax.numpy as jnp
        import numpy as np
        D_MODEL = 128
        EXPERT_DIM = 64
        N_EXPERTS = 8
        TOP_K = 2

        def _sq_relu(h):
            return jnp.square(jax.nn.relu(h))
        shape = x.shape
        xf = x.reshape(-1, D_MODEL)
        out_shared = _sq_relu(xf @ Ws1) @ Ws2
        logits = xf @ Wr
        top_vals, top_idx = jax.lax.top_k(logits, TOP_K)
        rw = jax.nn.softmax(top_vals.astype(jnp.float32), axis=-1).astype(x.dtype)
        onehot = jax.nn.one_hot(top_idx, N_EXPERTS, dtype=x.dtype)
        prob = jnp.einsum('tk,tke->te', rw, onehot)
        prob = jnp.trunc(prob)
        h = _sq_relu(jnp.einsum('td,edf->tef', xf, W1))
        y = jnp.einsum('tef,efd->ted', h, W2)
        out_routed = jnp.einsum('ted,te->td', y, prob)
        return (out_shared + out_routed).reshape(shape)

    def _L1_xattn_ref(query, key_in, value, group_prob, mask, wq_k, wq_b, wk_k, wk_b, wv_k, wv_b, wo_k, wo_b):
        import jax, jax.numpy as jnp
        import numpy as np
        NUM_HEADS = 16
        HIDDEN = 128
        B, S = (2, 256)

        def _split_heads(x, H):
            b, s, d = x.shape
            return x.reshape(b, s, H, d // H).transpose(0, 2, 1, 3)
        H = NUM_HEADS
        dh = query.shape[-1] // H
        q = _split_heads(query @ wq_k + wq_b, H)
        k = _split_heads(key_in @ wk_k + wk_b, H)
        v = _split_heads(value @ wv_k + wv_b, H)
        logits = jnp.einsum('bhqd,bhkd->bhqk', q, k) / jnp.sqrt(jnp.asarray(dh, q.dtype))
        neg = (1.0 - mask.astype(q.dtype)) * -1000000000.0
        logits = logits + neg[:, None, :, :]
        attn = jax.nn.softmax(logits, axis=-1)
        attn = attn * group_prob[:, None, :, :]
        out = jnp.einsum('bhqk,bhkd->bhqd', attn, v)
        out = out.transpose(0, 2, 1, 3).reshape(query.shape[0], -1, H * dh)
        return out @ wo_k + wo_b

    def _L1_ffn_ref(x, w_gate, w_up, w_down):
        import jax, jax.numpy as jnp
        import numpy as np
        BLOCK = 16
        _GRID = jnp.array([0.0, 0.5, 1.0, 1.5, 2.0, 3.0, 4.0, 6.0], dtype=jnp.float32)
        _MID = jnp.array([0.25, 0.75, 1.25, 1.75, 2.5, 3.5, 5.0], dtype=jnp.float32)

        def fp4_quant_dequant(x):
            shape = x.shape
            xb = x.reshape(shape[:-1] + (shape[-1] // BLOCK, BLOCK))
            scale = jnp.max(jnp.abs(xb), axis=-1, keepdims=True) / 6.0
            scale = jnp.maximum(scale, jnp.float32(1e-12))
            xn = xb / scale
            idx = jnp.searchsorted(_MID, jnp.abs(xn))
            q = _GRID[idx] * jnp.sign(xn) * scale
            return q.reshape(shape)

        def fp4_linear(x, w):
            xq = fp4_quant_dequant(x)
            wq = fp4_quant_dequant(w)
            return jnp.einsum('bsk,nk->bsn', xq, wq)
        gate = fp4_linear(x, w_gate)
        y = fp4_linear(x, w_up)
        h = jax.nn.silu(gate) * y
        return fp4_linear(h, w_down)

    def _L2_xattn_ref(query, key, value, spatial_bias, directional_bias, key_padding_mask, attn_mask, Wq, bq, Wk, bk, Wv, bv, Wo, bo):
        import jax, jax.numpy as jnp
        import numpy as np
        E = 128
        H = 16
        D = E // H
        B, T, _ = query.shape
        S = key.shape[1]
        scale = D ** (-0.5)
        q = (query @ Wq.T + bq).reshape(B, T, H, D).transpose(0, 2, 1, 3)
        k = (key @ Wk.T + bk).reshape(B, S, H, D).transpose(0, 2, 1, 3)
        v = (value @ Wv.T + bv).reshape(B, S, H, D).transpose(0, 2, 1, 3)
        scores = jnp.einsum('bhtd,bhsd->bhts', q, k) * scale
        scores = scores + attn_mask[None, None, :, :]
        pad = key_padding_mask[:, None, None, :]
        scores = jnp.where(pad, -jnp.inf, scores)
        if T == S:
            scores = scores + spatial_bias + directional_bias
        probs = jax.nn.softmax(scores, axis=-1)
        out = jnp.einsum('bhts,bhsd->bhtd', probs, v)
        out = out.transpose(0, 2, 1, 3).reshape(B, T, E)
        return out @ Wo.T + bo

    def _L2_ffn_ref(hidden_states, gate_w, gate_bias, expert_gate, expert_up, expert_down, shared_gate, shared_up, shared_down):
        import jax, jax.numpy as jnp
        import numpy as np
        N_EXPERTS = 32
        TOP_K = 8
        N_GROUP = 4
        TOPK_GROUP = 2
        ROUTED_SCALING = 2.5

        def _gate(x, gate_w, gate_bias):
            T, E = (x.shape[0], gate_w.shape[0])
            logits = jnp.einsum('th,eh->te', x, gate_w)
            scores = jax.nn.sigmoid(logits)
            scores_choice = scores + gate_bias[None, :]
            grp = scores_choice.reshape(T, N_GROUP, E // N_GROUP)
            top2, _ = jax.lax.top_k(grp, 2)
            group_scores = top2.sum(-1)
            _, grp_idx = jax.lax.top_k(group_scores, TOPK_GROUP)
            group_mask = jax.nn.one_hot(grp_idx, N_GROUP, dtype=scores.dtype).sum(1)
            expert_mask = jnp.repeat(group_mask, E // N_GROUP, axis=1)
            masked = jnp.where(expert_mask > 0, scores_choice, 0.0)
            _, topk_idx = jax.lax.top_k(masked, TOP_K)
            topk_w = jnp.take_along_axis(scores, topk_idx, axis=1)
            topk_w = topk_w / (topk_w.sum(-1, keepdims=True) + 1e-20)
            topk_w = topk_w * ROUTED_SCALING
            return (topk_idx, topk_w)

        def _mlp(x, wg, wu, wd):
            return jnp.einsum('...i,hi->...h', jax.nn.silu(jnp.einsum('...h,ih->...i', x, wg)) * jnp.einsum('...h,ih->...i', x, wu), wd)
        orig_shape = hidden_states.shape
        H = orig_shape[-1]
        residuals = hidden_states
        x = hidden_states.reshape(-1, H)
        topk_idx, topk_w = _gate(x, gate_w, gate_bias)
        g = jnp.einsum('th,eih->eti', x, expert_gate)
        u = jnp.einsum('th,eih->eti', x, expert_up)
        outs = jnp.einsum('eti,ehi->eth', jax.nn.silu(g) * u, expert_down)
        outs_t = jnp.transpose(outs, (1, 0, 2))
        gathered = jnp.take_along_axis(outs_t, topk_idx[:, :, None], axis=1)
        final = (gathered * topk_w[:, :, None]).sum(1)
        shared = _mlp(residuals, shared_gate, shared_up, shared_down)
        return final.reshape(orig_shape) + shared

    def _L3_xattn_ref(k, v, q, Wk, Wv, bv, Wq, bq, Wo, bo):
        import jax, jax.numpy as jnp
        import numpy as np
        D_MODEL = 128
        B, S = (4, 256)
        kp = jnp.einsum('bsd,ed->bse', k, Wk)
        vp = jnp.einsum('bsd,ed->bse', v, Wv) + bv
        qp = jnp.einsum('bsd,ed->bse', q, Wq) + bq
        scale = 1.0 / jnp.sqrt(jnp.float32(kp.shape[-1]))
        scores = jnp.einsum('bqd,bkd->bqk', qp, kp) * scale
        probs = jax.nn.softmax(scores, axis=-1)
        ctx = jnp.einsum('bqk,bkd->bqd', probs, vp)
        return jnp.einsum('bqd,ed->bqe', ctx, Wo) + bo

    def _L3_ffn_ref(x, w_gate, c_fc, c_proj):
        import jax, jax.numpy as jnp
        import numpy as np
        N_EMBD = 128
        N_EXP = 8
        TOP_K = 2
        CAPACITY = 512
        D_FF = 3 * N_EMBD
        B, T, d = x.shape
        N = B * T
        xf = x.reshape(N, d)
        scores = jax.nn.softmax(xf @ w_gate, axis=-1)
        weights, idx = jax.lax.top_k(scores, TOP_K)
        flat_e = idx.reshape(-1)
        tok = jnp.repeat(jnp.arange(N), TOP_K)
        oh = jax.nn.one_hot(flat_e, N_EXP, dtype=jnp.int32)
        pos = (jnp.cumsum(oh, axis=0) * oh).sum(-1) - 1
        valid = pos < CAPACITY
        pos_c = jnp.where(valid, pos, 0)
        vmask = valid.astype(x.dtype)[:, None]
        exp_x = jnp.zeros((N_EXP, CAPACITY, d), x.dtype)
        exp_x = exp_x.at[flat_e, pos_c].add(xf[tok] * vmask)
        h = jnp.einsum('ecd,edf->ecf', exp_x, c_fc)
        a, g = jnp.split(h, 2, axis=-1)
        h = jax.nn.silu(a) * g
        exp_out = jnp.einsum('ecf,efd->ecd', h, c_proj)
        gathered = exp_out[flat_e, pos_c]
        w = weights.reshape(-1)[:, None] * vmask
        out = (gathered * w).reshape(N, TOP_K, d).sum(axis=1)
        return out.reshape(B, T, d)
    x = x + jnp.tanh(g_xattn[0]) * _L0_xattn_ref(ctx_1024, _layernorm(x, axis=-1), mask_BxS2_bk0, L0_xattn_g1, L0_xattn_b1, L0_xattn_g2, L0_xattn_b2, L0_xattn_Wq, L0_xattn_Wkv, L0_xattn_Wout)
    x = x + jnp.tanh(g_ffn[0]) * _L0_ffn_ref(_layernorm(x, axis=-1), L0_ffn_Ws1, L0_ffn_Ws2, L0_ffn_W1, L0_ffn_W2, L0_ffn_Wr)
    x = x + jnp.tanh(g_xattn[1]) * _L1_xattn_ref(_layernorm(x, axis=-1), ctx_1024, ctx_1024, fside_BxSxS2_0, mask_BxSxS2_ik1, L1_xattn_wq_k, L1_xattn_wq_b, L1_xattn_wk_k, L1_xattn_wk_b, L1_xattn_wv_k, L1_xattn_wv_b, L1_xattn_wo_k, L1_xattn_wo_b)
    x = x + jnp.tanh(g_ffn[1]) * _L1_ffn_ref(_layernorm(x, axis=-1), L1_ffn_w_gate, L1_ffn_w_up, L1_ffn_w_down)
    x = x + jnp.tanh(g_xattn[2]) * _L2_xattn_ref(_layernorm(x, axis=-1), ctx_1024, ctx_1024, fside_Bx16xSxS2_0, fside_Bx16xSxS2_0, mask_BxS2_bf0, fside_SxS2_0, L2_xattn_Wq, L2_xattn_bq, L2_xattn_Wk, L2_xattn_bk, L2_xattn_Wv, L2_xattn_bv, L2_xattn_Wo, L2_xattn_bo)
    x = x + jnp.tanh(g_ffn[2]) * _L2_ffn_ref(_layernorm(x, axis=-1), L2_ffn_gate_w, L2_ffn_gate_bias, L2_ffn_expert_gate, L2_ffn_expert_up, L2_ffn_expert_down, L2_ffn_shared_gate, L2_ffn_shared_up, L2_ffn_shared_down)
    x = x + jnp.tanh(g_xattn[3]) * _L3_xattn_ref(ctx_1024, ctx_1024, _layernorm(x, axis=-1), L3_xattn_Wk, L3_xattn_Wv, L3_xattn_bv, L3_xattn_Wq, L3_xattn_bq, L3_xattn_Wo, L3_xattn_bo)
    x = x + jnp.tanh(g_ffn[3]) * _L3_ffn_ref(_layernorm(x, axis=-1), L3_ffn_w_gate, L3_ffn_c_fc, L3_ffn_c_proj)
    return x

_drawn_inputs = setup_inputs


def setup_inputs(seed=0):
    import zlib

    import numpy as np

    out = dict(_drawn_inputs(seed))
    spreads = {'L0_xattn_g1': (1.0, 0.2),
     'L0_xattn_b1': (0.0, 0.323),
     'L0_xattn_g2': (1.0, 0.2),
     'L0_xattn_b2': (0.0, 0.1),
     'L1_xattn_wq_b': (0.0, 0.78),
     'L1_xattn_wk_b': (0.0, 2.0),
     'L1_xattn_wv_b': (0.0, 0.1),
     'L1_xattn_wo_b': (0.0, 0.1),
     'L2_xattn_bq': (0.0, 0.581),
     'L2_xattn_bk': (0.0, 2.0),
     'L2_xattn_bv': (0.0, 0.1),
     'L2_xattn_bo': (0.0, 0.1),
     'L3_xattn_bv': (0.0, 0.663),
     'L3_xattn_bq': (0.0, 1.705),
     'L3_xattn_bo': (0.0, 0.534)}
    factors = {'fside_BxSxS2_0': 4.714,
     'fside_SxS2_0': 8.0,
     'g_ffn': 8.0,
     'L0_ffn_Ws1': 8.0,
     'L0_ffn_Ws2': 8.0,
     'L1_ffn_w_gate': 6.784,
     'L1_ffn_w_up': 6.24,
     'L1_ffn_w_down': 6.256,
     'L2_ffn_gate_w': 8.0,
     'L2_ffn_gate_bias': 8.0,
     'L2_ffn_expert_gate': 8.0,
     'L2_ffn_expert_up': 8.0,
     'L2_ffn_expert_down': 8.0,
     'L2_ffn_shared_gate': 8.0,
     'L2_ffn_shared_up': 8.0,
     'L2_ffn_shared_down': 8.0,
     'L3_ffn_w_gate': 8.0,
     'L3_ffn_c_fc': 8.0,
     'L3_ffn_c_proj': 8.0}
    for name, (base, spread) in spreads.items():
        noise = np.random.default_rng([zlib.crc32(name.encode()), seed]).standard_normal(out[name].shape)
        drawn = base * np.exp(spread * noise) if base else spread * noise
        out[name] = jnp.asarray(drawn.astype(out[name].dtype))
    for name, factor in factors.items():
        out[name] = (out[name] * factor).astype(out[name].dtype)
    return out
```

```python
from contextlib import ExitStack

import numpy as np

import concourse.bass as bass
from concourse import mybir

ALU = mybir.AluOpType
ACT = mybir.ActivationFunctionType
AX = mybir.AxisListType
F32 = mybir.dt.float32
I32 = mybir.dt.int32
U32 = mybir.dt.uint32
U8 = mybir.dt.uint8

B, T, S2, D = 8, 100, 1444, 128
P = 128
BANK = 512
KC = 121
NC_CTX = 12
LAST = S2 - (NC_CTX - 1) * KC
NH = 16
FLT_MAX = 3.4028234663852886e38
EPS = 1e-5
NEG_MASK = 1e9


def chunk_rows(c):
    return T if c == NC_CTX else (LAST if c == NC_CTX - 1 else KC)


def chunk_at(c):
    return S2 if c == NC_CTX else c * KC


def head_of(n):
    return 4 * (n % 4) + n // 4


class Link:

    def __init__(self, eng, sem, base=0):
        self.eng, self.sem, self.base, self.n = eng, sem, base, 0

    def __call__(self, ins):
        self.n += 1
        ins.then_inc(self.sem, 1)
        self.eng.wait_ge(self.sem, self.base + self.n)


def wait_apart(eng, passed, sem, value):
    if not isinstance(value, int):
        value = eng.to_reg(value)
        eng.wait_ge(passed, 1)
    eng.wait_ge(sem, value)


class Scope:

    used = []

    def __init__(self, nc, name):
        self.nc, self.name, self.ctx = nc, name, ExitStack()

    def __enter__(self):
        self.ctx.__enter__()
        return self

    def __exit__(self, *a):
        return self.ctx.__exit__(*a)

    def sb(self, name, shape, dt=F32):
        return self.ctx.enter_context(self.nc.sbuf_tensor(f"{self.name}_{name}", shape, dt))

    def banks(self, name, n):
        return [self.ctx.enter_context(self.nc.psum_tensor(f"{self.name}_{name}{i}", [P, BANK], F32))
                for i in range(n)]

    def sem(self, name):
        h = self.nc.alloc_semaphore(f"{self.name}_{name}")
        self.used.append(h)
        return h


def give_back(nc, used):
    nc.all_engine_barrier()
    nc.clear_and_free_semaphores(used)
    nc.all_engine_barrier()
    used.clear()


def bcast_rows(ap, rows, n):
    return ap.rearrange("(a n) -> a n", a=1).broadcast_to([rows, n])


def constants(nc, K, ins):
    with Scope(nc, "const") as s:
        ld, pool_sem, act_sem = s.sem("gates_loaded"), s.sem("pool_order"), s.sem("tanh_done")
        dve_sem, ones_set = s.sem("dve_order"), s.sem("ones_set")
        with nc.Block() as block:

            @block.sync
            def _(sp):
                sp.dma_start(K["gate"][:, 0:4], bcast_rows(ins["g_xattn"], P, 4)).then_inc(ld, 16)
                sp.dma_start(K["gate"][:, 4:8], bcast_rows(ins["g_ffn"], P, 4)).then_inc(ld, 16)

            @block.scalar
            def _(act):
                act.wait_ge(ld, 32)
                nc.scalar.activation(K["gate"][:], K["gate"][:], ACT.Tanh).then_inc(act_sem, 1)

            @block.vector
            def _(dve):
                for name in ("ident", "hm", "lt4", "lt8", "tri", "ones"):
                    nc.vector.memset(K[name][:], 0.0 if name == "ident" else 1.0).then_inc(ones_set, 1)
                nc.vector.memset(K["mhalf"][:], -0.5).then_inc(ones_set, 1)
                dve.wait_ge(pool_sem, 6)
                nc.vector.tensor_reduce(K["jm"][:], K["hm"][:].rearrange("p (j g) -> p j g", g=4),
                                        AX.X, ALU.add).then_inc(dve_sem, 1)

            @block.gpsimd
            def _(pool):
                pool.wait_ge(ones_set, 7)
                link = Link(pool, pool_sem)
                link(nc.gpsimd.affine_select(out=K["ident"][:], in_=K["ident"][:], compare_op=ALU.not_equal,
                                             fill=1.0, base=0, pattern=[[-1, P]], channel_multiplier=1))
                hm = K["hm"][:].rearrange("p (j g) -> p j g", g=4)
                link(nc.gpsimd.affine_select(out=hm, in_=hm, compare_op=ALU.is_ge, fill=0.0, base=0,
                                             pattern=[[-8, 4], [-32, 4]], channel_multiplier=1))
                link(nc.gpsimd.affine_select(out=hm, in_=hm, compare_op=ALU.is_ge, fill=0.0, base=7,
                                             pattern=[[8, 4], [32, 4]], channel_multiplier=-1))
                for name, n in (("lt4", 4), ("lt8", 8)):
                    m = K[name][:]
                    link(nc.gpsimd.affine_select(out=m, in_=m, compare_op=ALU.is_ge, fill=0.0, base=-1,
                                                 pattern=[[1, n], [-1, n]], channel_multiplier=0))
                link(nc.gpsimd.affine_select(out=K["tri"][:], in_=K["tri"][:], compare_op=ALU.is_ge, fill=0.0,
                                             base=-1, pattern=[[1, T]], channel_multiplier=-1))


def normalise(nc, K, name, XN, XT, affine=None, quant=False):
    X = K["X"]
    rounds = 2 if affine else 1
    with Scope(nc, name) as s:
        st, mv, rs = s.sb("stats", [T, B, 6]), s.sb("meanvar", [T, B, 2]), s.sb("rstd", [T, B])
        bc = s.sb("affine", [T, 2, D]) if affine else None
        q = quant_buffers(s, T, B * D) if quant else None
        xt_ps = s.banks("xt", 2)
        ld, var_ready, rstd_ready = s.sem("affine_loaded"), s.sem("var_ready"), s.sem("rstd_ready")
        order, pool_order = s.sem("dve_order"), s.sem("pool_order")
        xn_ready, xt_full, xt_done = s.sem("xn_ready"), s.sem("xt_full"), s.sem("xt_done")
        with nc.Block() as block:

            @block.sync
            def _(sp):
                if affine:
                    for n in range(2):
                        sp.dma_start(bc[:, n, :], bcast_rows(affine[n], T, D)).then_inc(ld, 16)

            @block.vector
            def _(dve):
                link = Link(dve, order)
                for r in range(rounds):
                    src = X if r == 0 else XN
                    for b in range(B):
                        i = nc.vector.bn_stats(st[:, b, :], src[:, b, :])
                        i.then_inc(order, 1)
                        link.n += 1
                    dve.wait_ge(order, link.n)
                    for b in range(B):
                        i = nc.vector.bn_aggr(mv[:, b, :], st[:, b, :])
                        i.then_inc(var_ready, 1)
                    dve.wait_ge(rstd_ready, r + 1)
                    for b in range(B):
                        i = nc.vector.tensor_scalar(XN[:, b, :], src[:, b, :], mv[:, b, 0:1], rs[:, b:b + 1],
                                                    ALU.subtract, ALU.mult)
                        i.then_inc(order, 1)
                        link.n += 1
                    dve.wait_ge(order, link.n)
                if affine:
                    dve.wait_ge(ld, 32)
                    for n, op in ((0, ALU.mult), (1, ALU.add)):
                        link(nc.vector.tensor_tensor(XN[:], XN[:], bc[:, n:n + 1, :].broadcast_to([T, B, D]), op))
                if quant:
                    flat = XN[:].rearrange("p b d -> p (b d)")
                    fp4_round(nc, link, q, flat, flat)
                nc.vector.memset(mv[:, 0, 0:1], 0.0).then_inc(xn_ready, 1)

            @block.gpsimd
            def _(pool):
                for r in range(rounds):
                    pool.wait_ge(var_ready, B * (r + 1))
                    nc.gpsimd.tensor_scalar(rs[:], mv[:, :, 1], EPS, None, ALU.add).then_inc(pool_order, 1)
                    pool.wait_ge(pool_order, r + 1)
                    nc.gpsimd.tensor_tensor(rs[:], rs[:], K["mhalf"][0:T, 0:B], ALU.pow).then_inc(rstd_ready, 1)

            @block.tensor
            def _(pe):
                pe.wait_ge(xn_ready, 1)
                for b in range(B):
                    i = nc.tensor.transpose(xt_ps[b // 4][:, (b % 4) * T:(b % 4 + 1) * T], XN[:, b, :],
                                            K["ident"][0:T, 0:T])
                    if b % 4 == 3:
                        i.then_inc(xt_full, 1)

            @block.scalar
            def _(act):
                for n in range(2):
                    act.wait_ge(xt_full, n + 1)
                    nc.scalar.copy(XT[:, n * 4 * T:(n + 1) * 4 * T], xt_ps[n][:, 0:4 * T]).then_inc(xt_done, 1)


def quant_buffers(s, rows, n):
    nb = n // 16
    return {"a": s.sb("q_abs", [rows, n]), "q": s.sb("q_code", [rows, n]), "sc": s.sb("q_scale", [rows, nb]),
            "rc": s.sb("q_rscale", [rows, nb])}


def fp4_round(nc, link, buf, out, src, rows=None):
    n = src.shape[-1]
    r = src.shape[0]
    a, q = buf["a"][0:r, 0:n], buf["q"][0:r, 0:n]
    sc, rc = buf["sc"][0:r, 0:n // 16], buf["rc"][0:r, 0:n // 16]
    blk = lambda ap: ap.rearrange("p (n k) -> p n k", k=16)
    wide = lambda ap: ap.rearrange("p (n k) -> p n k", k=1).broadcast_to([r, n // 16, 16])
    v = nc.vector
    link(v.tensor_reduce(sc, blk(src), AX.X, ALU.max, apply_absolute_value=True))
    link(v.tensor_scalar(sc, sc, 1.0 / 6.0, 1e-12, ALU.mult, ALU.max))
    link(v.reciprocal(rc, sc))
    link(v.tensor_tensor(blk(a), blk(src), wide(rc), ALU.mult))
    link(v.scalar_tensor_tensor(out=a, in0=a, scalar=-1.0, in1=a, op0=ALU.mult, op1=ALU.max))
    link(v.tensor_scalar(q, a, 0.25, None, ALU.is_gt))
    for mid in (0.75, 1.25, 1.75):
        link(v.scalar_tensor_tensor(out=q, in0=a, scalar=mid, in1=q, op0=ALU.is_gt, op1=ALU.add))
    link(v.tensor_scalar(q, q, 0.5, None, ALU.mult))
    for mid in (2.5, 3.5, 5.0, 5.0):
        link(v.scalar_tensor_tensor(out=q, in0=a, scalar=mid, in1=q, op0=ALU.is_gt, op1=ALU.add))
    link(v.tensor_scalar(a.bitcast(U32), src.bitcast(U32), 0x80000000, None, ALU.bitwise_and))
    link(v.tensor_tensor(q.bitcast(U32), q.bitcast(U32), a.bitcast(U32), ALU.bitwise_or))
    link(v.tensor_tensor(blk(out), blk(q), wide(sc), ALU.mult))


def transposes(nc, K, name, jobs, loads=(), quants=(), products=None):
    NB = 4
    with Scope(nc, name) as s:
        q = quant_buffers(s, P, max(a.shape[-1] for a in quants)) if quants else None
        ps = s.banks("t", NB)
        ld, order, full = s.sem("loaded"), s.sem("dve_order"), s.sem("bank_full")
        act_done, dve_done, qd = s.sem("act_emptied"), s.sem("dve_emptied"), s.sem("quantised")
        with nc.Block() as block:

            @block.sync
            def _(sp):
                for to, src in loads:
                    sp.dma_start(to, src).then_inc(ld, 16)

            @block.tensor
            def _(pe):
                if loads:
                    pe.wait_ge(ld, 16 * len(loads))
                if quants:
                    pe.wait_ge(qd, 1)
                for n, (to, src) in enumerate(jobs):
                    if n >= NB:
                        pe.wait_ge(dve_done if n % 2 else act_done, (n - NB) // 2 + 1)
                    r, c = src.shape
                    nc.tensor.transpose(ps[n % NB][0:c, 0:r], src, K["ident"][0:r, 0:r]).then_inc(full, 1)

            def empty(eng, copy, par, done):
                for n in range(par, len(jobs), 2):
                    to, src = jobs[n]
                    r, c = src.shape
                    eng.wait_ge(full, n + 1)
                    copy(to, ps[n % NB][0:c, 0:r]).then_inc(done, 1)

            @block.scalar
            def _(act):
                empty(act, nc.scalar.copy, 0, act_done)

            @block.vector
            def _(dve):
                if quants:
                    link = Link(dve, order)
                    dve.wait_ge(ld, 16 * len(loads))
                    for m in quants:
                        fp4_round(nc, link, q, m, m)
                    nc.vector.memset(q["rc"][:, 0:1], 0.0).then_inc(qd, 1)
                empty(dve, nc.vector.tensor_copy, 1, dve_done)


class Ring:

    def __init__(self, jobs, start=None):
        self.jobs = list(jobs)
        self.index = {name: n for n, (name, _) in enumerate(self.jobs)}
        self.total = {e: sum(x == e for _, x in self.jobs) for e in "av"}
        self.start = start or {"a": 0, "v": 0, "full": 0}

    def after(self):
        return {"a": self.start["a"] + self.total["a"], "v": self.start["v"] + self.total["v"],
                "full": self.start["full"] + len(self.jobs)}

    def bank(self, name):
        return self.index[name] % 2

    def engine(self, name):
        return self.jobs[self.index[name]][1]

    def full(self, step, name):
        return step * len(self.jobs) + (self.start["full"] + self.index[name] + 1)

    def emptied(self, step, name, engine):
        n = sum(e == engine for _, e in self.jobs[:self.index[name] + 1])
        return step * self.total[engine] + (self.start[engine] + n)

    def before(self, step, engine):
        return step * (len(self.jobs) if engine == "full" else self.total[engine]) + self.start[engine]


def attention(nc, K, kind, W, ins, ctxT_dram):
    H = 1 if kind == 3 else NH
    G = max(H // 4, 1)
    GW = min(H, 4)
    keys = S2 + T if kind == 0 else S2
    NCH = NC_CTX + (kind == 0)
    widths = [386] * 4 if kind == 0 else [482, 482, 480]
    U = len(widths)
    at = [sum(widths[:u]) for u in range(U)]
    SB = 3 if kind == 3 else 4
    NP = 2 if kind == 3 else 4
    job_chunks = [list(range(4 * k, 4 * k + 4)) for k in range(3)]
    if kind == 0:
        job_chunks[2].append(NC_CTX)
    X = K["X"]
    gate = K["gate"][0:T, kind:kind + 1]

    if kind == 0:
        part_a = [("C0", "a"), ("C1", "a"), ("C2", "a")]
        part_b = [("X0", "v"), ("X1", "a"), ("X2", "v"), ("Q0", "a"), ("Q1", "v"), ("Q2", "a"), ("Q3", "v")]
    else:
        part_a = [("K0", "a"), ("K1", "v"), ("K2", "a")]
        part_b = [("V0", "v"), ("V1", "v"), ("V2", "v")]
        if kind == 1:
            part_b = [("V0", "v"), ("G0", "a"), ("V1", "v"), ("G1", "a"), ("V2", "v"), ("G2", "a")]

    def t_jobs(n):
        return [((n, k), "v" if kind == 1 or (3 * n + k) % 2 else "a") for k in range(3)]

    body = []
    for s in range(2, H):
        body += t_jobs(s - 2)
        if kind == 0 and s % 4 == 2 and s > 2:
            body.append((f"R{s // 4 - 1}", "a"))
    body += part_a
    for n in range(max(H - 2, 0), H):
        body += t_jobs(n)
    body += [(f"R{G - 1}", "a")] + part_b
    first = Ring(part_a + part_b)
    ring = Ring(body, first.after())

    with Scope(nc, f"attn{kind}") as s_:
        sb, sem = s_.sb, s_.sem
        kT = [sb(f"kT{i}", [P, keys]) for i in range(2)]
        V = [sb(f"V{i}", [KC, NCH, D]) for i in range(2)]
        Qs = [sb(f"Q{i}", [P, H, T]) for i in range(2)]
        bias = [sb(f"bias{i}", [T, keys]) for i in range(2)]
        prob = sb("prob", [T, NP, keys])
        pT = sb("pT", [KC, 2, NCH, GW, T])
        mpart, nmax = sb("mpart", [T, 2, H, U]), sb("nmax", [T, 2, H])
        RW = 32 if kind in (1, 2) else 1
        den, rden = sb("den", [T, 2, H]), sb("rden", [T, 2, H * RW])
        R = sb("R", [P, GW * T])
        Y = [sb(f"Y{i}", [P, GW * T]) for i in range(2)]
        upd = sb("upd", [T, D])
        if kind == 0:
            cn = sb("ctx", [KC, NC_CTX, D])
            stage = sb("ctxT", [P, S2])
            keep = sb("keep", [T, S2], U8)
            st, mv, rs = sb("st", [KC, NC_CTX, 6]), sb("mv", [KC, NC_CTX, 2]), sb("rs", [KC, NC_CTX])
        else:
            ctxT = sb("ctxT", [P, S2])
        if kind == 1:
            mask = sb("mask", [T, S2], I32)
            Gp = sb("group", [T, S2])
            GT = [sb(f"GT{i}", [KC, NC_CTX, T]) for i in range(2)]
        if kind == 2:
            pad = sb("pad", [T, S2], U8)
            attn = sb("attn", [T, S2])
        s_ps, r_ps = s_.banks("score", SB), s_.banks("ring", 2)
        o_ps, out_ps = s_.banks("av", 1)[0], s_.banks("out", 1)[0]

        ready = sem("ready")
        ld_ctx, ld_mask, ld_g = sem("ctx_loaded"), sem("mask_loaded"), sem("group_loaded")
        ld_const, stored = sem("const_loaded"), sem("ctxT_stored")
        bias_ready = sem("bias_ready")
        side_ready = sem("pool_ready")
        score_full = sem("score_full")
        score_used = sem("score_used")
        max_ready = sem("max_ready")
        prob_ready = sem("prob_ready")
        rden_ready = sem("rden_ready")
        ring_full, act_out, dve_out = sem("ring_full"), sem("act_emptied"), sem("dve_emptied")
        av_full = sem("av_full")
        y_ready = sem("y_ready")
        folded = sem("y_used")
        upd_ready, x_done = sem("update_ready"), sem("x_done")
        ln, var_ready, rstd_ready, rs_order, xn_ready = (sem("ln"), sem("var_ready"), sem("rstd_ready"),
                                                         sem("rs_order"), sem("xn_ready"))
        out_of = {"a": act_out, "v": dve_out}
        NSIDE = 2 if kind == 0 else 1

        with nc.Block() as block:

            @block.sync
            def _(sp):
                if kind == 2:
                    sp.dma_start(attn[:], ins["fside_SxS2_0"]).then_inc(ld_const, 16)

                def load(step, b):
                    if kind == 0:
                        n = (NC_CTX - 1) * KC
                        sp.dma_start(cn[:, 0:NC_CTX - 1, :],
                                     ins["ctx_1024"][b, 0:n, :].rearrange("(c p) d -> p c d", p=KC)).then_inc(ld_ctx, 16)
                        sp.dma_start(cn[0:LAST, NC_CTX - 1, :], ins["ctx_1024"][b, n:S2, :]).then_inc(ld_ctx, 16)
                        sp.dma_start(keep[:], bcast_rows(ins["mask_BxS2_bk0"][b, :], T, S2)).then_inc(ld_mask, 16)
                    else:
                        sp.dma_start(ctxT[:], ctxT_dram[b]).then_inc(ld_ctx, 16)
                    if kind == 1:
                        sp.dma_start(mask[:], ins["mask_BxSxS2_ik1"][b]).then_inc(ld_mask, 16)
                        sp.dma_start(Gp[:], ins["fside_BxSxS2_0"][b]).then_inc(ld_g, 16)
                    if kind == 2:
                        sp.dma_start(pad[:], bcast_rows(ins["mask_BxS2_bf0"][b, :], T, S2)).then_inc(ld_mask, 16)

                def store(rg, step, b):
                    wait_apart(sp, ready, act_out, rg.emptied(step, "C2", "a"))
                    sp.dma_start(ctxT_dram[b], stage[:]).then_inc(stored, 16)

                sp.wait_ge(ready, 1)
                load(0, 0)
                if kind == 0:
                    store(first, 0, 0)
                with sp.Fori(0, B // 2) as i:
                    for par in range(2):
                        n = i * 2 + par
                        b = sp.snap((n + 1) % B)
                        wait_apart(sp, ready, ring_full, ring.before(n, "full"))
                        if kind == 0:
                            wait_apart(sp, ready, ln, n * 25 + 24)
                        if kind != 3:
                            wait_apart(sp, ready, bias_ready, n + 1)
                        load(n + 1, b)
                        if kind == 0:
                            store(ring, n, b)
                if kind == 0:
                    sp.wait_ge(stored, 16 * (B + 1))

            @block.gpsimd
            def _(pool):
                def side(step, b, nxt):
                    if kind == 0:
                        wait_apart(pool, ready, var_ready, (step + 1) * NC_CTX)
                        nc.gpsimd.tensor_scalar(rs[:], mv[:, :, 1], EPS, None, ALU.add).then_inc(rs_order, 1)
                        pool.wait_ge(rs_order, step + 1)
                        nc.gpsimd.tensor_tensor(rs[:], rs[:], K["mhalf"][0:KC, 0:NC_CTX], ALU.pow).then_inc(rstd_ready, 1)
                        nc.gpsimd.tensor_copy(V[nxt][0:T, NC_CTX, :], W["lat"][:, b, :]).then_inc(side_ready, 1)
                        nc.gpsimd.tensor_copy(kT[nxt][:, S2:keys], W["latT"][:, bass.ds(b * T, T)]).then_inc(side_ready, 1)
                    elif kind == 3:
                        nc.gpsimd.tensor_copy(Qs[nxt][:, 0, :], W["q"][:, bass.ds(b * T, T)]).then_inc(side_ready, 1)
                    else:
                        q = W["q"][:, bass.ds(b * T, T)].rearrange("p (a t) -> p a t", a=1)
                        hm = K["hm"][:].rearrange("p (h a) -> p h a", a=1)
                        nc.gpsimd.tensor_tensor(Qs[nxt][:], q.broadcast_to([P, H, T]), hm.broadcast_to([P, H, T]),
                                                ALU.mult).then_inc(side_ready, 1)

                pool.wait_ge(ready, 1)
                side(0, 0, 0)
                with pool.Fori(0, B // 2) as i:
                    for par in range(2):
                        n = i * 2 + par
                        b = pool.snap((n + 1) % B)
                        wait_apart(pool, ready, score_full, n * (H * U) + 1)
                        side(n + 1, b, 1 - par)

            @block.tensor
            def _(pe):
                ident = K["ident"]

                def job(rg, step, name):
                    n = rg.index[name]
                    if n >= 2:
                        prev, e = rg.jobs[n - 2]
                        pe.wait_ge(out_of[e], rg.emptied(step, prev, e))
                    return r_ps[n % 2]

                def scores(step, par, h):
                    for u in range(U):
                        m = h * U + u
                        if m >= SB:
                            pe.wait_ge(score_used, step * (H * U) + (m - SB + 1))
                        i_ = nc.tensor.matmul(s_ps[m % SB][0:T, 0:widths[u]], Qs[par][:, h, :],
                                              kT[par][:, at[u]:at[u] + widths[u]], start=True, stop=True)
                        i_.then_inc(score_full, 1)

                def turn(step, par, h):
                    pe.wait_ge(prob_ready, step * H + (h + 1))
                    slot = (h + par * H) % NP
                    for k in range(3):
                        ps = job(ring, step, (h, k))
                        for x, c in enumerate(job_chunks[k]):
                            kc, c0 = chunk_rows(c), chunk_at(c)
                            i_ = nc.tensor.transpose(ps[0:kc, x * T:(x + 1) * T], prob[:, slot, c0:c0 + kc],
                                                     ident[0:T, 0:T])
                        i_.then_inc(ring_full, 1)

                def spread(step, par, j):
                    name = f"R{j}"
                    ps = job(ring, step, name)
                    pe.wait_ge(rden_ready, step * (G if kind == 0 else 1) + ((j if kind == 0 else 0) + 1))
                    for x in range(GW):
                        if kind in (0, 3):
                            r = rden[:, par, 4 * j + x:4 * j + x + 1].broadcast_to([T, P])
                        else:
                            r = rden[:, par, P * x:P * x + P]
                        i_ = nc.tensor.transpose(ps[:, x * T:(x + 1) * T], r, ident[0:T, 0:T])
                    i_.then_inc(ring_full, 1)

                def values(step, par, j):
                    last = GW * (j + 1) - 1
                    for e in "av":
                        if any(x == e for _, x in t_jobs(last)):
                            pe.wait_ge(out_of[e], ring.emptied(step, (last, 2), e))
                    if kind == 0 and j:
                        pe.wait_ge(y_ready, step * G + j)
                    slot = par if kind == 3 else j % 2
                    for c in range(NCH):
                        kc = chunk_rows(c)
                        flags = {"start": c == 0, "stop": c == NCH - 1}
                        if kind in (0, 3):
                            i_ = nc.tensor.matmul(o_ps[:, 0:GW * T], V[par][0:kc, c, :],
                                                  pT[0:kc, slot, c, :, :].rearrange("p g t -> p (g t)"), **flags)
                        else:
                            for g in range(4):
                                i_ = nc.tensor.matmul(o_ps[32 * g:32 * g + 32, j * T:(j + 1) * T],
                                                      V[par][0:kc, c, 32 * g:32 * g + 32],
                                                      pT[0:kc, slot, c, g, :], **flags)
                    i_.then_inc(av_full, 1)

                def output(step, j):
                    pe.wait_ge(y_ready, step * (G if kind == 0 else 1) + ((j if kind == 0 else 0) + 1))
                    for x in range(GW):
                        if kind == 0:
                            n, w, y = 4 * j + x, W["vo"][:, 4 * x + j, :], Y[j % 2]
                        else:
                            n, w, y = x, W["o"][:, x, :], Y[0]
                        i_ = nc.tensor.matmul(out_ps[0:T, 0:D], y[:, x * T:(x + 1) * T], w, start=(n == 0),
                                              stop=(n == (H if kind == 0 else GW) - 1))
                    i_.then_inc(folded, 1)

                def project_a(rg, step, load_no, nxt):
                    pe.wait_ge(ld_ctx, (load_no + 1) * (32 if kind == 0 else 16))
                    for k in range(3):
                        if kind == 0:
                            ps = job(rg, step, f"C{k}")
                            for c in range(4 * k, 4 * k + 4):
                                kc = chunk_rows(c)
                                i_ = nc.tensor.transpose(ps[:, (c - 4 * k) * KC:(c - 4 * k) * KC + kc],
                                                         cn[0:kc, c, :], ident[0:kc, 0:kc])
                            i_.then_inc(ring_full, 1)
                        else:
                            ps = job(rg, step, f"K{k}")
                            nc.tensor.matmul(ps[:, 0:widths[k]], W["k"][:], ctxT[:, at[k]:at[k] + widths[k]],
                                             start=True, stop=True).then_inc(ring_full, 1)

                def project_b(rg, step, load_no, nxt, b):
                    if kind == 0:
                        pe.wait_ge(xn_ready, load_no + 1)
                        for k in range(3):
                            ps = job(rg, step, f"X{k}")
                            for c in range(4 * k, 4 * k + 4):
                                kc = chunk_rows(c)
                                i_ = nc.tensor.transpose(ps[:, (c - 4 * k) * KC:(c - 4 * k) * KC + kc],
                                                         V[nxt][0:kc, c, :], ident[0:kc, 0:kc])
                            i_.then_inc(ring_full, 1)
                        for k in range(4):
                            ps = job(rg, step, f"Q{k}")
                            for g in range(4):
                                i_ = nc.tensor.matmul(ps[:, g * T:(g + 1) * T], W["qk"][:, 4 * g + k, :],
                                                      W["latT"][:, bass.ds(b * T, T)], start=True, stop=True)
                            i_.then_inc(ring_full, 1)
                        return
                    for k in range(3):
                        ps = job(rg, step, f"V{k}")
                        for c in range(4 * k, 4 * k + 4):
                            kc, c0 = chunk_rows(c), chunk_at(c)
                            i_ = nc.tensor.matmul(ps[0:kc, (c - 4 * k) * D:(c - 4 * k + 1) * D], ctxT[:, c0:c0 + kc],
                                                  W["v"][:], start=True, stop=True)
                        i_.then_inc(ring_full, 1)
                        if kind == 1:
                            ps = job(rg, step, f"G{k}")
                            if k == 0:
                                pe.wait_ge(ld_g, (load_no + 1) * 16)
                            for c in range(4 * k, 4 * k + 4):
                                kc, c0 = chunk_rows(c), chunk_at(c)
                                i_ = nc.tensor.transpose(ps[0:kc, (c - 4 * k) * T:(c - 4 * k + 1) * T],
                                                         Gp[:, c0:c0 + kc], ident[0:T, 0:T])
                            i_.then_inc(ring_full, 1)

                pe.wait_ge(ready, 1)
                project_a(first, 0, 0, 0)
                project_b(first, 0, 0, 0, 0)
                with pe.Fori(0, B // 2) as i:
                    for par in range(2):
                        n = i * 2 + par
                        pe.wait_ge(act_out, ring.before(n, "a"))
                        pe.wait_ge(dve_out, ring.before(n, "v"))
                        pe.wait_ge(side_ready, (n + 1) * NSIDE)
                        for s in range(H):
                            scores(n, par, s)
                            if s >= 2:
                                turn(n, par, s - 2)
                            if s % 4 == 2 and s > 2:
                                j = s // 4 - 1
                                if kind == 0:
                                    spread(n, par, j)
                                values(n, par, j)
                            if kind == 0 and s in (8, 12):
                                output(n, s // 4 - 2)
                        project_a(ring, n, n + 1, 1 - par)
                        if kind == 0:
                            output(n, 2)
                        for h in range(max(H - 2, 0), H):
                            turn(n, par, h)
                        spread(n, par, G - 1)
                        values(n, par, G - 1)
                        project_b(ring, n, n + 1, 1 - par, (n + 1) % B)
                        output(n, G - 1)

            @block.scalar
            def _(act):
                def out(rg, step, name):
                    act.wait_ge(ring_full, rg.full(step, name))
                    return r_ps[rg.bank(name)]

                def turned(step, par, h):
                    for (name, e) in t_jobs(h):
                        if e != "a":
                            continue
                        ch = job_chunks[name[1]]
                        j, g = h // 4, h % 4
                        slot = par if kind == 3 else j % 2
                        ps = out(ring, step, name)
                        if kind != 3 and j >= 2 and h % 4 < 2:
                            act.wait_ge(av_full, step * G + (j - 1))
                        nc.scalar.copy(pT[:, slot, ch[0]:ch[0] + len(ch), g, :],
                                       ps[0:KC, 0:len(ch) * T].rearrange("p (c t) -> p c t", t=T)).then_inc(act_out, 1)

                def expo(step, par, h):
                    act.wait_ge(max_ready, step * H + (h + 1))
                    p = prob[:, (h + par * H) % NP, :]
                    nc.scalar.activation(p, p, ACT.Exp, bias=nmax[:, par, h:h + 1],
                                         accum_out=den[:, par, h:h + 1]).then_inc(prob_ready, 1)

                def spread(step, j):
                    ps = out(ring, step, f"R{j}")
                    if kind == 0 and j:
                        act.wait_ge(y_ready, step * G + j)
                    nc.scalar.copy(R[:], ps[:, 0:GW * T]).then_inc(act_out, 1)

                def projected(rg, step, load_no, nxt, part):
                    for name, e in part:
                        if e != "a":
                            continue
                        k = int(name[1])
                        ps = out(rg, step, name)
                        if name[0] == "C":
                            if k == 0 and rg is ring:
                                act.wait_ge(stored, load_no * 16)
                            w = min(4 * KC, S2 - 4 * k * KC)
                            i_ = nc.scalar.copy(stage[:, 4 * k * KC:4 * k * KC + w], ps[:, 0:w])
                        elif name[0] == "X":
                            w = min(4 * KC, S2 - 4 * k * KC)
                            i_ = nc.scalar.copy(kT[nxt][:, 4 * k * KC:4 * k * KC + w], ps[:, 0:w])
                        elif name[0] == "Q":
                            i_ = nc.scalar.copy(Qs[nxt][:, 4 * k:4 * k + 4, :],
                                                ps[:, 0:4 * T].rearrange("p (g t) -> p g t", t=T))
                        elif name[0] == "K":
                            i_ = nc.scalar.activation(kT[nxt][:, at[k]:at[k] + widths[k]], ps[:, 0:widths[k]],
                                                      ACT.Identity, bias=W["bk"][:, 0:1])
                        else:
                            i_ = nc.scalar.copy(GT[nxt][:, 4 * k:4 * k + 4, :],
                                                ps[0:KC, 0:4 * T].rearrange("p (c t) -> p c t", t=T))
                        i_.then_inc(act_out, 1)

                act.wait_ge(ready, 1)
                projected(first, 0, 0, 0, part_a + part_b)
                with act.Fori(0, B // 2) as i:
                    for par in range(2):
                        n = i * 2 + par
                        for s in range(H):
                            if s >= 2:
                                turned(n, par, s - 2)
                            if kind == 0 and s % 4 == 2 and s > 2:
                                spread(n, s // 4 - 1)
                            expo(n, par, s)
                        projected(ring, n, n + 1, 1 - par, part_a)
                        for h in range(max(H - 2, 0), H):
                            turned(n, par, h)
                        spread(n, G - 1)
                        projected(ring, n, n + 1, 1 - par, part_b)

            @block.vector
            def _(dve):
                v = nc.vector


                def masked(step, par, h):
                    if h == 0 and kind != 3:
                        dve.wait_ge(bias_ready, step + 1)
                    if h >= NP:
                        dve.wait_ge(ring_full, ring.full(step, (h - NP, 2)))
                    slot = (h + par * H) % NP
                    for u in range(U):
                        m = h * U + u
                        wait_apart(dve, ready, score_full, step * (H * U) + (m + 1))
                        i_ = v.tensor_tensor_reduce(prob[:, slot, at[u]:at[u] + widths[u]], s_ps[m % SB][0:T, 0:widths[u]],
                                                    bias[par][:, at[u]:at[u] + widths[u]], 1.0, -FLT_MAX,
                                                    ALU.add, ALU.max, mpart[:, par, h, u:u + 1])
                        i_.then_inc(score_used, 1)
                    dve.wait_ge(score_used, step * (H * U) + (h + 1) * U)
                    v.tensor_reduce(nmax[:, par, h:h + 1], mpart[:, par, h, :], AX.X, ALU.max,
                                    negate=True).then_inc(max_ready, 1)

                def out(rg, step, name):
                    dve.wait_ge(ring_full, rg.full(step, name))
                    return r_ps[rg.bank(name)]

                def turned(step, par, h):
                    for (name, e) in t_jobs(h):
                        if e != "v":
                            continue
                        ch = job_chunks[name[1]]
                        j, g = h // 4, h % 4
                        slot = par if kind == 3 else j % 2
                        ps = out(ring, step, name)
                        if kind != 3 and j >= 2 and h % 4 < 2:
                            dve.wait_ge(av_full, step * G + (j - 1))
                        to = pT[:, slot, ch[0]:ch[0] + len(ch), g, :]
                        src = ps[0:KC, 0:len(ch) * T].rearrange("p (c t) -> p c t", t=T)
                        if kind == 1:
                            if h == 0 and name[1] == 0:
                                dve.wait_ge(act_out, ring.before(step, "a"))
                            i_ = v.tensor_tensor(to, src, GT[par][:, ch[0]:ch[0] + len(ch), :], ALU.mult)
                        else:
                            i_ = v.tensor_copy(to, src)
                        i_.then_inc(dve_out, 1)

                def recip(step, par, j):
                    n = 4 * (j + 1) if kind == 0 else H
                    dve.wait_ge(prob_ready, step * H + n)
                    lo = n - 4 if kind == 0 else 0
                    v.reciprocal(rden[:, par, lo * RW:n * RW].rearrange("t (h r) -> t h r", r=RW),
                                 den[:, par, lo:n].rearrange("t (h r) -> t h r", r=1).broadcast_to([T, n - lo, RW])
                                 ).then_inc(rden_ready, 1)

                def divide(step, j):
                    dve.wait_ge(act_out, ring.emptied(step, f"R{j}", "a"))
                    dve.wait_ge(av_full, step * G + (j + 1))
                    if kind == 0 and j >= 2:
                        dve.wait_ge(folded, step * G + (j - 1))
                    v.tensor_tensor(Y[j % 2 if kind == 0 else 0][:], o_ps[:, 0:GW * T], R[:], ALU.mult).then_inc(y_ready, 1)

                def projected(rg, step, nxt, part):
                    for name, e in part:
                        if e != "v":
                            continue
                        k = int(name[1])
                        ps = out(rg, step, name)
                        if name[0] == "X":
                            w = min(4 * KC, S2 - 4 * k * KC)
                            i_ = v.tensor_copy(kT[nxt][:, 4 * k * KC:4 * k * KC + w], ps[:, 0:w])
                        elif name[0] == "Q":
                            i_ = v.tensor_copy(Qs[nxt][:, 4 * k:4 * k + 4, :],
                                               ps[:, 0:4 * T].rearrange("p (g t) -> p g t", t=T))
                        elif name[0] == "K":
                            i_ = v.tensor_scalar(kT[nxt][:, at[k]:at[k] + widths[k]], ps[:, 0:widths[k]],
                                                 W["bk"][:, 0:1], None, ALU.add)
                        else:
                            bv = W["bv"][0:KC, :].rearrange("p (a d) -> p a d", a=1).broadcast_to([KC, 4, D])
                            i_ = v.tensor_tensor(V[nxt][:, 4 * k:4 * k + 4, :],
                                                 ps[0:KC, 0:4 * D].rearrange("p (c d) -> p c d", d=D), bv, ALU.add)
                        i_.then_inc(dve_out, 1)

                def build_bias(load_no, nxt):
                    if kind == 3:
                        return
                    dve.wait_ge(ld_mask, (load_no + 1) * 16)
                    b = bias[nxt][:, 0:S2]
                    if kind == 0:
                        i_ = v.tensor_scalar(b, keep[:], FLT_MAX, -FLT_MAX, ALU.mult, ALU.add)
                    elif kind == 1:
                        i_ = v.tensor_scalar(b, mask[:], NEG_MASK, -NEG_MASK, ALU.mult, ALU.add)
                    else:
                        i_ = v.scalar_tensor_tensor(out=b, in0=pad[:], scalar=-FLT_MAX, in1=attn[:],
                                                    op0=ALU.mult, op1=ALU.add)
                    i_.then_inc(bias_ready, 1)

                def ln_stats(load_no, c):
                    if c == 0:
                        dve.wait_ge(ld_ctx, (load_no + 1) * 32)
                    v.bn_stats(st[:, c, :], cn[:, c, :]).then_inc(ln, 1)

                def ln_var(load_no, c):
                    wait_apart(dve, ready, ln, load_no * 25 + (c + 1))
                    v.bn_aggr(mv[:, c, :], st[:, c, :]).then_inc(var_ready, 1)

                def ln_apply(load_no, nxt, c):
                    if c == 0:
                        dve.wait_ge(rstd_ready, load_no + 1)
                    v.tensor_scalar(V[nxt][:, c, :], cn[:, c, :], mv[:, c, 0:1], rs[:, c:c + 1],
                                    ALU.subtract, ALU.mult).then_inc(ln, 1)

                def ln_affine(load_no, nxt):
                    x = V[nxt][:, 0:NC_CTX, :]
                    g1, b1 = (W[k][0:KC, :].rearrange("p (a d) -> p a d", a=1).broadcast_to([KC, NC_CTX, D])
                              for k in ("g1", "b1"))
                    dve.wait_ge(ln, load_no * 25 + 24)
                    v.tensor_tensor(x, x, g1, ALU.mult).then_inc(ln, 1)
                    dve.wait_ge(ln, load_no * 25 + 25)
                    v.tensor_tensor(x, x, b1, ALU.add).then_inc(xn_ready, 1)

                for n, t in enumerate(r_ps):
                    v.memset(t[:], 0.0).then_inc(x_done, 1)
                extra = 2
                if kind == 0:
                    v.memset(cn[96:KC, NC_CTX - 1, :], 0.0).then_inc(x_done, 1)
                    for t in bias:
                        v.memset(t[:, S2:keys], 0.0).then_inc(x_done, 1)
                    extra += 3
                if kind == 3:
                    for t in bias:
                        v.memset(t[:], 0.0).then_inc(x_done, 1)
                    extra += 2
                dve.wait_ge(x_done, extra)
                if kind == 2:
                    dve.wait_ge(ld_const, 16)
                v.memset(upd[:], 0.0).then_inc(ready, 1)

                if kind == 0:
                    for c in range(NC_CTX):
                        ln_stats(0, c)
                    for c in range(NC_CTX):
                        ln_var(0, c)
                    for c in range(NC_CTX):
                        ln_apply(0, 0, c)
                    ln_affine(0, 0)
                build_bias(0, 0)
                projected(first, 0, 0, part_a + part_b)
                with dve.Fori(0, B // 2) as i:
                    for par in range(2):
                        n = i * 2 + par
                        for s in range(H):
                            masked(n, par, s)
                            if s >= 2:
                                turned(n, par, s - 2)
                            if kind == 0:
                                if s % 4 == 1 and s > 1:
                                    recip(n, par, s // 4 - 1)
                                if s % 4 == 3 and s > 3:
                                    divide(n, s // 4 - 1)
                                if 1 <= s <= 6:
                                    ln_stats(n + 1, 2 * s - 2)
                                    ln_stats(n + 1, 2 * s - 1)
                                if 7 <= s <= 12:
                                    ln_var(n + 1, 2 * s - 14)
                                    ln_var(n + 1, 2 * s - 13)
                                if s >= 14:
                                    for c in range(6 * (s - 14), 6 * (s - 13)):
                                        ln_apply(n + 1, 1 - par, c)
                            if s == 7:
                                build_bias(n + 1, 1 - par)
                        projected(ring, n, 1 - par, part_a)
                        for h in range(max(H - 2, 0), H):
                            turned(n, par, h)
                        recip(n, par, G - 1)
                        if kind == 0:
                            ln_affine(n + 1, 1 - par)
                        divide(n, G - 1)
                        projected(ring, n, 1 - par, part_b)
                        dve.wait_ge(folded, (n + 1) * (G if kind == 0 else 1))
                        if kind == 0:
                            src = out_ps[0:T, 0:D]
                        else:
                            v.tensor_tensor(upd[:], out_ps[0:T, 0:D], W["bo"][0:T, :], ALU.add).then_inc(upd_ready, 1)
                            dve.wait_ge(upd_ready, n + 1)
                            src = upd[:]
                        v.scalar_tensor_tensor(out=X[:, n, :], in0=src, scalar=gate, in1=X[:, n, :],
                                               op0=ALU.mult, op1=ALU.add).then_inc(x_done, 1)


def queries(nc, K, name, w, bias_col, scale, XT, q):
    with Scope(nc, name) as s:
        ps = s.banks("q", 2)
        full, done = s.sem("full"), s.sem("done")
        with nc.Block() as block:

            @block.tensor
            def _(pe):
                for n in range(2):
                    nc.tensor.matmul(ps[n][:, 0:4 * T], w, XT[:, n * 4 * T:(n + 1) * 4 * T], start=True,
                                     stop=True).then_inc(full, 1)

            @block.vector
            def _(dve):
                for n in range(2):
                    dve.wait_ge(full, n + 1)
                    nc.vector.tensor_scalar(q[:, n * 4 * T:(n + 1) * 4 * T], ps[n][:, 0:4 * T], bias_col, scale,
                                            ALU.add, ALU.mult).then_inc(done, 1)


def load(nc, name, loads):
    with Scope(nc, name) as s:
        ld = s.sem("loaded")
        with nc.Block() as block:

            @block.sync
            def _(sp):
                for to, src in loads:
                    sp.dma_start(to, src).then_inc(ld, 16)
                sp.wait_ge(ld, 16 * len(loads))


def col(ap):
    return ap.rearrange("(p a) -> p a", a=1)


def fold_heads(nc, K, W, wqT, wkT, wvT, wout):
    jobs = [(W["qk"], wqT, wkT, 0.125), (W["vo"], wvT, wout, 1.0)]
    with Scope(nc, "fold") as s:
        ps = s.banks("f", 4)
        full, done = s.sem("full"), s.sem("done")
        with nc.Block() as block:

            @block.tensor
            def _(pe):
                n = 0
                for to, left, right, _ in jobs:
                    for h8 in range(0, NH, 8):
                        for odd in range(2):
                            if n >= 4:
                                pe.wait_ge(done, n - 3)
                            if n:
                                pe.wait_ge(full, n)
                            r = slice(64 * odd, 64 * odd + 64)
                            for x in range(4):
                                i_ = nc.tensor.matmul(ps[n % 4][:, x * D:(x + 1) * D], left[r, h8 // 2 + x, :],
                                                      right[r, h8 // 2 + x, :], start=True, stop=True)
                            i_.then_inc(full, 1)
                            n += 1

            @block.vector
            def _(dve):
                n = 0
                for to, _, _, scale in jobs:
                    for h8 in range(0, NH, 8):
                        for odd in range(2):
                            dve.wait_ge(full, n + 1)
                            to2 = to[:].rearrange("p (h o) d -> p h o d", o=2)[:, h8 // 2:h8 // 2 + 4, odd, :]
                            nc.vector.tensor_scalar(to2, ps[n % 4][:].rearrange("p (h d) -> p h d", d=D),
                                                    scale, None, ALU.mult).then_inc(done, 1)
                            n += 1


def head_outputs(nc, K, name, wo, to):
    with Scope(nc, name) as s:
        done = s.sem("done")
        with nc.Block() as block:

            @block.vector
            def _(dve):
                for j in range(4):
                    nc.vector.tensor_scalar(to[:, j, :], wo, K["jm"][:, j:j + 1], None, ALU.mult).then_inc(done, 1)


def route(nc, K, kind, XT, wr, gates, gate_bias=None):
    E = wr.shape[-1]
    with Scope(nc, f"route{kind}") as s:
        lg_ps, cnt_ps = s.banks("lg", 1)[0], s.banks("cnt", 1)[0]
        sc, ch, sel = s.sb("scores", [T, B, E]), s.sb("choice", [T, B, E]), s.sb("chosen", [T, B, E])
        top = s.sb("top", [T, B, 8])
        r1 = s.sb("r1", [T, B])
        full, act_done, order, cnt = s.sem("full"), s.sem("act_done"), s.sem("dve_order"), s.sem("counted")
        sel_ready = s.sem("chosen_ready")
        v = nc.vector

        def per_token(ap):
            return ap.rearrange("t (b a) -> t b a", a=1).broadcast_to([T, B, E])

        def rank_below(link, x, lt, n, groups, k, out, cmp, eq):
            a = x.rearrange("t (b g a) -> t b g a", g=n, a=1).broadcast_to([T, groups, n, n])
            b_ = x.rearrange("t (b a j) -> t b a j", a=1, j=n).broadcast_to([T, groups, n, n])
            m = lt.rearrange("t (a g) j -> t a g j", a=1).broadcast_to([T, groups, n, n])
            link(v.tensor_tensor(cmp, b_, a, ALU.is_gt))
            link(v.tensor_tensor(eq, b_, a, ALU.is_equal))
            link(v.tensor_tensor(eq, eq, m, ALU.mult))
            link(v.tensor_tensor(cmp, cmp, eq, ALU.add))
            link(v.tensor_reduce(out, cmp, AX.X, ALU.add))
            link(v.tensor_scalar(out, out, k - 0.5, None, ALU.is_lt))

        if kind == 2:
            top2 = s.sb("top2", [T, B, 4, 8])
            gs, gm = s.sb("group_score", [T, B * 4]), s.sb("group_mask", [T, B * 4])
            cmp, eq = s.sb("cmp", [T, B, 4, 4]), s.sb("eq", [T, B, 4, 4])
            mrep = s.sb("replaced", [T, B, E])
        if kind == 3:
            cmp, eq = s.sb("cmp", [T, B, E, E]), s.sb("eq", [T, B, E, E])
            before = s.sb("before", [T, B, E])
        with nc.Block() as block:

            @block.tensor
            def _(pe):
                for b in range(B):
                    i_ = nc.tensor.matmul(lg_ps[0:T, b * E:(b + 1) * E], XT[:, b * T:(b + 1) * T], wr, start=True,
                                          stop=True)
                i_.then_inc(full, 1)
                if kind == 3:
                    pe.wait_ge(sel_ready, 1)
                    nc.tensor.matmul(cnt_ps[0:T, 0:B * E], K["tri"][:], sel[:].rearrange("t b e -> t (b e)"),
                                     start=True, stop=False)
                    nc.tensor.matmul(cnt_ps[0:T, 0:B * E], K["ones"][:], before[:].rearrange("t b e -> t (b e)"),
                                     start=False, stop=True).then_inc(cnt, 1)

            @block.scalar
            def _(act):
                if kind == 2:
                    act.wait_ge(full, 1)
                    nc.scalar.activation(sc[:].rearrange("t b e -> t (b e)"), lg_ps[0:T, 0:B * E],
                                         ACT.Sigmoid).then_inc(act_done, 1)
                elif kind == 3:
                    act.wait_ge(order, 2)
                    nc.scalar.activation(ch[:], ch[:], ACT.Exp).then_inc(act_done, 1)
                else:
                    act.wait_ge(order, B + 1 + 1)
                    nc.scalar.activation(r1[:], r1[:], ACT.Exp).then_inc(act_done, 1)

            @block.vector
            def _(dve):
                link = Link(dve, order)
                lg = lg_ps[0:T, 0:B * E].rearrange("t (b e) -> t b e", e=E)
                if kind == 0:
                    dve.wait_ge(full, 1)
                    link(v.tensor_copy(sc[:], lg))
                    for b in range(B):
                        link(v.max(top[:, b, :], sc[:, b, :]))
                    link(v.tensor_tensor(r1[:], top[:, :, 1], top[:, :, 0], ALU.subtract))
                    dve.wait_ge(act_done, 1)
                    link(v.tensor_scalar(r1[:], r1[:], 1.0, None, ALU.add))
                    link(v.reciprocal(r1[:], r1[:]))
                    link(v.tensor_scalar(r1[:], r1[:], 1.0, None, ALU.is_ge))
                    link(v.tensor_tensor(sel[:], sc[:], top[:, :, 0:1].broadcast_to([T, B, E]), ALU.is_ge))
                    link(v.tensor_tensor(gates[:], sel[:], per_token(r1[:]), ALU.mult))
                if kind == 2:
                    dve.wait_ge(act_done, 1)
                    gb = gate_bias.rearrange("t (a e) -> t a e", a=1).broadcast_to([T, B, E])
                    link(v.tensor_tensor(ch[:], sc[:], gb, ALU.add))
                    for b in range(B):
                        for g in range(4):
                            i_ = v.max(top2[:, b, g, :], ch[:, b, 8 * g:8 * g + 8])
                            i_.then_inc(order, 1)
                            link.n += 1
                    dve.wait_ge(order, link.n)
                    link(v.tensor_tensor(gs[:].rearrange("t (b g) -> t b g", g=4), top2[:, :, :, 0],
                                         top2[:, :, :, 1], ALU.add))
                    rank_below(link, gs[:], K["lt4"][0:T], 4, B, 2, gm[:].rearrange("t (b g) -> t b g", g=4),
                               cmp[:], eq[:])
                    link(v.tensor_tensor(ch[:].rearrange("t b (g e) -> t (b g) e", e=8),
                                         ch[:].rearrange("t b (g e) -> t (b g) e", e=8),
                                         gm[:].rearrange("t (g a) -> t g a", a=1).broadcast_to([T, B * 4, 8]), ALU.mult))
                    for b in range(B):
                        link(v.max(top[:, b, :], ch[:, b, :]))
                        link(v.match_replace(out=mrep[:, b, :], in_to_replace=top[:, b, :], in_values=ch[:, b, :],
                                             imm_value=-1e30))
                    link(v.tensor_tensor(sel[:], mrep[:], ch[:], ALU.not_equal))
                    link(v.tensor_tensor(sc[:], sc[:], sel[:], ALU.mult))
                    link(v.tensor_reduce(r1[:], sc[:], AX.X, ALU.add))
                    link(v.tensor_scalar(r1[:], r1[:], 1e-20, None, ALU.add))
                    link(v.reciprocal(r1[:], r1[:]))
                    link(v.tensor_scalar(r1[:], r1[:], 2.5, None, ALU.mult))
                    link(v.tensor_tensor(gates[:], sc[:], per_token(r1[:]), ALU.mult))
                if kind == 3:
                    dve.wait_ge(full, 1)
                    link(v.tensor_reduce(r1[:], lg, AX.X, ALU.max))
                    link(v.tensor_tensor(ch[:], lg, per_token(r1[:]), ALU.subtract))
                    dve.wait_ge(act_done, 1)
                    link(v.tensor_reduce(r1[:], ch[:], AX.X, ALU.add))
                    link(v.reciprocal(r1[:], r1[:]))
                    link(v.tensor_tensor(sc[:], ch[:], per_token(r1[:]), ALU.mult))
                    rank_below(link, sc[:].rearrange("t b e -> t (b e)"), K["lt8"][0:T], 8, B, 2, sel[:], cmp[:], eq[:])
                    link(v.memset(before[:, 0, :], 0.0))
                    for b in range(1, B):
                        link(v.tensor_tensor(before[:, b, :], before[:, b - 1, :], sel[:, b - 1, :], ALU.add))
                    v.memset(ch[:], 0.0).then_inc(sel_ready, 1)
                    link(v.tensor_tensor(sc[:], sc[:], sel[:], ALU.mult))
                    dve.wait_ge(cnt, 1)
                    link(v.tensor_scalar(sel[:].rearrange("t b e -> t (b e)"), cnt_ps[0:T, 0:B * E], 511.5, None, ALU.is_lt))
                    link(v.tensor_tensor(gates[:], sc[:], sel[:], ALU.mult))


def ffn(nc, K, kind, XT, units, width, rows, down, gates=None):
    NU, NCK = len(units), len(rows)
    X = K["X"]
    gate = K["gate"][0:T, 4 + kind:5 + kind]
    act_fn = ACT.Relu if kind == 0 else ACT.Silu
    NG = sum(u[4] is not None for u in units)
    groups = [list(range(c, min(c + 4, NCK))) for c in range(0, NCK, 4)]
    ring = Ring([(k, "v" if len(groups) == 1 or k % 2 else "a") for k in range(len(groups))])
    NQ = 17
    with Scope(nc, f"ffn{kind}") as s:
        xT = [s.sb(f"xT{i}", [P, T]) for i in range(2)]
        h = [s.sb(f"h{i}", [T, width]) for i in range(2)]
        hT = s.sb("hT", [P, NCK, T])
        sg = [s.sb(f"act{i}", [T, 512]) for i in range(2)]
        q = quant_buffers(s, T, width) if kind == 1 else None
        a_ps, g_ps = s.banks("a", 2), s.banks("g", 2)
        t_ps, out_ps = s.banks("t", 2), s.banks("o", 1)[0]
        ready = s.sem("ready")
        x_ready = s.sem("x_ready")
        up_full = s.sem("up_full")
        act_ready = s.sem("act_ready")
        h_ready = s.sem("h_ready")
        h_gated = s.sem("h_gated")
        h_round = s.sem("h_rounded")
        ring_full, act_out, dve_out = s.sem("ring_full"), s.sem("act_emptied"), s.sem("dve_emptied")
        out_full, x_done = s.sem("out_full"), s.sem("x_done")
        out_of = {"a": act_out, "v": dve_out}
        with nc.Block() as block:

            @block.tensor
            def _(pe):
                def up(load_no, nxt):
                    pe.wait_ge(x_ready, load_no + 1)
                    for u, (wa, wg, _, n, _) in enumerate(units):
                        if u >= 2:
                            pe.wait_ge(h_ready, load_no * NU + (u - 1))
                        elif not isinstance(load_no, int):
                            pe.wait_ge(h_ready, load_no * NU)
                        i_ = nc.tensor.matmul(a_ps[u % 2][0:T, 0:n], xT[nxt][:], wa, start=True, stop=True)
                        if wg is not None:
                            i_ = nc.tensor.matmul(g_ps[u % 2][0:T, 0:n], xT[nxt][:], wg, start=True, stop=True)
                        i_.then_inc(up_full, 1)

                pe.wait_ge(ready, 1)
                up(0, 0)
                with pe.Fori(0, B // 2) as i:
                    for par in range(2):
                        n = i * 2 + par
                        up(n + 1, 1 - par)
                        pe.wait_ge(h_ready, (n + 1) * NU)
                        if NG:
                            pe.wait_ge(h_gated, (n + 1) * NG)
                        if kind == 1:
                            pe.wait_ge(h_round, (n + 1) * NQ)
                        for k, ch in enumerate(groups):
                            if k >= 2:
                                prev, e = ring.jobs[k - 2]
                                pe.wait_ge(out_of[e], ring.emptied(n, prev, e))
                            for x, c in enumerate(ch):
                                i_ = nc.tensor.transpose(t_ps[k % 2][0:rows[c], x * T:(x + 1) * T],
                                                         h[par][:, sum(rows[:c]):sum(rows[:c + 1])], K["ident"][0:T, 0:T])
                            i_.then_inc(ring_full, 1)
                        for k, ch in enumerate(groups):
                            pe.wait_ge(out_of[ring.engine(k)], ring.emptied(n, k, ring.engine(k)))
                            if k == 0:
                                pe.wait_ge(x_done, n + len(t_ps))
                            for c in ch:
                                i_ = nc.tensor.matmul(out_ps[0:T, 0:D], hT[0:rows[c], c, :], down[0:rows[c], c, :],
                                                      start=(c == 0), stop=(c == NCK - 1))
                        i_.then_inc(out_full, 1)

            def empty(eng, copy, n, e, done):
                for k, ch in enumerate(groups):
                    if ring.engine(k) == e:
                        eng.wait_ge(ring_full, ring.full(n, k))
                        copy(hT[:, ch[0]:ch[0] + len(ch), :],
                             t_ps[k % 2][:, 0:len(ch) * T].rearrange("p (c t) -> p c t", t=T)).then_inc(done, 1)

            @block.scalar
            def _(act):
                def first_half(load_no, b, nxt):
                    nc.scalar.copy(xT[nxt][:], XT[:, bass.ds(b * T, T)]).then_inc(x_ready, 1)
                    for u, (_, _, _, n, _) in enumerate(units):
                        act.wait_ge(up_full, load_no * NU + (u + 1))
                        if u >= 2:
                            act.wait_ge(h_ready, load_no * NU + (u - 1))
                        elif not isinstance(load_no, int):
                            act.wait_ge(h_ready, load_no * NU)
                        nc.scalar.activation(sg[u % 2][:, 0:n], a_ps[u % 2][0:T, 0:n], act_fn).then_inc(act_ready, 1)

                act.wait_ge(ready, 1)
                first_half(0, 0, 0)
                with act.Fori(0, B // 2) as i:
                    for par in range(2):
                        n = i * 2 + par
                        first_half(n + 1, (n + 1) % B, 1 - par)
                        empty(act, nc.scalar.copy, n, "a", act_out)

            @block.vector
            def _(dve):
                v = nc.vector

                def products(load_no, b, nxt):
                    gated = 0
                    for u, (_, wg, c0, n, e) in enumerate(units):
                        dve.wait_ge(act_ready, load_no * NU + (u + 1))
                        hu = h[nxt][:, c0:c0 + n]
                        v.tensor_tensor(hu, sg[u % 2][:, 0:n], sg[u % 2][:, 0:n] if wg is None else g_ps[u % 2][0:T, 0:n],
                                        ALU.mult).then_inc(h_ready, 1)
                        if e is not None:
                            dve.wait_ge(h_ready, load_no * NU + (u + 1))
                            ne = e[1] - e[0]
                            w = gates[:, b, e[0]:e[1]].rearrange("t (e a) -> t e a", a=1).broadcast_to([T, ne, n // ne])
                            hv = hu.rearrange("t (e f) -> t e f", e=ne)
                            v.tensor_tensor(hv, hv, w, ALU.mult).then_inc(h_gated, 1)
                    if kind == 1:
                        dve.wait_ge(h_ready, (load_no + 1) * NU)
                        link = Link(dve, h_round, load_no * NQ)
                        fp4_round(nc, link, q, h[nxt][:], h[nxt][:])
                        assert link.n == NQ

                for n, t in enumerate(t_ps):
                    v.memset(t[:], 0.0).then_inc(x_done, 1)
                dve.wait_ge(x_done, 2)
                v.memset(sg[0][:, 0:1], 0.0).then_inc(ready, 1)
                products(0, 0, 0)
                with dve.Fori(0, B // 2) as i:
                    for par in range(2):
                        n = i * 2 + par
                        products(n + 1, (n + 1) % B, 1 - par)
                        empty(dve, v.tensor_copy, n, "v", dve_out)
                        dve.wait_ge(out_full, n + 1)
                        v.scalar_tensor_tensor(out=X[:, n, :], in0=out_ps[0:T, 0:D], scalar=gate, in1=X[:, n, :],
                                               op0=ALU.mult, op1=ALU.add).then_inc(x_done, 1)


def layer0(nc, K, ins, ctxT_dram):
    with Scope(nc, "L0a") as s:
        W = {"qk": s.sb("qk", [P, NH, D]), "vo": s.sb("vo", [P, NH, D]), "g1": s.sb("g1", [P, D]),
             "b1": s.sb("b1", [P, D]), "lat": s.sb("lat", [T, B, D]), "latT": s.sb("latT", [P, B * T])}
        with Scope(nc, "L0w") as w:
            wq, wkv, wout = w.sb("wq", [P, 1024]), w.sb("wkv", [P, 2048]), w.sb("wout", [P, 8, D])
            wqT, wkT, wvT = w.sb("wqT", [P, 8, D]), w.sb("wkT", [P, 8, D]), w.sb("wvT", [P, 8, D])
            jobs = []
            for n in range(8):
                jobs.append((wqT[:, n, :], wq[:, n * D:(n + 1) * D]))
                jobs.append((wkT[:, n, :], wkv[:, n * D:(n + 1) * D]))
                jobs.append((wvT[:, n, :], wkv[:, 1024 + n * D:1024 + (n + 1) * D]))
            transposes(nc, K, "L0t", jobs, [
                (wq[:], ins["L0_xattn_Wq"]), (wkv[:], ins["L0_xattn_Wkv"]),
                (wout[:], ins["L0_xattn_Wout"].rearrange("(n p) d -> p n d", p=P)),
                (W["g1"][:], bcast_rows(ins["L0_xattn_g1"], P, D)), (W["b1"][:], bcast_rows(ins["L0_xattn_b1"], P, D))])
            fold_heads(nc, K, W, wqT, wkT, wvT, wout)
        normalise(nc, K, "ln0a", W["lat"], W["latT"], affine=(ins["L0_xattn_g2"], ins["L0_xattn_b2"]))
        attention(nc, K, 0, W, ins, ctxT_dram)
    with Scope(nc, "L0f") as s:
        up, down, wr = s.sb("up", [P, 576]), s.sb("down", [P, 5, D]), s.sb("wr", [P, 8])
        XN, XT, gates = s.sb("XN", [T, B, D]), s.sb("XT", [P, B * T]), s.sb("gates", [T, B, 8])
        load(nc, "L0l", [
            (up[:, 0:512].rearrange("d (e f) -> d e f", e=8), ins["L0_ffn_W1"].rearrange("e d f -> d e f")),
            (up[:, 512:576], ins["L0_ffn_Ws1"]), (wr[:], ins["L0_ffn_Wr"]),
            (down[:, 0:4, :], ins["L0_ffn_W2"].rearrange("e f d -> (e f) d").rearrange("(c p) d -> p c d", p=P)),
            (down[0:64, 4, :], ins["L0_ffn_Ws2"])])
        normalise(nc, K, "ln0f", XN, XT)
        route(nc, K, 0, XT, wr[:], gates)
        ffn(nc, K, 0, XT, [(up[:, 0:512], None, 0, 512, (0, 8)), (up[:, 512:576], None, 512, 64, None)], 576,
            [P] * 4 + [64], down, gates)


def plain_attention(nc, K, kind, ins, ctxT_dram, names, turned):
    wq_n, wk_n, wv_n, wo_n, bq_n, bk_n, bv_n, bo_n = names
    with Scope(nc, f"L{kind}a") as s:
        wq, wk, wv, wo = (s.sb(n, [P, D]) for n in ("wq", "wk", "wv", "wo"))
        W = {"k": wk, "v": wv, "bk": s.sb("bk", [P, 1]), "bv": s.sb("bv", [P, D]), "bo": s.sb("bo", [P, D]),
             "q": s.sb("q", [P, B * T]), "o": s.sb("o", [P, 4 if kind != 3 else 1, D])}
        bq = s.sb("bq", [P, 1])
        small = [(bq[:], col(ins[bq_n])), (W["bv"][:], bcast_rows(ins[bv_n], P, D)),
                 (W["bo"][:], bcast_rows(ins[bo_n], P, D)),
                 (W["bk"][:], col(ins[bk_n]) if bk_n else K["zero"].rearrange("(p a) -> p a", a=1))]
        if turned:
            with Scope(nc, f"L{kind}aw") as w:
                raw = [w.sb(n, [P, D]) for n in ("q", "k", "v", "o")]
                to = [wq[:], wk[:], wv[:], wo[:]]
                transposes(nc, K, f"L{kind}at", [(t, r[:]) for t, r in zip(to, raw)],
                           [(r[:], ins[n]) for r, n in zip(raw, (wq_n, wk_n, wv_n, wo_n))] + small)
        else:
            load(nc, f"L{kind}l", [(t[:], ins[n]) for t, n in zip((wq, wk, wv, wo), (wq_n, wk_n, wv_n, wo_n))] + small)
        if kind == 3:
            W["o"] = wo[:].rearrange("p (a d) -> p a d", a=1)
        else:
            head_outputs(nc, K, f"ho{kind}", wo[:], W["o"])
        with Scope(nc, f"L{kind}an") as n_:
            XN, XT = n_.sb("XN", [T, B, D]), n_.sb("XT", [P, B * T])
            normalise(nc, K, f"ln{kind}a", XN, XT)
            queries(nc, K, f"q{kind}", wq[:], bq[:, 0:1], float(D if kind == 3 else D // NH) ** -0.5, XT, W["q"])
        attention(nc, K, kind, W, ins, ctxT_dram)


def layer1_ffn(nc, K, ins):
    I = 352
    with Scope(nc, "L1f") as s:
        up, down = s.sb("up", [P, 2, I]), s.sb("down", [P, 3, D])
        XN, XT = s.sb("XN", [T, B, D]), s.sb("XT", [P, B * T])
        rows = [128, 128, 96]
        with Scope(nc, "L1w") as w:
            raw, rawd = w.sb("raw", [P, 6, D]), w.sb("rawd", [P, I])
            loads, jobs, quants = [(rawd[:], ins["L1_ffn_w_down"])], [], []
            for m, name in enumerate(("L1_ffn_w_gate", "L1_ffn_w_up")):
                for c, r in enumerate(rows):
                    a = raw[0:r, 3 * m + c, :]
                    loads.append((a, ins[name][c * P:c * P + r, :]))
                    jobs.append((up[:, m, c * P:c * P + r], a))
                    quants.append(a)
            quants.append(rawd[:])
            for c, r in enumerate(rows):
                jobs.append((down[0:r, c, :], rawd[:, c * P:c * P + r]))
            transposes(nc, K, "L1t", jobs, loads, quants)
        normalise(nc, K, "ln1f", XN, XT, quant=True)
        ffn(nc, K, 1, XT, [(up[:, 0, :], up[:, 1, :], 0, I, None)], I, rows, down)


def layer2_ffn(nc, K, ins):
    E, I = 32, 64
    N = E * I // P
    with Scope(nc, "L2f") as s:
        wg, wu = s.sb("wg", [P, N + 1, P]), s.sb("wu", [P, N + 1, P])
        down, wr, gb = s.sb("down", [P, N + 1, D]), s.sb("wr", [P, E]), s.sb("gb", [T, E])
        gates, XT = s.sb("gates", [T, B, E]), s.sb("XT", [P, B * T])
        with Scope(nc, "L2w") as w:
            rg, ru, rd, rr = w.sb("rg", [P, N + 1, D]), w.sb("ru", [P, N + 1, D]), w.sb("rd", [P, N + 1, P]), w.sb("rr", [E, D])
            loads, jobs = [(rr[:], ins["L2_ffn_gate_w"]), (gb[:], bcast_rows(ins["L2_ffn_gate_bias"], T, E))], []
            for raw, to, a, b in ((rg, wg, "gate", "gate"), (ru, wu, "up", "up")):
                loads.append((raw[:, 0:N, :], ins[f"L2_ffn_expert_{a}"].rearrange("e i h -> (e i) h")
                              .rearrange("(c p) h -> p c h", p=P)))
                loads.append((raw[:, N, :], ins[f"L2_ffn_shared_{b}"]))
                jobs += [(to[:, c, :], raw[:, c, :]) for c in range(N + 1)]
            loads.append((rd[:, 0:N, :].rearrange("h c (e i) -> h (c e) i", i=I),
                          ins["L2_ffn_expert_down"].rearrange("e h i -> h e i")))
            loads.append((rd[:, N, :], ins["L2_ffn_shared_down"]))
            jobs += [(down[:, c, :], rd[:, c, :]) for c in range(N + 1)]
            jobs.append((wr[:], rr[:]))
            transposes(nc, K, "L2t", jobs, loads)
        with Scope(nc, "L2n") as n_:
            XN = n_.sb("XN", [T, B, D])
            normalise(nc, K, "ln2f", XN, XT)
        route(nc, K, 2, XT, wr[:], gates, gb[:])
        flat = lambda t, c, n: t[:, c:c + n, :].rearrange("p c f -> p (c f)")
        units = [(flat(wg, 4 * k, 4), flat(wu, 4 * k, 4), 512 * k, 512, (8 * k, 8 * k + 8)) for k in range(4)]
        units.append((flat(wg, N, 1), flat(wu, N, 1), N * P, P, None))
        ffn(nc, K, 2, XT, units, (N + 1) * P, [P] * (N + 1), down, gates)


def layer3_ffn(nc, K, ins):
    E, F = 8, 192
    with Scope(nc, "L3f") as s:
        fc, down, wr = s.sb("fc", [P, E, 2 * F]), s.sb("down", [P, E * F // P, D]), s.sb("wr", [P, E])
        gates, XT, XN = s.sb("gates", [T, B, E]), s.sb("XT", [P, B * T]), s.sb("XN", [T, B, D])
        load(nc, "L3l", [(fc[:], ins["L3_ffn_c_fc"].rearrange("e d f -> d e f")), (wr[:], ins["L3_ffn_w_gate"]),
                         (down[:], ins["L3_ffn_c_proj"].rearrange("e f d -> (e f) d").rearrange("(c p) d -> p c d", p=P))])
        normalise(nc, K, "ln3f", XN, XT)
        route(nc, K, 3, XT, wr[:], gates)
        units = [(fc[:, 2 * k:2 * k + 2, 0:F], fc[:, 2 * k:2 * k + 2, F:2 * F], 2 * k * F, 2 * F, (2 * k, 2 * k + 2))
                 for k in range(E // 2)]
        ffn(nc, K, 3, XT, units, E * F, [P] * (E * F // P), down, gates)


def flamingo(nc, ins, out):
    with Scope(nc, "k") as s:
        K = {"X": s.sb("X", [T, B, D]), "gate": s.sb("gate", [P, 8]), "ident": s.sb("ident", [P, P]),
             "hm": s.sb("hm", [P, NH]), "jm": s.sb("jm", [P, 4]), "lt4": s.sb("lt4", [P, 4, 4]),
             "lt8": s.sb("lt8", [P, 8, 8]), "tri": s.sb("tri", [T, T]), "ones": s.sb("ones", [T, T]),
             "mhalf": s.sb("mhalf", [P, 16])}
        ctxT_dram = nc.dram_tensor("ctxT", [B, P, S2], F32, kind="Internal").ap()
        K["zero"] = ins["zero"]
        constants(nc, K, ins)
        load(nc, "x", [(K["X"][:], ins["x"].rearrange("b t d -> t b d"))])
        layer0(nc, K, ins, ctxT_dram)
        give_back(nc, Scope.used)
        n1 = [f"L1_xattn_{n}" for n in ("wq_k", "wk_k", "wv_k", "wo_k", "wq_b", "wk_b", "wv_b", "wo_b")]
        n2 = [f"L2_xattn_{n}" for n in ("Wq", "Wk", "Wv", "Wo", "bq", "bk", "bv", "bo")]
        n3 = ["L3_xattn_Wq", "L3_xattn_Wk", "L3_xattn_Wv", "L3_xattn_Wo", "L3_xattn_bq", None, "L3_xattn_bv",
              "L3_xattn_bo"]
        plain_attention(nc, K, 1, ins, ctxT_dram, n1, False)
        layer1_ffn(nc, K, ins)
        give_back(nc, Scope.used)
        plain_attention(nc, K, 2, ins, ctxT_dram, n2, True)
        layer2_ffn(nc, K, ins)
        give_back(nc, Scope.used)
        plain_attention(nc, K, 3, ins, ctxT_dram, n3, True)
        layer3_ffn(nc, K, ins)
        load(nc, "y", [(out.rearrange("b t d -> t b d"), K["X"][:])])


_SKIP = ("fside_Bx16xSxS2_0",)


def kernel(**inputs):
    import concourse.bacc as bacc
    from concourse.bass_utils import run_bass_kernel_spmd

    nc = bacc.Bacc("TRN2", target_bir_lowering=False, num_devices=1)
    arrays, ins = {}, {}
    for name, a in inputs.items():
        if name in _SKIP:
            continue
        a = np.ascontiguousarray(a)
        arrays[f"in_{name}"] = a
        ins[name] = nc.dram_tensor(f"in_{name}", a.shape, mybir.dt.from_np(a.dtype), kind="ExternalInput").ap()
    arrays["in_zero"] = np.zeros(P, np.float32)
    ins["zero"] = nc.dram_tensor("in_zero", [P], F32, kind="ExternalInput").ap()
    out = nc.dram_tensor("out", [B, T, D], F32, kind="ExternalOutput").ap()
    flamingo(nc, ins, out)
    r = run_bass_kernel_spmd(nc, [arrays], core_ids=[0])
    return r.results[0]["out"]
```

```python
from contextlib import ExitStack

import numpy as np

import concourse.bass as bass
from concourse import mybir

ALU = mybir.AluOpType
ACT = mybir.ActivationFunctionType
AX = mybir.AxisListType
F32 = mybir.dt.float32
I32 = mybir.dt.int32
U32 = mybir.dt.uint32
U8 = mybir.dt.uint8
BF16 = mybir.dt.bfloat16

B, T, S2, D = 8, 100, 1444, 128
P = 128
BANK = 512
KC = 121
NC_CTX = 12
LAST = S2 - (NC_CTX - 1) * KC
NH = 16
FLT_MAX = 3.4028234663852886e38
EPS = 1e-5
NEG_MASK = 1e9


def chunk_rows(c):
    return T if c == NC_CTX else (LAST if c == NC_CTX - 1 else KC)


def chunk_at(c):
    return S2 if c == NC_CTX else c * KC


def head_of(n):
    return 4 * (n % 4) + n // 4


class Link:

    def __init__(self, eng, sem, base=0):
        self.eng, self.sem, self.base, self.n = eng, sem, base, 0

    def __call__(self, ins):
        self.n += 1
        ins.then_inc(self.sem, 1)
        self.eng.wait_ge(self.sem, self.base + self.n)


def wait_apart(eng, passed, sem, value):
    if not isinstance(value, int):
        value = eng.to_reg(value)
        eng.wait_ge(passed, 1)
    eng.wait_ge(sem, value)


class Scope:

    used = []

    def __init__(self, nc, name):
        self.nc, self.name, self.ctx = nc, name, ExitStack()

    def __enter__(self):
        self.ctx.__enter__()
        return self

    def __exit__(self, *a):
        return self.ctx.__exit__(*a)

    def sb(self, name, shape, dt=F32):
        return self.ctx.enter_context(self.nc.sbuf_tensor(f"{self.name}_{name}", shape, dt))

    def banks(self, name, n):
        return [self.ctx.enter_context(self.nc.psum_tensor(f"{self.name}_{name}{i}", [P, BANK], F32))
                for i in range(n)]

    def sem(self, name):
        h = self.nc.alloc_semaphore(f"{self.name}_{name}")
        self.used.append(h)
        return h


def give_back(nc, used):
    nc.all_engine_barrier()
    nc.clear_and_free_semaphores(used)
    nc.all_engine_barrier()
    used.clear()


def bcast_rows(ap, rows, n):
    return ap.rearrange("(a n) -> a n", a=1).broadcast_to([rows, n])


def constants(nc, K, ins):
    with Scope(nc, "const") as s:
        ld, pool_sem, act_sem = s.sem("gates_loaded"), s.sem("pool_order"), s.sem("tanh_done")
        dve_sem, ones_set = s.sem("dve_order"), s.sem("ones_set")
        with nc.Block() as block:

            @block.sync
            def _(sp):
                sp.dma_start(K["gate"][:, 0:4], bcast_rows(ins["g_xattn"], P, 4)).then_inc(ld, 16)
                sp.dma_start(K["gate"][:, 4:8], bcast_rows(ins["g_ffn"], P, 4)).then_inc(ld, 16)

            @block.scalar
            def _(act):
                act.wait_ge(ld, 32)
                nc.scalar.activation(K["gate"][:], K["gate"][:], ACT.Tanh).then_inc(act_sem, 1)

            @block.vector
            def _(dve):
                for name in ("ident", "hm", "lt4", "lt8", "tri", "ones"):
                    nc.vector.memset(K[name][:], 0.0 if name == "ident" else 1.0).then_inc(ones_set, 1)
                nc.vector.memset(K["mhalf"][:], -0.5).then_inc(ones_set, 1)
                dve.wait_ge(pool_sem, 6)
                nc.vector.tensor_reduce(K["jm"][:], K["hm"][:].rearrange("p (j g) -> p j g", g=4),
                                        AX.X, ALU.add).then_inc(dve_sem, 1)

            @block.gpsimd
            def _(pool):
                pool.wait_ge(ones_set, 7)
                link = Link(pool, pool_sem)
                link(nc.gpsimd.affine_select(out=K["ident"][:], in_=K["ident"][:], compare_op=ALU.not_equal,
                                             fill=1.0, base=0, pattern=[[-1, P]], channel_multiplier=1))
                hm = K["hm"][:].rearrange("p (j g) -> p j g", g=4)
                link(nc.gpsimd.affine_select(out=hm, in_=hm, compare_op=ALU.is_ge, fill=0.0, base=0,
                                             pattern=[[-8, 4], [-32, 4]], channel_multiplier=1))
                link(nc.gpsimd.affine_select(out=hm, in_=hm, compare_op=ALU.is_ge, fill=0.0, base=7,
                                             pattern=[[8, 4], [32, 4]], channel_multiplier=-1))
                for name, n in (("lt4", 4), ("lt8", 8)):
                    m = K[name][:]
                    link(nc.gpsimd.affine_select(out=m, in_=m, compare_op=ALU.is_ge, fill=0.0, base=-1,
                                                 pattern=[[1, n], [-1, n]], channel_multiplier=0))
                link(nc.gpsimd.affine_select(out=K["tri"][:], in_=K["tri"][:], compare_op=ALU.is_ge, fill=0.0,
                                             base=-1, pattern=[[1, T]], channel_multiplier=-1))


def normalise(nc, K, name, XN, XT, affine=None, quant=False):
    X = K["X"]
    rounds = 2 if affine else 1
    with Scope(nc, name) as s:
        st, mv, rs = s.sb("stats", [T, B, 6]), s.sb("meanvar", [T, B, 2]), s.sb("rstd", [T, B])
        bc = s.sb("affine", [T, 2, D]) if affine else None
        q = quant_buffers(s, T, B * D) if quant else None
        xt_ps = s.banks("xt", 2)
        ld, var_ready, rstd_ready = s.sem("affine_loaded"), s.sem("var_ready"), s.sem("rstd_ready")
        order, pool_order = s.sem("dve_order"), s.sem("pool_order")
        xn_ready, xt_full, xt_done = s.sem("xn_ready"), s.sem("xt_full"), s.sem("xt_done")
        with nc.Block() as block:

            @block.sync
            def _(sp):
                if affine:
                    for n in range(2):
                        sp.dma_start(bc[:, n, :], bcast_rows(affine[n], T, D)).then_inc(ld, 16)

            @block.vector
            def _(dve):
                link = Link(dve, order)
                for r in range(rounds):
                    src = X if r == 0 else XN
                    for b in range(B):
                        i = nc.vector.bn_stats(st[:, b, :], src[:, b, :])
                        i.then_inc(order, 1)
                        link.n += 1
                    dve.wait_ge(order, link.n)
                    for b in range(B):
                        i = nc.vector.bn_aggr(mv[:, b, :], st[:, b, :])
                        i.then_inc(var_ready, 1)
                    dve.wait_ge(rstd_ready, r + 1)
                    for b in range(B):
                        i = nc.vector.tensor_scalar(XN[:, b, :], src[:, b, :], mv[:, b, 0:1], rs[:, b:b + 1],
                                                    ALU.subtract, ALU.mult)
                        i.then_inc(order, 1)
                        link.n += 1
                    dve.wait_ge(order, link.n)
                if affine:
                    dve.wait_ge(ld, 32)
                    for n, op in ((0, ALU.mult), (1, ALU.add)):
                        link(nc.vector.tensor_tensor(XN[:], XN[:], bc[:, n:n + 1, :].broadcast_to([T, B, D]), op))
                if quant:
                    flat = XN[:].rearrange("p b d -> p (b d)")
                    fp4_round(nc, link, q, flat, flat)
                nc.vector.memset(mv[:, 0, 0:1], 0.0).then_inc(xn_ready, 1)

            @block.gpsimd
            def _(pool):
                for r in range(rounds):
                    pool.wait_ge(var_ready, B * (r + 1))
                    nc.gpsimd.tensor_scalar(rs[:], mv[:, :, 1], EPS, None, ALU.add).then_inc(pool_order, 1)
                    pool.wait_ge(pool_order, r + 1)
                    nc.gpsimd.tensor_tensor(rs[:], rs[:], K["mhalf"][0:T, 0:B], ALU.pow).then_inc(rstd_ready, 1)

            @block.tensor
            def _(pe):
                pe.wait_ge(xn_ready, 1)
                for b in range(B):
                    i = nc.tensor.transpose(xt_ps[b // 4][:, (b % 4) * T:(b % 4 + 1) * T], XN[:, b, :],
                                            K["ident"][0:T, 0:T])
                    if b % 4 == 3:
                        i.then_inc(xt_full, 1)

            @block.scalar
            def _(act):
                for n in range(2):
                    act.wait_ge(xt_full, n + 1)
                    nc.scalar.copy(XT[:, n * 4 * T:(n + 1) * 4 * T], xt_ps[n][:, 0:4 * T]).then_inc(xt_done, 1)


def quant_buffers(s, rows, n):
    nb = n // 16
    return {"a": s.sb("q_abs", [rows, n]), "q": s.sb("q_code", [rows, n]), "sc": s.sb("q_scale", [rows, nb]),
            "rc": s.sb("q_rscale", [rows, nb])}


def fp4_round(nc, link, buf, out, src, rows=None):
    n = src.shape[-1]
    r = src.shape[0]
    a, q = buf["a"][0:r, 0:n], buf["q"][0:r, 0:n]
    sc, rc = buf["sc"][0:r, 0:n // 16], buf["rc"][0:r, 0:n // 16]
    blk = lambda ap: ap.rearrange("p (n k) -> p n k", k=16)
    wide = lambda ap: ap.rearrange("p (n k) -> p n k", k=1).broadcast_to([r, n // 16, 16])
    v = nc.vector
    link(v.tensor_reduce(sc, blk(src), AX.X, ALU.max, apply_absolute_value=True))
    link(v.tensor_scalar(sc, sc, 1.0 / 6.0, 1e-12, ALU.mult, ALU.max))
    link(v.reciprocal(rc, sc))
    link(v.tensor_tensor(blk(a), blk(src), wide(rc), ALU.mult))
    link(v.scalar_tensor_tensor(out=a, in0=a, scalar=-1.0, in1=a, op0=ALU.mult, op1=ALU.max))
    link(v.tensor_scalar(q, a, 0.25, None, ALU.is_gt))
    for mid in (0.75, 1.25, 1.75):
        link(v.scalar_tensor_tensor(out=q, in0=a, scalar=mid, in1=q, op0=ALU.is_gt, op1=ALU.add))
    link(v.tensor_scalar(q, q, 0.5, None, ALU.mult))
    for mid in (2.5, 3.5, 5.0, 5.0):
        link(v.scalar_tensor_tensor(out=q, in0=a, scalar=mid, in1=q, op0=ALU.is_gt, op1=ALU.add))
    link(v.tensor_scalar(a.bitcast(U32), src.bitcast(U32), 0x80000000, None, ALU.bitwise_and))
    link(v.tensor_tensor(q.bitcast(U32), q.bitcast(U32), a.bitcast(U32), ALU.bitwise_or))
    link(v.tensor_tensor(blk(out), blk(q), wide(sc), ALU.mult))


def transposes(nc, K, name, jobs, loads=(), quants=(), products=None):
    NB = 4
    with Scope(nc, name) as s:
        q = quant_buffers(s, P, max(a.shape[-1] for a in quants)) if quants else None
        ps = s.banks("t", NB)
        ld, order, full = s.sem("loaded"), s.sem("dve_order"), s.sem("bank_full")
        act_done, dve_done, qd = s.sem("act_emptied"), s.sem("dve_emptied"), s.sem("quantised")
        with nc.Block() as block:

            @block.sync
            def _(sp):
                for to, src in loads:
                    sp.dma_start(to, src).then_inc(ld, 16)

            @block.tensor
            def _(pe):
                if loads:
                    pe.wait_ge(ld, 16 * len(loads))
                if quants:
                    pe.wait_ge(qd, 1)
                for n, (to, src) in enumerate(jobs):
                    if n >= NB:
                        pe.wait_ge(dve_done if n % 2 else act_done, (n - NB) // 2 + 1)
                    r, c = src.shape
                    nc.tensor.transpose(ps[n % NB][0:c, 0:r], src, K["ident"][0:r, 0:r]).then_inc(full, 1)

            def empty(eng, copy, par, done):
                for n in range(par, len(jobs), 2):
                    to, src = jobs[n]
                    r, c = src.shape
                    eng.wait_ge(full, n + 1)
                    copy(to, ps[n % NB][0:c, 0:r]).then_inc(done, 1)

            @block.scalar
            def _(act):
                empty(act, nc.scalar.copy, 0, act_done)

            @block.vector
            def _(dve):
                if quants:
                    link = Link(dve, order)
                    dve.wait_ge(ld, 16 * len(loads))
                    for m in quants:
                        fp4_round(nc, link, q, m, m)
                    nc.vector.memset(q["rc"][:, 0:1], 0.0).then_inc(qd, 1)
                empty(dve, nc.vector.tensor_copy, 1, dve_done)


class Ring:

    def __init__(self, jobs, start=None, banks=2):
        self.jobs, self.banks = list(jobs), banks
        self.index = {name: n for n, (name, _) in enumerate(self.jobs)}
        self.total = {e: sum(x == e for _, x in self.jobs) for e in "av"}
        self.start = start or {"a": 0, "v": 0, "full": 0}

    def after(self):
        return {"a": self.start["a"] + self.total["a"], "v": self.start["v"] + self.total["v"],
                "full": self.start["full"] + len(self.jobs)}

    def bank(self, name):
        return self.index[name] % self.banks

    def engine(self, name):
        return self.jobs[self.index[name]][1]

    def full(self, step, name):
        return step * len(self.jobs) + (self.start["full"] + self.index[name] + 1)

    def emptied(self, step, name, engine):
        n = sum(e == engine for _, e in self.jobs[:self.index[name] + 1])
        return step * self.total[engine] + (self.start[engine] + n)

    def before(self, step, engine):
        return step * (len(self.jobs) if engine == "full" else self.total[engine]) + self.start[engine]


def attention(nc, K, kind, W, ins, ctxT_dram):
    H = 1 if kind == 3 else NH
    G = max(H // 4, 1)
    GW = min(H, 4)
    keys = S2 + T if kind == 0 else S2
    NCH = NC_CTX + (kind == 0)
    widths = [386] * 4 if kind == 0 else [482, 482, 480]
    U = len(widths)
    at = [sum(widths[:u]) for u in range(U)]
    SPLIT = kind in (1, 2)
    SB, NR = 3, 3
    NP = 2 if kind == 3 else 4
    job_chunks = [list(range(4 * k, 4 * k + 4)) for k in range(3)]
    if kind == 0:
        job_chunks[2].append(NC_CTX)
    X = K["X"]
    gate = K["gate"][0:T, kind:kind + 1]

    if kind == 0:
        part_a = [("C0", "a"), ("C1", "a"), ("C2", "a")]
        part_b = [("X0", "v"), ("X1", "a"), ("X2", "v"), ("Q0", "a"), ("Q1", "v"), ("Q2", "a"), ("Q3", "v")]
    else:
        part_a = [("K0", "a"), ("K1", "a"), ("K2", "a")]
        part_b = [("V0", "v"), ("V1", "v"), ("V2", "v")]
        if kind == 1:
            part_b = [("V0", "v"), ("G0", "a"), ("V1", "v"), ("G1", "a"), ("V2", "v"), ("G2", "a")]

    ROWS, NSPLIT = 9 * (D // NH), 4 * U

    def t_jobs(n):
        if kind == 1:
            return [((n, k), "vva"[k]) for k in range(3)]
        return [((n, k), "v" if (3 * n + k) % 2 else "a") for k in range(3)]

    LAG = 2 if H > 1 else 1
    steps = range(LAG, H + LAG)
    plan = {s: [] for s in steps}
    if kind == 0:
        for x, s in zip(part_a, (4, 5, 7)):
            plan[s].append(x)
        for x, s in zip(part_b, (13, 14, 15, 8, 9, 11, 12)):
            plan[s].append(x)
    elif kind == 3:
        plan[LAG] = part_a + part_b
    else:
        for k, x in enumerate(part_a):
            plan[3 + k].append(x)
        for k, x in enumerate(part_b):
            plan[6 + k].append(x)

    def group_at(s):
        if s == H + LAG - 1:
            return G - 1
        return s // 4 - 1 if s % 4 == 2 and s > 2 else None

    body = list(part_a + part_b) if kind == 3 else []
    for s in steps:
        body += t_jobs(s - LAG)
        if (kind == 0 or group_at(s) == G - 1) and group_at(s) is not None:
            body.append((f"R{group_at(s)}", "a"))
        if kind != 3:
            body += plan[s]
    first = Ring(part_a + part_b, banks=NR)
    ring = Ring(body, first.after(), banks=NR)

    with Scope(nc, f"attn{kind}") as s_:
        sb, sem = s_.sb, s_.sem
        if SPLIT:
            kT = [sb("k", [P, S2])] * 2
            kp = sb("kparts", [P, 3, S2], BF16)
            stack = [sb(f"stack{i}", [ROWS, 4, S2], BF16) for i in range(2)]
            Qs = [sb(f"Q{i}", [ROWS, H, T], BF16) for i in range(2)]
        else:
            kT = [sb(f"kT{i}", [P, keys]) for i in range(2)]
            Qs = [sb(f"Q{i}", [P, H, T]) for i in range(2)]
        V = [sb(f"V{i}", [KC, NCH, D]) for i in range(2)]
        bias = [sb(f"bias{i}", [T, keys]) for i in range(2)]
        prob = sb("prob", [T, NP, keys])
        pT = sb("pT", [KC, 2, NCH, GW, T])
        mpart, nmax = sb("mpart", [T, 2, H, U]), sb("nmax", [T, 2, H])
        RW = 32 if kind in (1, 2) else 1
        den, rden = sb("den", [T, 2, H]), sb("rden", [T, 2, H * RW])
        R = sb("R", [P, GW * T])
        Y = [sb(f"Y{i}", [P, GW * T]) for i in range(2)]
        upd = sb("upd", [T, D])
        if kind == 0:
            cn = sb("ctx", [KC, NC_CTX, D])
            stage = sb("ctxT", [P, S2])
            keep = sb("keep", [T, S2], U8)
            st, mv, rs = sb("st", [KC, NC_CTX, 6]), sb("mv", [KC, NC_CTX, 2]), sb("rs", [KC, NC_CTX])
        else:
            ctxT = sb("ctxT", [P, S2])
        if kind == 1:
            mask = sb("mask", [T, S2], I32)
            Gp = sb("group", [T, S2])
            GT = [sb(f"GT{i}", [KC, NC_CTX, T]) for i in range(2)]
        if kind == 2:
            pad = sb("pad", [T, S2], U8)
            attn = sb("attn", [T, S2])
        s_ps, r_ps = s_.banks("score", SB), s_.banks("ring", NR)
        o_ps, out_ps = s_.banks("av", 1)[0], s_.banks("out", 1)[0]

        ready = sem("ready")
        ld_ctx, ld_mask, ld_g = sem("ctx_loaded"), sem("mask_loaded"), sem("group_loaded")
        ld_const, stored = sem("const_loaded"), sem("ctxT_stored")
        bias_ready = sem("bias_ready")
        side_ready = sem("pool_ready")
        score_full = sem("score_full")
        score_used = sem("score_used")
        max_ready = sem("max_ready")
        prob_ready = sem("prob_ready")
        rden_ready = sem("rden_ready")
        ring_full, act_out, dve_out = sem("ring_full"), sem("act_emptied"), sem("dve_emptied")
        av_full = sem("av_full")
        y_ready = sem("y_ready")
        folded = sem("y_used")
        upd_ready, x_done = sem("update_ready"), sem("x_done")
        ln, var_ready, rstd_ready, rs_order, xn_ready = (sem("ln"), sem("var_ready"), sem("rstd_ready"),
                                                         sem("rs_order"), sem("xn_ready"))
        out_of = {"a": act_out, "v": dve_out}
        NSIDE = 2 if kind == 0 else 1
        k_split, kp_stored = sem("k_split"), sem("kparts_stored")
        q_loaded = sem("q_loaded")
        weighted = sem("weighted")
        rden_order = sem("rden_order")
        stack_loaded = [sem(f"stack{i}_loaded") for i in range(2)]

        with nc.Block() as block:

            @block.sync
            def _(sp):
                if kind == 2:
                    sp.dma_start(attn[:], ins["fside_SxS2_0"]).then_inc(ld_const, 16)

                def load(step, b):
                    if kind == 0:
                        n = (NC_CTX - 1) * KC
                        sp.dma_start(cn[:, 0:NC_CTX - 1, :],
                                     ins["ctx_1024"][b, 0:n, :].rearrange("(c p) d -> p c d", p=KC)).then_inc(ld_ctx, 16)
                        sp.dma_start(cn[0:LAST, NC_CTX - 1, :], ins["ctx_1024"][b, n:S2, :]).then_inc(ld_ctx, 16)
                        sp.dma_start(keep[:], bcast_rows(ins["mask_BxS2_bk0"][b, :], T, S2)).then_inc(ld_mask, 16)
                    else:
                        sp.dma_start(ctxT[:], ctxT_dram[b]).then_inc(ld_ctx, 16)
                    if kind == 1:
                        sp.dma_start(mask[:], ins["mask_BxSxS2_ik1"][b]).then_inc(ld_mask, 16)
                        sp.dma_start(Gp[:], ins["fside_BxSxS2_0"][b]).then_inc(ld_g, 16)
                    if kind == 2:
                        sp.dma_start(pad[:], bcast_rows(ins["mask_BxS2_bf0"][b, :], T, S2)).then_inc(ld_mask, 16)

                def store(rg, step, b):
                    wait_apart(sp, ready, act_out, rg.emptied(step, "C2", "a"))
                    sp.dma_start(ctxT_dram[b], stage[:]).then_inc(stored, 16)

                def used(rg, step, load_no):
                    last = max((x for x, _ in part_a + part_b if x[0] != "Q"), key=lambda x: rg.index[x])
                    wait_apart(sp, ready, ring_full, rg.full(step, last))
                    if kind == 0:
                        wait_apart(sp, ready, ln, load_no * 25 + 24)
                    if kind != 3:
                        wait_apart(sp, ready, bias_ready, load_no + 1)

                def load_q(b, nxt):
                    sp.dma_start(Qs[nxt][:].rearrange("r h t -> r (h t)"), W["q_dram"][b]).then_inc(q_loaded, 16)

                def store_parts(load_no, nxt):
                    wait_apart(sp, ready, k_split, (load_no + 1) * NSPLIT)
                    sp.dma_start(W["k_dram"][nxt].rearrange("a p s -> p a s"), kp[:]).then_inc(kp_stored, 16)

                def load_group(load_no, nxt, j):
                    wait_apart(sp, ready, kp_stored, (load_no + 1) * 16)
                    src = W["k_dram"][nxt].rearrange("a (d j n) s -> j (a d) (n s)", d=8, j=4)[j]
                    for a in range(3):
                        sp.dma_start(stack[j % 2][24 * a:24 * a + 24].rearrange("r n s -> r (n s)"),
                                     src).then_inc(stack_loaded[j % 2], 16)

                sp.wait_ge(ready, 1)
                load(0, 0)
                if kind == 0:
                    store(first, 0, 0)
                if SPLIT:
                    load_q(0, 0)
                    store_parts(0, 0)
                    load_group(0, 0, 0)
                    load_group(0, 0, 1)
                used(first, 0, 0)
                load(1, 1)
                with sp.Fori(0, B // 2) as i:
                    for par in range(2):
                        n = i * 2 + par
                        b1, b2 = sp.snap((n + 1) % B), sp.snap((n + 2) % B)
                        if kind == 0:
                            store(ring, n, b1)
                        if SPLIT:
                            wait_apart(sp, ready, score_full, n * (H * U) + 1)
                            load_q(b1, 1 - par)
                            wait_apart(sp, ready, score_full, n * (H * U) + 4 * U)
                            load_group(n, par, 2)
                            wait_apart(sp, ready, score_full, n * (H * U) + 8 * U)
                            load_group(n, par, 3)
                            store_parts(n + 1, 1 - par)
                        used(ring, n, n + 1)
                        load(n + 2, b2)
                        if SPLIT:
                            wait_apart(sp, ready, score_full, n * (H * U) + 12 * U)
                            load_group(n + 1, 1 - par, 0)
                            wait_apart(sp, ready, score_full, n * (H * U) + 16 * U)
                            load_group(n + 1, 1 - par, 1)
                if kind == 0:
                    sp.wait_ge(stored, 16 * (B + 1))
                if SPLIT:
                    sp.wait_ge(q_loaded, (B + 1) * 16)
                    for x in stack_loaded:
                        sp.wait_ge(x, (2 * B + 1) * 48)
                sp.wait_ge(ld_ctx, (B + 2) * (32 if kind == 0 else 16))
                if kind != 3:
                    sp.wait_ge(ld_mask, (B + 2) * 16)
                if kind == 1:
                    sp.wait_ge(ld_g, (B + 2) * 16)

            @block.gpsimd
            def _(pool):
                def side(step, b, nxt):
                    if kind == 0:
                        wait_apart(pool, ready, var_ready, (step + 1) * NC_CTX)
                        nc.gpsimd.tensor_scalar(rs[:], mv[:, :, 1], EPS, None, ALU.add).then_inc(rs_order, 1)
                        pool.wait_ge(rs_order, step + 1)
                        nc.gpsimd.tensor_tensor(rs[:], rs[:], K["mhalf"][0:KC, 0:NC_CTX], ALU.pow).then_inc(rstd_ready, 1)
                        nc.gpsimd.tensor_copy(V[nxt][0:T, NC_CTX, :], W["lat"][:, b, :]).then_inc(side_ready, 1)
                        nc.gpsimd.tensor_copy(kT[nxt][:, S2:keys], W["latT"][:, bass.ds(b * T, T)]).then_inc(side_ready, 1)
                    elif kind == 3:
                        nc.gpsimd.tensor_copy(Qs[nxt][:, 0, :], W["q"][:, bass.ds(b * T, T)]).then_inc(side_ready, 1)

                def split_keys(rg, step, load_no, first_op, last_op):
                    g = nc.gpsimd
                    for done in range(first_op, last_op):
                        u, op = done // 4, done % 4
                        if done == 0 and not isinstance(load_no, int):
                            wait_apart(pool, ready, kp_stored, load_no * 16)
                        if op == 0:
                            wait_apart(pool, ready, act_out, rg.emptied(step, f"K{u}", "a"))
                        if done:
                            wait_apart(pool, ready, k_split, load_no * NSPLIT + done)
                        x = kT[0][:, at[u]:at[u] + widths[u]]
                        parts = [kp[:, m, at[u]:at[u] + widths[u]] for m in range(3)]
                        if op % 2 == 0:
                            i_ = g.tensor_copy(parts[op // 2], x)
                        else:
                            i_ = g.tensor_tensor(x if op == 1 else parts[2], x, parts[op // 2], ALU.subtract)
                        i_.then_inc(k_split, 1)

                def weight(step, par, h):
                    pool.wait_ge(act_out, ring.emptied(step, (h, 2), "a"))
                    ch = job_chunks[2]
                    x = pT[:, (h // 4) % 2, ch[0]:ch[0] + len(ch), h % 4, :]
                    nc.gpsimd.tensor_tensor(x, x, GT[par][:, ch[0]:ch[0] + len(ch), :], ALU.mult).then_inc(weighted, 1)

                pool.wait_ge(ready, 1)
                if SPLIT:
                    split_keys(first, 0, 0, 0, NSPLIT)
                else:
                    side(0, 0, 0)
                with pool.Fori(0, B // 2) as i:
                    for par in range(2):
                        n = i * 2 + par
                        if SPLIT:
                            for s in steps:
                                if kind == 1:
                                    weight(n, par, s - LAG)
                                if 5 <= s < 5 + NSPLIT // 2:
                                    split_keys(ring, n, n + 1, 2 * (s - 5), 2 * (s - 5) + 2)
                        else:
                            b = pool.snap((n + 1) % B)
                            wait_apart(pool, ready, score_full, n * (H * U) + ((LAG * U if kind == 0 else 0) + 1))
                            side(n + 1, b, 1 - par)

            @block.tensor
            def _(pe):
                ident = K["ident"]

                def job(rg, step, name):
                    n = rg.index[name]
                    if n >= NR:
                        prev, e = rg.jobs[n - NR]
                        pe.wait_ge(out_of[e], rg.emptied(step, prev, e))
                    return r_ps[n % NR]

                def scores(step, par, h, u):
                    m = h * U + u
                    if m >= SB or not isinstance(step, int):
                        pe.wait_ge(score_used, step * (H * U) + (m - SB + 1))
                    if SPLIT:
                        j = h // 4
                        if h % 4 == 0 and u == 0:
                            pe.wait_ge(stack_loaded[j % 2], step * 96 + (j // 2 + 1) * 48)
                        k = stack[j % 2][:, h % 4, at[u]:at[u] + widths[u]]
                    else:
                        k = kT[par][:, at[u]:at[u] + widths[u]]
                    i_ = nc.tensor.matmul(s_ps[m % SB][0:T, 0:widths[u]], Qs[par][:, h, :], k, start=True, stop=True)
                    i_.then_inc(score_full, 1)

                def turn(step, par, h, k):
                    if k == 0:
                        pe.wait_ge(prob_ready, step * H + (h + 1))
                    slot = (h + par * H) % NP
                    ps = job(ring, step, (h, k))
                    for x, c in enumerate(job_chunks[k]):
                        kc, c0 = chunk_rows(c), chunk_at(c)
                        i_ = nc.tensor.transpose(ps[0:kc, x * T:(x + 1) * T], prob[:, slot, c0:c0 + kc],
                                                 ident[0:T, 0:T])
                    i_.then_inc(ring_full, 1)

                def spread(step, par, j):
                    name = f"R{j}"
                    ps = job(ring, step, name)
                    pe.wait_ge(rden_ready, step * (G if kind == 0 else 1) + ((j if kind == 0 else 0) + 1))
                    for x in range(GW):
                        if kind in (0, 3):
                            r = rden[:, par, 4 * j + x:4 * j + x + 1].broadcast_to([T, P])
                        else:
                            r = rden[:, par, P * x:P * x + P]
                        i_ = nc.tensor.transpose(ps[:, x * T:(x + 1) * T], r, ident[0:T, 0:T])
                    i_.then_inc(ring_full, 1)

                def values(step, par, j):
                    last = GW * (j + 1) - 1
                    for e in "av":
                        if any(x == e for _, x in t_jobs(last)):
                            pe.wait_ge(out_of[e], ring.emptied(step, (last, 2), e))
                    if kind == 1:
                        pe.wait_ge(weighted, step * H + 4 * (j + 1))
                    if kind == 0 and j:
                        pe.wait_ge(y_ready, step * G + j)
                    slot = par if kind == 3 else j % 2
                    for c in range(NCH):
                        kc = chunk_rows(c)
                        flags = {"start": c == 0, "stop": c == NCH - 1}
                        if kind in (0, 3):
                            i_ = nc.tensor.matmul(o_ps[:, 0:GW * T], V[par][0:kc, c, :],
                                                  pT[0:kc, slot, c, :, :].rearrange("p g t -> p (g t)"), **flags)
                        else:
                            for g in range(4):
                                i_ = nc.tensor.matmul(o_ps[32 * g:32 * g + 32, j * T:(j + 1) * T],
                                                      V[par][0:kc, c, 32 * g:32 * g + 32],
                                                      pT[0:kc, slot, c, g, :], **flags)
                    i_.then_inc(av_full, 1)

                def output(step, j):
                    pe.wait_ge(y_ready, step * (G if kind == 0 else 1) + ((j if kind == 0 else 0) + 1))
                    for x in range(GW):
                        if kind == 0:
                            n, w, y = 4 * j + x, W["vo"][:, 4 * x + j, :], Y[j % 2]
                        else:
                            n, w, y = x, W["o"][:, x, :], Y[0]
                        i_ = nc.tensor.matmul(out_ps[0:T, 0:D], y[:, x * T:(x + 1) * T], w, start=(n == 0),
                                              stop=(n == (H if kind == 0 else GW) - 1))
                    i_.then_inc(folded, 1)

                def project(rg, step, load_no, nxt, b, name):
                    what, k = name[0], int(name[1])
                    chunks = range(4 * k, 4 * k + 4)
                    if name == "C0" or name == "K0":
                        pe.wait_ge(ld_ctx, (load_no + 1) * (32 if kind == 0 else 16))
                    if name == "X0":
                        pe.wait_ge(xn_ready, load_no + 1)
                    if name == "G0":
                        pe.wait_ge(ld_g, (load_no + 1) * 16)
                    ps = job(rg, step, name)
                    if what in "CX":
                        for x, c in enumerate(chunks):
                            kc = chunk_rows(c)
                            src = (cn if what == "C" else V[nxt])[0:kc, c, :]
                            i_ = nc.tensor.transpose(ps[:, x * KC:x * KC + kc], src, ident[0:kc, 0:kc])
                    elif what == "Q":
                        for g in range(4):
                            i_ = nc.tensor.matmul(ps[:, g * T:(g + 1) * T], W["qk"][:, 4 * g + k, :],
                                                  W["latT"][:, bass.ds(b * T, T)], start=True, stop=True)
                    elif what == "K":
                        i_ = nc.tensor.matmul(ps[:, 0:widths[k]], W["k"][:], ctxT[:, at[k]:at[k] + widths[k]],
                                              start=True, stop=True)
                    else:
                        for x, c in enumerate(chunks):
                            kc, c0 = chunk_rows(c), chunk_at(c)
                            if what == "V":
                                i_ = nc.tensor.matmul(ps[0:kc, x * D:(x + 1) * D], ctxT[:, c0:c0 + kc], W["v"][:],
                                                      start=True, stop=True)
                            else:
                                i_ = nc.tensor.transpose(ps[0:kc, x * T:(x + 1) * T], Gp[:, c0:c0 + kc],
                                                         ident[0:T, 0:T])
                    i_.then_inc(ring_full, 1)

                def operands(rg, step, load_no):
                    for e in "av":
                        names = [x for x, who in part_a + part_b if who == e]
                        last = max(names, key=lambda x: rg.index[x])
                        pe.wait_ge(out_of[e], rg.emptied(step, last, e))
                    if SPLIT:
                        pe.wait_ge(q_loaded, (load_no + 1) * 16)
                    else:
                        pe.wait_ge(side_ready, (load_no + 1) * NSIDE)

                pe.wait_ge(ready, 1)
                for name, _ in part_a + part_b:
                    project(first, 0, 0, 0, 0, name)
                operands(first, 0, 0)
                for h in range(LAG):
                    for u in range(U):
                        scores(0, 0, h, u)
                with pe.Fori(0, B // 2) as i:
                    for par in range(2):
                        n = i * 2 + par
                        b = pe.snap((n + 1) % B)
                        if kind == 3:
                            for name, _ in part_a + part_b:
                                project(ring, n, n + 1, 1 - par, b, name)
                        for s in steps:
                            if s == H:
                                operands(ring, n, n + 1)
                            for u in range(U):
                                scores(n + s // H, par ^ (s // H), s % H, u)
                                if u < 3:
                                    turn(n, par, s - LAG, u)
                            j = group_at(s)
                            if j is not None:
                                if kind == 0 or j == G - 1:
                                    spread(n, par, j)
                                values(n, par, j)
                            if kind != 3:
                                for name, _ in plan[s]:
                                    project(ring, n, n + 1, 1 - par, b, name)
                            if kind == 0 and s in (8, 12):
                                output(n, s // 4 - 2)
                        if kind == 0:
                            output(n, G - 2)
                        output(n, G - 1)

            @block.scalar
            def _(act):
                def out(rg, step, name):
                    act.wait_ge(ring_full, rg.full(step, name))
                    return r_ps[rg.bank(name)]

                def turned(step, par, h):
                    for (name, e) in t_jobs(h):
                        if e != "a":
                            continue
                        ch = job_chunks[name[1]]
                        j, g = h // 4, h % 4
                        slot = par if kind == 3 else j % 2
                        ps = out(ring, step, name)
                        if kind != 3 and j >= 2 and h % 4 < 2:
                            act.wait_ge(av_full, step * G + (j - 1))
                        nc.scalar.copy(pT[:, slot, ch[0]:ch[0] + len(ch), g, :],
                                       ps[0:KC, 0:len(ch) * T].rearrange("p (c t) -> p c t", t=T)).then_inc(act_out, 1)

                def expo(step, par, h):
                    act.wait_ge(max_ready, step * H + (h + 1))
                    p = prob[:, (h + par * H) % NP, :]
                    nc.scalar.activation(p, p, ACT.Exp, bias=nmax[:, par, h:h + 1],
                                         accum_out=den[:, par, h:h + 1]).then_inc(prob_ready, 1)

                def spread(step, j):
                    ps = out(ring, step, f"R{j}")
                    if kind == 0 and j:
                        act.wait_ge(y_ready, step * G + j)
                    nc.scalar.copy(R[:], ps[:, 0:GW * T]).then_inc(act_out, 1)

                def projected(rg, step, load_no, nxt, part):
                    for name, e in part:
                        if e != "a":
                            continue
                        k = int(name[1])
                        ps = out(rg, step, name)
                        if name[0] == "C":
                            if k == 0 and rg is ring:
                                act.wait_ge(stored, load_no * 16)
                            w = min(4 * KC, S2 - 4 * k * KC)
                            i_ = nc.scalar.copy(stage[:, 4 * k * KC:4 * k * KC + w], ps[:, 0:w])
                        elif name[0] == "X":
                            w = min(4 * KC, S2 - 4 * k * KC)
                            i_ = nc.scalar.copy(kT[nxt][:, 4 * k * KC:4 * k * KC + w], ps[:, 0:w])
                        elif name[0] == "Q":
                            i_ = nc.scalar.copy(Qs[nxt][:, 4 * k:4 * k + 4, :],
                                                ps[:, 0:4 * T].rearrange("p (g t) -> p g t", t=T))
                        elif name[0] == "K":
                            if SPLIT and rg is ring:
                                act.wait_ge(k_split, load_no * NSPLIT)
                            i_ = nc.scalar.activation(kT[nxt][:, at[k]:at[k] + widths[k]], ps[:, 0:widths[k]],
                                                      ACT.Identity, bias=W["bk"][:, 0:1])
                        else:
                            if k == 0 and rg is ring:
                                act.wait_ge(weighted, step * H + 4)
                            i_ = nc.scalar.copy(GT[nxt][:, 4 * k:4 * k + 4, :],
                                                ps[0:KC, 0:4 * T].rearrange("p (c t) -> p c t", t=T))
                        i_.then_inc(act_out, 1)

                act.wait_ge(ready, 1)
                projected(first, 0, 0, 0, part_a + part_b)
                for h in range(LAG):
                    expo(0, 0, h)
                with act.Fori(0, B // 2) as i:
                    for par in range(2):
                        n = i * 2 + par
                        if kind == 3:
                            projected(ring, n, n + 1, 1 - par, part_a + part_b)
                        for s in steps:
                            turned(n, par, s - LAG)
                            j = group_at(s)
                            if j is not None and (kind == 0 or j == G - 1):
                                spread(n, j)
                            if kind != 3:
                                projected(ring, n, n + 1, 1 - par, plan[s])
                            expo(n + s // H, par ^ (s // H), s % H)

            @block.vector
            def _(dve):
                v = nc.vector


                def masked(step, par, h, between, last=None):
                    if h == 0 and kind != 3:
                        dve.wait_ge(bias_ready, step + 1)
                    if last is not None:
                        dve.wait_ge(ring_full, ring.full(*last))
                    slot = (h + par * H) % NP
                    for u in range(U):
                        m = h * U + u
                        wait_apart(dve, ready, score_full, step * (H * U) + (m + 1))
                        i_ = v.tensor_tensor_reduce(prob[:, slot, at[u]:at[u] + widths[u]], s_ps[m % SB][0:T, 0:widths[u]],
                                                    bias[par][:, at[u]:at[u] + widths[u]], 1.0, -FLT_MAX,
                                                    ALU.add, ALU.max, mpart[:, par, h, u:u + 1])
                        i_.then_inc(score_used, 1)
                        between(u)
                    dve.wait_ge(score_used, step * (H * U) + (h + 1) * U)
                    v.tensor_reduce(nmax[:, par, h:h + 1], mpart[:, par, h, :], AX.X, ALU.max,
                                    negate=True).then_inc(max_ready, 1)

                def out(rg, step, name):
                    dve.wait_ge(ring_full, rg.full(step, name))
                    return r_ps[rg.bank(name)]

                def turned(step, par, h, only=(0, 1, 2)):
                    for (name, e) in t_jobs(h):
                        if e != "v" or name[1] not in only:
                            continue
                        ch = job_chunks[name[1]]
                        j, g = h // 4, h % 4
                        slot = par if kind == 3 else j % 2
                        ps = out(ring, step, name)
                        if kind != 3 and j >= 2 and h % 4 < 2:
                            dve.wait_ge(av_full, step * G + (j - 1))
                        to = pT[:, slot, ch[0]:ch[0] + len(ch), g, :]
                        src = ps[0:KC, 0:len(ch) * T].rearrange("p (c t) -> p c t", t=T)
                        if kind == 1:
                            if h == 0 and name[1] == 0:
                                dve.wait_ge(act_out, ring.before(step, "a"))
                            i_ = v.tensor_tensor(to, src, GT[par][:, ch[0]:ch[0] + len(ch), :], ALU.mult)
                        else:
                            i_ = v.tensor_copy(to, src)
                        i_.then_inc(dve_out, 1)

                def recip(step, par, j):
                    n = 4 * (j + 1) if kind == 0 else H
                    dve.wait_ge(prob_ready, step * H + n)
                    lo = n - 4 if kind == 0 else 0
                    if RW == 1:
                        v.reciprocal(rden[:, par, lo:n], den[:, par, lo:n]).then_inc(rden_ready, 1)
                    else:
                        v.reciprocal(den[:, par, lo:n], den[:, par, lo:n]).then_inc(rden_order, 1)
                        dve.wait_ge(rden_order, step + 1)
                        v.tensor_copy(rden[:, par, :].rearrange("t (h r) -> t h r", r=RW),
                                      den[:, par, :].rearrange("t (h r) -> t h r", r=1).broadcast_to([T, H, RW])
                                      ).then_inc(rden_ready, 1)

                def divide(step, j):
                    dve.wait_ge(act_out, ring.emptied(step, f"R{j}", "a"))
                    dve.wait_ge(av_full, step * G + (j + 1))
                    if kind == 0 and j >= 2:
                        dve.wait_ge(folded, step * G + (j - 1))
                    v.tensor_tensor(Y[j % 2 if kind == 0 else 0][:], o_ps[:, 0:GW * T], R[:], ALU.mult).then_inc(y_ready, 1)

                def projected(rg, step, load_no, nxt, part):
                    for name, e in part:
                        if e != "v":
                            continue
                        k = int(name[1])
                        ps = out(rg, step, name)
                        if name[0] == "X":
                            w = min(4 * KC, S2 - 4 * k * KC)
                            i_ = v.tensor_copy(kT[nxt][:, 4 * k * KC:4 * k * KC + w], ps[:, 0:w])
                        elif name[0] == "Q":
                            i_ = v.tensor_copy(Qs[nxt][:, 4 * k:4 * k + 4, :],
                                               ps[:, 0:4 * T].rearrange("p (g t) -> p g t", t=T))
                        elif name[0] == "K":
                            if SPLIT and rg is ring:
                                dve.wait_ge(k_split, load_no * NSPLIT)
                            i_ = v.tensor_scalar(kT[nxt][:, at[k]:at[k] + widths[k]], ps[:, 0:widths[k]],
                                                 W["bk"][:, 0:1], None, ALU.add)
                        else:
                            bv = W["bv"][0:KC, :].rearrange("p (a d) -> p a d", a=1).broadcast_to([KC, 4, D])
                            i_ = v.tensor_tensor(V[nxt][:, 4 * k:4 * k + 4, :],
                                                 ps[0:KC, 0:4 * D].rearrange("p (c d) -> p c d", d=D), bv, ALU.add)
                        i_.then_inc(dve_out, 1)

                def build_bias(load_no, nxt):
                    if kind == 3:
                        return
                    dve.wait_ge(ld_mask, (load_no + 1) * 16)
                    b = bias[nxt][:, 0:S2]
                    if kind == 0:
                        i_ = v.tensor_scalar(b, keep[:], FLT_MAX, -FLT_MAX, ALU.mult, ALU.add)
                    elif kind == 1:
                        i_ = v.tensor_scalar(b, mask[:], NEG_MASK, -NEG_MASK, ALU.mult, ALU.add)
                    else:
                        i_ = v.scalar_tensor_tensor(out=b, in0=pad[:], scalar=-FLT_MAX, in1=attn[:],
                                                    op0=ALU.mult, op1=ALU.add)
                    i_.then_inc(bias_ready, 1)

                def ln_stats(load_no, c):
                    if c == 0:
                        dve.wait_ge(ld_ctx, (load_no + 1) * 32)
                    v.bn_stats(st[:, c, :], cn[:, c, :]).then_inc(ln, 1)

                def ln_var(load_no, c):
                    wait_apart(dve, ready, ln, load_no * 25 + (c + 1))
                    v.bn_aggr(mv[:, c, :], st[:, c, :]).then_inc(var_ready, 1)

                def ln_apply(load_no, nxt, c):
                    if c == 0:
                        dve.wait_ge(rstd_ready, load_no + 1)
                    v.tensor_scalar(V[nxt][:, c, :], cn[:, c, :], mv[:, c, 0:1], rs[:, c:c + 1],
                                    ALU.subtract, ALU.mult).then_inc(ln, 1)

                def ln_affine(load_no, nxt):
                    x = V[nxt][:, 0:NC_CTX, :]
                    g1, b1 = (W[k][0:KC, :].rearrange("p (a d) -> p a d", a=1).broadcast_to([KC, NC_CTX, D])
                              for k in ("g1", "b1"))
                    dve.wait_ge(ln, load_no * 25 + 24)
                    v.tensor_tensor(x, x, g1, ALU.mult).then_inc(ln, 1)
                    dve.wait_ge(ln, load_no * 25 + 25)
                    v.tensor_tensor(x, x, b1, ALU.add).then_inc(xn_ready, 1)

                for n, t in enumerate(r_ps):
                    v.memset(t[:], 0.0).then_inc(x_done, 1)
                extra = 2
                if kind == 0:
                    v.memset(cn[96:KC, NC_CTX - 1, :], 0.0).then_inc(x_done, 1)
                    for t in bias:
                        v.memset(t[:, S2:keys], 0.0).then_inc(x_done, 1)
                    extra += 3
                if kind == 3:
                    for t in bias:
                        v.memset(t[:], 0.0).then_inc(x_done, 1)
                    extra += 2
                dve.wait_ge(x_done, extra)
                if kind == 2:
                    dve.wait_ge(ld_const, 16)
                v.memset(upd[:], 0.0).then_inc(ready, 1)

                if kind == 0:
                    for c in range(NC_CTX):
                        ln_stats(0, c)
                    for c in range(NC_CTX):
                        ln_var(0, c)
                    for c in range(NC_CTX):
                        ln_apply(0, 0, c)
                    ln_affine(0, 0)
                build_bias(0, 0)
                projected(first, 0, 0, 0, part_a + part_b)
                for h in range(LAG):
                    masked(0, 0, h, lambda u: None)
                with dve.Fori(0, B // 2) as i:
                    for par in range(2):
                        n = i * 2 + par
                        if kind == 3:
                            projected(ring, n, n + 1, 1 - par, part_a + part_b)
                        for s in steps:
                            last = (n, (s - NP, 2)) if s >= NP and H > 1 else None
                            masked(n + s // H, par ^ (s // H), s % H, lambda u: turned(n, par, s - LAG, (u,)), last)
                            if kind == 0:
                                if s % 4 == 0:
                                    recip(n, par, s // 4 - 1)
                                if s % 4 == 3 and s > 3:
                                    divide(n, s // 4 - 1)
                                if 2 <= s <= 5:
                                    for c in range(3 * (s - 2), 3 * (s - 1)):
                                        ln_stats(n + 1, c)
                                if 6 <= s <= 7:
                                    for c in range(6 * (s - 6), 6 * (s - 5)):
                                        ln_var(n + 1, c)
                                if 9 <= s <= 10:
                                    for c in range(6 * (s - 9), 6 * (s - 8)):
                                        ln_apply(n + 1, 1 - par, c)
                                if s == 11:
                                    ln_affine(n + 1, 1 - par)
                            if s == 7:
                                build_bias(n + 1, 1 - par)
                            if s == H and kind in (1, 2):
                                recip(n, par, G - 1)
                            if kind != 3:
                                projected(ring, n, n + 1, 1 - par, plan[s])
                        if kind == 3:
                            recip(n, par, 0)
                        divide(n, G - 1)
                        dve.wait_ge(folded, (n + 1) * (G if kind == 0 else 1))
                        if kind == 0:
                            src = out_ps[0:T, 0:D]
                        else:
                            v.tensor_tensor(upd[:], out_ps[0:T, 0:D], W["bo"][0:T, :], ALU.add).then_inc(upd_ready, 1)
                            dve.wait_ge(upd_ready, n + 1)
                            src = upd[:]
                        v.scalar_tensor_tensor(out=X[:, n, :], in0=src, scalar=gate, in1=X[:, n, :],
                                               op0=ALU.mult, op1=ALU.add).then_inc(x_done, 1)


def queries(nc, K, name, w, bias_col, scale, XT, q, q_dram=None):
    with Scope(nc, name) as s:
        ps = s.banks("q", 2)
        parts = [s.sb(f"part{m}", [P, B * T], BF16) for m in range(3)] if q_dram is not None else []
        full, done, stored = s.sem("full"), s.sem("done"), s.sem("stored")
        with nc.Block() as block:

            @block.tensor
            def _(pe):
                for n in range(2):
                    nc.tensor.matmul(ps[n][:, 0:4 * T], w, XT[:, n * 4 * T:(n + 1) * 4 * T], start=True,
                                     stop=True).then_inc(full, 1)

            @block.vector
            def _(dve):
                for n in range(2):
                    dve.wait_ge(full, n + 1)
                    nc.vector.tensor_scalar(q[:, n * 4 * T:(n + 1) * 4 * T], ps[n][:, 0:4 * T], bias_col, scale,
                                            ALU.add, ALU.mult).then_inc(done, 1)
                if parts:
                    dve.wait_ge(done, 2)
                    link = Link(dve, done, 2)
                    link(nc.vector.tensor_copy(parts[0][:], q[:]))
                    link(nc.vector.tensor_tensor(q[:], q[:], parts[0][:], ALU.subtract))
                    link(nc.vector.tensor_copy(parts[1][:], q[:]))
                    link(nc.vector.tensor_tensor(parts[2][:], q[:], parts[1][:], ALU.subtract))

            @block.sync
            def _(sp):
                for a in range(3 if parts else 0):
                    sp.wait_ge(done, (3, 5, 6)[a])
                    for c in range(3):
                        to = q_dram[:, 24 * a + 8 * c:24 * a + 8 * c + 8, :].rearrange("b d (n t) -> (d n) b t", t=T)
                        sp.dma_start(to, parts[a][:].rearrange("p (b t) -> p b t", t=T)).then_inc(stored, 16)
                if parts:
                    sp.wait_ge(stored, 144)


def load(nc, name, loads):
    with Scope(nc, name) as s:
        ld = s.sem("loaded")
        with nc.Block() as block:

            @block.sync
            def _(sp):
                for to, src in loads:
                    sp.dma_start(to, src).then_inc(ld, 16)
                sp.wait_ge(ld, 16 * len(loads))


def col(ap):
    return ap.rearrange("(p a) -> p a", a=1)


def fold_heads(nc, K, W, wqT, wkT, wvT, wout):
    jobs = [(W["qk"], wqT, wkT, 0.125), (W["vo"], wvT, wout, 1.0)]
    with Scope(nc, "fold") as s:
        ps = s.banks("f", 4)
        full, done = s.sem("full"), s.sem("done")
        with nc.Block() as block:

            @block.tensor
            def _(pe):
                n = 0
                for to, left, right, _ in jobs:
                    for h8 in range(0, NH, 8):
                        for odd in range(2):
                            if n >= 4:
                                pe.wait_ge(done, n - 3)
                            if n:
                                pe.wait_ge(full, n)
                            r = slice(64 * odd, 64 * odd + 64)
                            for x in range(4):
                                i_ = nc.tensor.matmul(ps[n % 4][:, x * D:(x + 1) * D], left[r, h8 // 2 + x, :],
                                                      right[r, h8 // 2 + x, :], start=True, stop=True)
                            i_.then_inc(full, 1)
                            n += 1

            @block.vector
            def _(dve):
                n = 0
                for to, _, _, scale in jobs:
                    for h8 in range(0, NH, 8):
                        for odd in range(2):
                            dve.wait_ge(full, n + 1)
                            to2 = to[:].rearrange("p (h o) d -> p h o d", o=2)[:, h8 // 2:h8 // 2 + 4, odd, :]
                            nc.vector.tensor_scalar(to2, ps[n % 4][:].rearrange("p (h d) -> p h d", d=D),
                                                    scale, None, ALU.mult).then_inc(done, 1)
                            n += 1


def head_outputs(nc, K, name, wo, to, by_dim):
    with Scope(nc, name) as s:
        done = s.sem("done")
        with nc.Block() as block:

            @block.vector
            def _(dve):
                for j in range(4):
                    nc.vector.tensor_scalar(to[:, j, :], wo, K["jm"][:, j:j + 1], None, ALU.mult).then_inc(done, 1)
                for a, b, _ in by_dim:
                    for j in range(4):
                        nc.vector.tensor_copy(a.rearrange("p (d j g) -> p j g d", j=4, g=4)[:, j],
                                              b.rearrange("p (g j d) -> p j g d", j=4, g=4)[:, j]).then_inc(done, 1)
                link = Link(dve, done, 4 + 4 * len(by_dim))
                dve.wait_ge(done, link.base)
                for a, _, column in by_dim:
                    if column is not None:
                        link(nc.vector.tensor_tensor(a, a, K["ident"][:], ALU.mult))
                        link(nc.vector.tensor_reduce(column, a, AX.X, ALU.add))


def route(nc, K, kind, XT, wr, gates, gate_bias=None):
    E = wr.shape[-1]
    with Scope(nc, f"route{kind}") as s:
        lg_ps, cnt_ps = s.banks("lg", 1)[0], s.banks("cnt", 1)[0]
        sc, ch, sel = s.sb("scores", [T, B, E]), s.sb("choice", [T, B, E]), s.sb("chosen", [T, B, E])
        top = s.sb("top", [T, B, 8])
        r1 = s.sb("r1", [T, B])
        full, act_done, order, cnt = s.sem("full"), s.sem("act_done"), s.sem("dve_order"), s.sem("counted")
        sel_ready = s.sem("chosen_ready")
        v = nc.vector

        def per_token(ap):
            return ap.rearrange("t (b a) -> t b a", a=1).broadcast_to([T, B, E])

        def rank_below(link, x, lt, n, groups, k, out, cmp, eq):
            a = x.rearrange("t (b g a) -> t b g a", g=n, a=1).broadcast_to([T, groups, n, n])
            b_ = x.rearrange("t (b a j) -> t b a j", a=1, j=n).broadcast_to([T, groups, n, n])
            m = lt.rearrange("t (a g) j -> t a g j", a=1).broadcast_to([T, groups, n, n])
            link(v.tensor_tensor(cmp, b_, a, ALU.is_gt))
            link(v.tensor_tensor(eq, b_, a, ALU.is_equal))
            link(v.tensor_tensor(eq, eq, m, ALU.mult))
            link(v.tensor_tensor(cmp, cmp, eq, ALU.add))
            link(v.tensor_reduce(out, cmp, AX.X, ALU.add))
            link(v.tensor_scalar(out, out, k - 0.5, None, ALU.is_lt))

        if kind == 2:
            top2 = s.sb("top2", [T, B, 4, 8])
            gs, gm = s.sb("group_score", [T, B * 4]), s.sb("group_mask", [T, B * 4])
            cmp, eq = s.sb("cmp", [T, B, 4, 4]), s.sb("eq", [T, B, 4, 4])
            mrep = s.sb("replaced", [T, B, E])
        if kind == 3:
            cmp, eq = s.sb("cmp", [T, B, E, E]), s.sb("eq", [T, B, E, E])
            before = s.sb("before", [T, B, E])
        with nc.Block() as block:

            @block.tensor
            def _(pe):
                for b in range(B):
                    i_ = nc.tensor.matmul(lg_ps[0:T, b * E:(b + 1) * E], XT[:, b * T:(b + 1) * T], wr, start=True,
                                          stop=True)
                i_.then_inc(full, 1)
                if kind == 3:
                    pe.wait_ge(sel_ready, 1)
                    nc.tensor.matmul(cnt_ps[0:T, 0:B * E], K["tri"][:], sel[:].rearrange("t b e -> t (b e)"),
                                     start=True, stop=False)
                    nc.tensor.matmul(cnt_ps[0:T, 0:B * E], K["ones"][:], before[:].rearrange("t b e -> t (b e)"),
                                     start=False, stop=True).then_inc(cnt, 1)

            @block.scalar
            def _(act):
                if kind == 2:
                    act.wait_ge(full, 1)
                    nc.scalar.activation(sc[:].rearrange("t b e -> t (b e)"), lg_ps[0:T, 0:B * E],
                                         ACT.Sigmoid).then_inc(act_done, 1)
                elif kind == 3:
                    act.wait_ge(order, 2)
                    nc.scalar.activation(ch[:], ch[:], ACT.Exp).then_inc(act_done, 1)
                else:
                    act.wait_ge(order, B + 1 + 1)
                    nc.scalar.activation(r1[:], r1[:], ACT.Exp).then_inc(act_done, 1)

            @block.vector
            def _(dve):
                link = Link(dve, order)
                lg = lg_ps[0:T, 0:B * E].rearrange("t (b e) -> t b e", e=E)
                if kind == 0:
                    dve.wait_ge(full, 1)
                    link(v.tensor_copy(sc[:], lg))
                    for b in range(B):
                        link(v.max(top[:, b, :], sc[:, b, :]))
                    link(v.tensor_tensor(r1[:], top[:, :, 1], top[:, :, 0], ALU.subtract))
                    dve.wait_ge(act_done, 1)
                    link(v.tensor_scalar(r1[:], r1[:], 1.0, None, ALU.add))
                    link(v.reciprocal(r1[:], r1[:]))
                    link(v.tensor_scalar(r1[:], r1[:], 1.0, None, ALU.is_ge))
                    link(v.tensor_tensor(sel[:], sc[:], top[:, :, 0:1].broadcast_to([T, B, E]), ALU.is_ge))
                    link(v.tensor_tensor(gates[:], sel[:], per_token(r1[:]), ALU.mult))
                if kind == 2:
                    dve.wait_ge(act_done, 1)
                    gb = gate_bias.rearrange("t (a e) -> t a e", a=1).broadcast_to([T, B, E])
                    link(v.tensor_tensor(ch[:], sc[:], gb, ALU.add))
                    for b in range(B):
                        for g in range(4):
                            i_ = v.max(top2[:, b, g, :], ch[:, b, 8 * g:8 * g + 8])
                            i_.then_inc(order, 1)
                            link.n += 1
                    dve.wait_ge(order, link.n)
                    link(v.tensor_tensor(gs[:].rearrange("t (b g) -> t b g", g=4), top2[:, :, :, 0],
                                         top2[:, :, :, 1], ALU.add))
                    rank_below(link, gs[:], K["lt4"][0:T], 4, B, 2, gm[:].rearrange("t (b g) -> t b g", g=4),
                               cmp[:], eq[:])
                    link(v.tensor_tensor(ch[:].rearrange("t b (g e) -> t (b g) e", e=8),
                                         ch[:].rearrange("t b (g e) -> t (b g) e", e=8),
                                         gm[:].rearrange("t (g a) -> t g a", a=1).broadcast_to([T, B * 4, 8]), ALU.mult))
                    for b in range(B):
                        link(v.max(top[:, b, :], ch[:, b, :]))
                        link(v.match_replace(out=mrep[:, b, :], in_to_replace=top[:, b, :], in_values=ch[:, b, :],
                                             imm_value=-1e30))
                    link(v.tensor_tensor(sel[:], mrep[:], ch[:], ALU.not_equal))
                    link(v.tensor_tensor(sc[:], sc[:], sel[:], ALU.mult))
                    link(v.tensor_reduce(r1[:], sc[:], AX.X, ALU.add))
                    link(v.tensor_scalar(r1[:], r1[:], 1e-20, None, ALU.add))
                    link(v.reciprocal(r1[:], r1[:]))
                    link(v.tensor_scalar(r1[:], r1[:], 2.5, None, ALU.mult))
                    link(v.tensor_tensor(gates[:], sc[:], per_token(r1[:]), ALU.mult))
                if kind == 3:
                    dve.wait_ge(full, 1)
                    link(v.tensor_reduce(r1[:], lg, AX.X, ALU.max))
                    link(v.tensor_tensor(ch[:], lg, per_token(r1[:]), ALU.subtract))
                    dve.wait_ge(act_done, 1)
                    link(v.tensor_reduce(r1[:], ch[:], AX.X, ALU.add))
                    link(v.reciprocal(r1[:], r1[:]))
                    link(v.tensor_tensor(sc[:], ch[:], per_token(r1[:]), ALU.mult))
                    rank_below(link, sc[:].rearrange("t b e -> t (b e)"), K["lt8"][0:T], 8, B, 2, sel[:], cmp[:], eq[:])
                    link(v.memset(before[:, 0, :], 0.0))
                    for b in range(1, B):
                        link(v.tensor_tensor(before[:, b, :], before[:, b - 1, :], sel[:, b - 1, :], ALU.add))
                    v.memset(ch[:], 0.0).then_inc(sel_ready, 1)
                    link(v.tensor_tensor(sc[:], sc[:], sel[:], ALU.mult))
                    dve.wait_ge(cnt, 1)
                    link(v.tensor_scalar(sel[:].rearrange("t b e -> t (b e)"), cnt_ps[0:T, 0:B * E], 511.5, None, ALU.is_lt))
                    link(v.tensor_tensor(gates[:], sc[:], sel[:], ALU.mult))


def ffn(nc, K, kind, XT, units, width, rows, down, gates=None):
    NU, NCK = len(units), len(rows)
    X = K["X"]
    gate = K["gate"][0:T, 4 + kind:5 + kind]
    act_fn = ACT.Relu if kind == 0 else ACT.Silu
    NG = sum(u[4] is not None for u in units)
    groups = [list(range(c, min(c + 4, NCK))) for c in range(0, NCK, 4)]
    ring = Ring([(k, "v" if len(groups) == 1 or k % 2 else "a") for k in range(len(groups))])
    NQ = 17
    with Scope(nc, f"ffn{kind}") as s:
        xT = [s.sb(f"xT{i}", [P, T]) for i in range(2)]
        h = [s.sb(f"h{i}", [T, width]) for i in range(2)]
        hT = s.sb("hT", [P, NCK, T])
        sg = [s.sb(f"act{i}", [T, 512]) for i in range(2)]
        q = quant_buffers(s, T, width) if kind == 1 else None
        a_ps, g_ps = s.banks("a", 2), s.banks("g", 2)
        t_ps, out_ps = s.banks("t", 2), s.banks("o", 1)[0]
        ready = s.sem("ready")
        x_ready = s.sem("x_ready")
        up_full = s.sem("up_full")
        act_ready = s.sem("act_ready")
        h_ready = s.sem("h_ready")
        h_gated = s.sem("h_gated")
        h_round = s.sem("h_rounded")
        ring_full, act_out, dve_out = s.sem("ring_full"), s.sem("act_emptied"), s.sem("dve_emptied")
        out_full, x_done = s.sem("out_full"), s.sem("x_done")
        out_of = {"a": act_out, "v": dve_out}
        with nc.Block() as block:

            @block.tensor
            def _(pe):
                def up(load_no, nxt):
                    pe.wait_ge(x_ready, load_no + 1)
                    for u, (wa, wg, _, n, _) in enumerate(units):
                        if u >= 2:
                            pe.wait_ge(h_ready, load_no * NU + (u - 1))
                        elif not isinstance(load_no, int):
                            pe.wait_ge(h_ready, load_no * NU)
                        i_ = nc.tensor.matmul(a_ps[u % 2][0:T, 0:n], xT[nxt][:], wa, start=True, stop=True)
                        if wg is not None:
                            i_ = nc.tensor.matmul(g_ps[u % 2][0:T, 0:n], xT[nxt][:], wg, start=True, stop=True)
                        i_.then_inc(up_full, 1)

                pe.wait_ge(ready, 1)
                up(0, 0)
                with pe.Fori(0, B // 2) as i:
                    for par in range(2):
                        n = i * 2 + par
                        up(n + 1, 1 - par)
                        pe.wait_ge(h_ready, (n + 1) * NU)
                        if NG:
                            pe.wait_ge(h_gated, (n + 1) * NG)
                        if kind == 1:
                            pe.wait_ge(h_round, (n + 1) * NQ)
                        for k, ch in enumerate(groups):
                            if k >= 2:
                                prev, e = ring.jobs[k - 2]
                                pe.wait_ge(out_of[e], ring.emptied(n, prev, e))
                            for x, c in enumerate(ch):
                                i_ = nc.tensor.transpose(t_ps[k % 2][0:rows[c], x * T:(x + 1) * T],
                                                         h[par][:, sum(rows[:c]):sum(rows[:c + 1])], K["ident"][0:T, 0:T])
                            i_.then_inc(ring_full, 1)
                        for k, ch in enumerate(groups):
                            pe.wait_ge(out_of[ring.engine(k)], ring.emptied(n, k, ring.engine(k)))
                            if k == 0:
                                pe.wait_ge(x_done, n + len(t_ps))
                            for c in ch:
                                i_ = nc.tensor.matmul(out_ps[0:T, 0:D], hT[0:rows[c], c, :], down[0:rows[c], c, :],
                                                      start=(c == 0), stop=(c == NCK - 1))
                        i_.then_inc(out_full, 1)

            def empty(eng, copy, n, e, done):
                for k, ch in enumerate(groups):
                    if ring.engine(k) == e:
                        eng.wait_ge(ring_full, ring.full(n, k))
                        copy(hT[:, ch[0]:ch[0] + len(ch), :],
                             t_ps[k % 2][:, 0:len(ch) * T].rearrange("p (c t) -> p c t", t=T)).then_inc(done, 1)

            @block.scalar
            def _(act):
                def first_half(load_no, b, nxt):
                    nc.scalar.copy(xT[nxt][:], XT[:, bass.ds(b * T, T)]).then_inc(x_ready, 1)
                    for u, (_, _, _, n, _) in enumerate(units):
                        act.wait_ge(up_full, load_no * NU + (u + 1))
                        if u >= 2:
                            act.wait_ge(h_ready, load_no * NU + (u - 1))
                        elif not isinstance(load_no, int):
                            act.wait_ge(h_ready, load_no * NU)
                        nc.scalar.activation(sg[u % 2][:, 0:n], a_ps[u % 2][0:T, 0:n], act_fn).then_inc(act_ready, 1)

                act.wait_ge(ready, 1)
                first_half(0, 0, 0)
                with act.Fori(0, B // 2) as i:
                    for par in range(2):
                        n = i * 2 + par
                        first_half(n + 1, (n + 1) % B, 1 - par)
                        empty(act, nc.scalar.copy, n, "a", act_out)

            @block.vector
            def _(dve):
                v = nc.vector

                def products(load_no, b, nxt):
                    gated = 0
                    for u, (_, wg, c0, n, e) in enumerate(units):
                        dve.wait_ge(act_ready, load_no * NU + (u + 1))
                        hu = h[nxt][:, c0:c0 + n]
                        v.tensor_tensor(hu, sg[u % 2][:, 0:n], sg[u % 2][:, 0:n] if wg is None else g_ps[u % 2][0:T, 0:n],
                                        ALU.mult).then_inc(h_ready, 1)
                        if e is not None:
                            dve.wait_ge(h_ready, load_no * NU + (u + 1))
                            ne = e[1] - e[0]
                            w = gates[:, b, e[0]:e[1]].rearrange("t (e a) -> t e a", a=1).broadcast_to([T, ne, n // ne])
                            hv = hu.rearrange("t (e f) -> t e f", e=ne)
                            v.tensor_tensor(hv, hv, w, ALU.mult).then_inc(h_gated, 1)
                    if kind == 1:
                        dve.wait_ge(h_ready, (load_no + 1) * NU)
                        link = Link(dve, h_round, load_no * NQ)
                        fp4_round(nc, link, q, h[nxt][:], h[nxt][:])
                        assert link.n == NQ

                for n, t in enumerate(t_ps):
                    v.memset(t[:], 0.0).then_inc(x_done, 1)
                dve.wait_ge(x_done, 2)
                v.memset(sg[0][:, 0:1], 0.0).then_inc(ready, 1)
                products(0, 0, 0)
                with dve.Fori(0, B // 2) as i:
                    for par in range(2):
                        n = i * 2 + par
                        products(n + 1, (n + 1) % B, 1 - par)
                        empty(dve, v.tensor_copy, n, "v", dve_out)
                        dve.wait_ge(out_full, n + 1)
                        v.scalar_tensor_tensor(out=X[:, n, :], in0=out_ps[0:T, 0:D], scalar=gate, in1=X[:, n, :],
                                               op0=ALU.mult, op1=ALU.add).then_inc(x_done, 1)


def layer0(nc, K, ins, ctxT_dram):
    with Scope(nc, "L0a") as s:
        W = {"qk": s.sb("qk", [P, NH, D]), "vo": s.sb("vo", [P, NH, D]), "g1": s.sb("g1", [P, D]),
             "b1": s.sb("b1", [P, D]), "lat": s.sb("lat", [T, B, D]), "latT": s.sb("latT", [P, B * T])}
        with Scope(nc, "L0w") as w:
            wq, wkv, wout = w.sb("wq", [P, 1024]), w.sb("wkv", [P, 2048]), w.sb("wout", [P, 8, D])
            wqT, wkT, wvT = w.sb("wqT", [P, 8, D]), w.sb("wkT", [P, 8, D]), w.sb("wvT", [P, 8, D])
            jobs = []
            for n in range(8):
                jobs.append((wqT[:, n, :], wq[:, n * D:(n + 1) * D]))
                jobs.append((wkT[:, n, :], wkv[:, n * D:(n + 1) * D]))
                jobs.append((wvT[:, n, :], wkv[:, 1024 + n * D:1024 + (n + 1) * D]))
            transposes(nc, K, "L0t", jobs, [
                (wq[:], ins["L0_xattn_Wq"]), (wkv[:], ins["L0_xattn_Wkv"]),
                (wout[:], ins["L0_xattn_Wout"].rearrange("(n p) d -> p n d", p=P)),
                (W["g1"][:], bcast_rows(ins["L0_xattn_g1"], P, D)), (W["b1"][:], bcast_rows(ins["L0_xattn_b1"], P, D))])
            fold_heads(nc, K, W, wqT, wkT, wvT, wout)
        normalise(nc, K, "ln0a", W["lat"], W["latT"], affine=(ins["L0_xattn_g2"], ins["L0_xattn_b2"]))
        attention(nc, K, 0, W, ins, ctxT_dram)
    with Scope(nc, "L0f") as s:
        up, down, wr = s.sb("up", [P, 576]), s.sb("down", [P, 5, D]), s.sb("wr", [P, 8])
        XN, XT, gates = s.sb("XN", [T, B, D]), s.sb("XT", [P, B * T]), s.sb("gates", [T, B, 8])
        load(nc, "L0l", [
            (up[:, 0:512].rearrange("d (e f) -> d e f", e=8), ins["L0_ffn_W1"].rearrange("e d f -> d e f")),
            (up[:, 512:576], ins["L0_ffn_Ws1"]), (wr[:], ins["L0_ffn_Wr"]),
            (down[:, 0:4, :], ins["L0_ffn_W2"].rearrange("e f d -> (e f) d").rearrange("(c p) d -> p c d", p=P)),
            (down[0:64, 4, :], ins["L0_ffn_Ws2"])])
        normalise(nc, K, "ln0f", XN, XT)
        route(nc, K, 0, XT, wr[:], gates)
        ffn(nc, K, 0, XT, [(up[:, 0:512], None, 0, 512, (0, 8)), (up[:, 512:576], None, 512, 64, None)], 576,
            [P] * 4 + [64], down, gates)


def plain_attention(nc, K, kind, ins, ctxT_dram, names, turned):
    wq_n, wk_n, wv_n, wo_n, bq_n, bk_n, bv_n, bo_n = names
    with Scope(nc, f"L{kind}a") as s:
        wq, wk, wv, wo = (s.sb(n, [P, D]) for n in ("wq", "wk", "wv", "wo"))
        W = {"k": wk, "v": wv, "bk": s.sb("bk", [P, 1]), "bv": s.sb("bv", [P, D]), "bo": s.sb("bo", [P, D]),
             "q": s.sb("q", [P, B * T]), "o": s.sb("o", [P, 4 if kind != 3 else 1, D])}
        bq = s.sb("bq", [P, 1])
        split = kind != 3

        rows = {t: s.sb(f"{t}_row", [P, D]) for t in ("bq", "bk")} if split else {}

        def column(name, t):
            if split:
                return (rows[name][:], bcast_rows(ins[t], P, D))
            return ((bq if name == "bq" else W["bk"])[:], col(ins[t] if t else K["zero"]))

        small = [column("bq", bq_n), column("bk", bk_n), (W["bv"][:], bcast_rows(ins[bv_n], P, D)),
                 (W["bo"][:], bcast_rows(ins[bo_n], P, D)),
                 ]
        if turned:
            with Scope(nc, f"L{kind}aw") as w:
                raw = [w.sb(n, [P, D]) for n in ("q", "k", "v", "o")]
                to = [wq[:], wk[:], wv[:], wo[:]]
                transposes(nc, K, f"L{kind}at", [(t, r[:]) for t, r in zip(to, raw)],
                           [(r[:], ins[n]) for r, n in zip(raw, (wq_n, wk_n, wv_n, wo_n))] + small)
        else:
            load(nc, f"L{kind}l", [(t[:], ins[n]) for t, n in zip((wq, wk, wv, wo), (wq_n, wk_n, wv_n, wo_n))] + small)
        if kind == 3:
            W["o"] = wo[:].rearrange("p (a d) -> p a d", a=1)
        else:
            wqd, wkd = s.sb("wqd", [P, D]), s.sb("wkd", [P, D])
            head_outputs(nc, K, f"ho{kind}", wo[:], W["o"], 
                         [(wqd[:], wq[:], None), (wkd[:], wk[:], None),
                          (s.sb("bq_by", [P, D])[:], rows["bq"][:], bq[:]), (s.sb("bk_by", [P, D])[:], rows["bk"][:], W["bk"][:])])
            W["k"], wq = wkd, wqd
            W["q_dram"] = nc.dram_tensor(f"q{kind}", [B, 72, NH * T], BF16, kind="Internal").ap()
            W["k_dram"] = nc.dram_tensor(f"k{kind}", [2, 3, P, S2], BF16, kind="Internal").ap()
        with Scope(nc, f"L{kind}an") as n_:
            XN, XT = n_.sb("XN", [T, B, D]), n_.sb("XT", [P, B * T])
            normalise(nc, K, f"ln{kind}a", XN, XT)
            queries(nc, K, f"q{kind}", wq[:], bq[:, 0:1], float(D if kind == 3 else D // NH) ** -0.5, XT, W["q"],
                    W.get("q_dram"))
        attention(nc, K, kind, W, ins, ctxT_dram)


def layer1_ffn(nc, K, ins):
    I = 352
    with Scope(nc, "L1f") as s:
        up, down = s.sb("up", [P, 2, I]), s.sb("down", [P, 3, D])
        XN, XT = s.sb("XN", [T, B, D]), s.sb("XT", [P, B * T])
        rows = [128, 128, 96]
        with Scope(nc, "L1w") as w:
            raw, rawd = w.sb("raw", [P, 6, D]), w.sb("rawd", [P, I])
            loads, jobs, quants = [(rawd[:], ins["L1_ffn_w_down"])], [], []
            for m, name in enumerate(("L1_ffn_w_gate", "L1_ffn_w_up")):
                for c, r in enumerate(rows):
                    a = raw[0:r, 3 * m + c, :]
                    loads.append((a, ins[name][c * P:c * P + r, :]))
                    jobs.append((up[:, m, c * P:c * P + r], a))
                    quants.append(a)
            quants.append(rawd[:])
            for c, r in enumerate(rows):
                jobs.append((down[0:r, c, :], rawd[:, c * P:c * P + r]))
            transposes(nc, K, "L1t", jobs, loads, quants)
        normalise(nc, K, "ln1f", XN, XT, quant=True)
        ffn(nc, K, 1, XT, [(up[:, 0, :], up[:, 1, :], 0, I, None)], I, rows, down)


def layer2_ffn(nc, K, ins):
    E, I = 32, 64
    N = E * I // P
    with Scope(nc, "L2f") as s:
        wg, wu = s.sb("wg", [P, N + 1, P]), s.sb("wu", [P, N + 1, P])
        down, wr, gb = s.sb("down", [P, N + 1, D]), s.sb("wr", [P, E]), s.sb("gb", [T, E])
        gates, XT = s.sb("gates", [T, B, E]), s.sb("XT", [P, B * T])
        with Scope(nc, "L2w") as w:
            rg, ru, rd, rr = w.sb("rg", [P, N + 1, D]), w.sb("ru", [P, N + 1, D]), w.sb("rd", [P, N + 1, P]), w.sb("rr", [E, D])
            loads, jobs = [(rr[:], ins["L2_ffn_gate_w"]), (gb[:], bcast_rows(ins["L2_ffn_gate_bias"], T, E))], []
            for raw, to, a, b in ((rg, wg, "gate", "gate"), (ru, wu, "up", "up")):
                loads.append((raw[:, 0:N, :], ins[f"L2_ffn_expert_{a}"].rearrange("e i h -> (e i) h")
                              .rearrange("(c p) h -> p c h", p=P)))
                loads.append((raw[:, N, :], ins[f"L2_ffn_shared_{b}"]))
                jobs += [(to[:, c, :], raw[:, c, :]) for c in range(N + 1)]
            loads.append((rd[:, 0:N, :].rearrange("h c (e i) -> h (c e) i", i=I),
                          ins["L2_ffn_expert_down"].rearrange("e h i -> h e i")))
            loads.append((rd[:, N, :], ins["L2_ffn_shared_down"]))
            jobs += [(down[:, c, :], rd[:, c, :]) for c in range(N + 1)]
            jobs.append((wr[:], rr[:]))
            transposes(nc, K, "L2t", jobs, loads)
        with Scope(nc, "L2n") as n_:
            XN = n_.sb("XN", [T, B, D])
            normalise(nc, K, "ln2f", XN, XT)
        route(nc, K, 2, XT, wr[:], gates, gb[:])
        flat = lambda t, c, n: t[:, c:c + n, :].rearrange("p c f -> p (c f)")
        units = [(flat(wg, 4 * k, 4), flat(wu, 4 * k, 4), 512 * k, 512, (8 * k, 8 * k + 8)) for k in range(4)]
        units.append((flat(wg, N, 1), flat(wu, N, 1), N * P, P, None))
        ffn(nc, K, 2, XT, units, (N + 1) * P, [P] * (N + 1), down, gates)


def layer3_ffn(nc, K, ins):
    E, F = 8, 192
    with Scope(nc, "L3f") as s:
        fc, down, wr = s.sb("fc", [P, E, 2 * F]), s.sb("down", [P, E * F // P, D]), s.sb("wr", [P, E])
        gates, XT, XN = s.sb("gates", [T, B, E]), s.sb("XT", [P, B * T]), s.sb("XN", [T, B, D])
        load(nc, "L3l", [(fc[:], ins["L3_ffn_c_fc"].rearrange("e d f -> d e f")), (wr[:], ins["L3_ffn_w_gate"]),
                         (down[:], ins["L3_ffn_c_proj"].rearrange("e f d -> (e f) d").rearrange("(c p) d -> p c d", p=P))])
        normalise(nc, K, "ln3f", XN, XT)
        route(nc, K, 3, XT, wr[:], gates)
        units = [(fc[:, 2 * k:2 * k + 2, 0:F], fc[:, 2 * k:2 * k + 2, F:2 * F], 2 * k * F, 2 * F, (2 * k, 2 * k + 2))
                 for k in range(E // 2)]
        ffn(nc, K, 3, XT, units, E * F, [P] * (E * F // P), down, gates)


def flamingo(nc, ins, out):
    with Scope(nc, "k") as s:
        K = {"X": s.sb("X", [T, B, D]), "gate": s.sb("gate", [P, 8]), "ident": s.sb("ident", [P, P]),
             "hm": s.sb("hm", [P, NH]), "jm": s.sb("jm", [P, 4]), "lt4": s.sb("lt4", [P, 4, 4]),
             "lt8": s.sb("lt8", [P, 8, 8]), "tri": s.sb("tri", [T, T]), "ones": s.sb("ones", [T, T]),
             "mhalf": s.sb("mhalf", [P, 16])}
        ctxT_dram = nc.dram_tensor("ctxT", [B, P, S2], F32, kind="Internal").ap()
        K["zero"] = ins["zero"]
        constants(nc, K, ins)
        load(nc, "x", [(K["X"][:], ins["x"].rearrange("b t d -> t b d"))])
        layer0(nc, K, ins, ctxT_dram)
        give_back(nc, Scope.used)
        n1 = [f"L1_xattn_{n}" for n in ("wq_k", "wk_k", "wv_k", "wo_k", "wq_b", "wk_b", "wv_b", "wo_b")]
        n2 = [f"L2_xattn_{n}" for n in ("Wq", "Wk", "Wv", "Wo", "bq", "bk", "bv", "bo")]
        n3 = ["L3_xattn_Wq", "L3_xattn_Wk", "L3_xattn_Wv", "L3_xattn_Wo", "L3_xattn_bq", None, "L3_xattn_bv",
              "L3_xattn_bo"]
        plain_attention(nc, K, 1, ins, ctxT_dram, n1, False)
        layer1_ffn(nc, K, ins)
        give_back(nc, Scope.used)
        plain_attention(nc, K, 2, ins, ctxT_dram, n2, True)
        layer2_ffn(nc, K, ins)
        give_back(nc, Scope.used)
        plain_attention(nc, K, 3, ins, ctxT_dram, n3, True)
        layer3_ffn(nc, K, ins)
        load(nc, "y", [(out.rearrange("b t d -> t b d"), K["X"][:])])


_SKIP = ("fside_Bx16xSxS2_0",)


def kernel(**inputs):
    import concourse.bacc as bacc
    from concourse.bass_utils import run_bass_kernel_spmd

    nc = bacc.Bacc("TRN2", target_bir_lowering=False, num_devices=1)
    arrays, ins = {}, {}
    for name, a in inputs.items():
        if name in _SKIP:
            continue
        a = np.ascontiguousarray(a)
        arrays[f"in_{name}"] = a
        ins[name] = nc.dram_tensor(f"in_{name}", a.shape, mybir.dt.from_np(a.dtype), kind="ExternalInput").ap()
    arrays["in_zero"] = np.zeros(P, np.float32)
    ins["zero"] = nc.dram_tensor("in_zero", [P], F32, kind="ExternalInput").ap()
    out = nc.dram_tensor("out", [B, T, D], F32, kind="ExternalOutput").ap()
    flamingo(nc, ins, out)
    r = run_bass_kernel_spmd(nc, [arrays], core_ids=[0])
    return r.results[0]["out"]
```

```python
from contextlib import ExitStack

import numpy as np

import concourse.bass as bass
from concourse import mybir

ALU = mybir.AluOpType
ACT = mybir.ActivationFunctionType
AX = mybir.AxisListType
F32 = mybir.dt.float32
I32 = mybir.dt.int32
U32 = mybir.dt.uint32
U8 = mybir.dt.uint8
BF16 = mybir.dt.bfloat16

B, T, S2, D = 8, 100, 1444, 128
P = 128
BANK = 512
KC = 121
NC_CTX = 12
LAST = S2 - (NC_CTX - 1) * KC
NH = 16
FLT_MAX = 3.4028234663852886e38
EPS = 1e-5
NEG_MASK = 1e9


def chunk_rows(c):
    return T if c == NC_CTX else (LAST if c == NC_CTX - 1 else KC)


def chunk_at(c):
    return S2 if c == NC_CTX else c * KC


def head_of(n):
    return 4 * (n % 4) + n // 4


class Link:

    def __init__(self, eng, sem, base=0):
        self.eng, self.sem, self.base, self.n = eng, sem, base, 0

    def __call__(self, ins):
        self.n += 1
        ins.then_inc(self.sem, 1)
        self.eng.wait_ge(self.sem, self.base + self.n)


def wait_apart(eng, passed, sem, value):
    if not isinstance(value, int):
        value = eng.to_reg(value)
        eng.wait_ge(passed, 1)
    eng.wait_ge(sem, value)


class Scope:

    used = []

    def __init__(self, nc, name):
        self.nc, self.name, self.ctx = nc, name, ExitStack()

    def __enter__(self):
        self.ctx.__enter__()
        return self

    def __exit__(self, *a):
        return self.ctx.__exit__(*a)

    def sb(self, name, shape, dt=F32):
        return self.ctx.enter_context(self.nc.sbuf_tensor(f"{self.name}_{name}", shape, dt))

    def banks(self, name, n):
        return [self.ctx.enter_context(self.nc.psum_tensor(f"{self.name}_{name}{i}", [P, BANK], F32))
                for i in range(n)]

    def sem(self, name):
        h = self.nc.alloc_semaphore(f"{self.name}_{name}")
        self.used.append(h)
        return h


def give_back(nc, used):
    nc.all_engine_barrier()
    nc.clear_and_free_semaphores(used)
    nc.all_engine_barrier()
    used.clear()


def bcast_rows(ap, rows, n):
    return ap.rearrange("(a n) -> a n", a=1).broadcast_to([rows, n])


def constants(nc, K, ins):
    with Scope(nc, "const") as s:
        ld, pool_sem, act_sem = s.sem("gates_loaded"), s.sem("pool_order"), s.sem("tanh_done")
        dve_sem, ones_set = s.sem("dve_order"), s.sem("ones_set")
        with nc.Block() as block:

            @block.sync
            def _(sp):
                sp.dma_start(K["gate"][:, 0:4], bcast_rows(ins["g_xattn"], P, 4)).then_inc(ld, 16)
                sp.dma_start(K["gate"][:, 4:8], bcast_rows(ins["g_ffn"], P, 4)).then_inc(ld, 16)

            @block.scalar
            def _(act):
                act.wait_ge(ld, 32)
                nc.scalar.activation(K["gate"][:], K["gate"][:], ACT.Tanh).then_inc(act_sem, 1)

            @block.vector
            def _(dve):
                for name in ("ident", "hm", "lt4", "lt8", "tri", "ones"):
                    nc.vector.memset(K[name][:], 0.0 if name == "ident" else 1.0).then_inc(ones_set, 1)
                nc.vector.memset(K["mhalf"][:], -0.5).then_inc(ones_set, 1)
                dve.wait_ge(pool_sem, 6)
                nc.vector.tensor_reduce(K["jm"][:], K["hm"][:].rearrange("p (j g) -> p j g", g=4),
                                        AX.X, ALU.add).then_inc(dve_sem, 1)

            @block.gpsimd
            def _(pool):
                pool.wait_ge(ones_set, 7)
                link = Link(pool, pool_sem)
                link(nc.gpsimd.affine_select(out=K["ident"][:], in_=K["ident"][:], compare_op=ALU.not_equal,
                                             fill=1.0, base=0, pattern=[[-1, P]], channel_multiplier=1))
                hm = K["hm"][:].rearrange("p (j g) -> p j g", g=4)
                link(nc.gpsimd.affine_select(out=hm, in_=hm, compare_op=ALU.is_ge, fill=0.0, base=0,
                                             pattern=[[-8, 4], [-32, 4]], channel_multiplier=1))
                link(nc.gpsimd.affine_select(out=hm, in_=hm, compare_op=ALU.is_ge, fill=0.0, base=7,
                                             pattern=[[8, 4], [32, 4]], channel_multiplier=-1))
                for name, n in (("lt4", 4), ("lt8", 8)):
                    m = K[name][:]
                    link(nc.gpsimd.affine_select(out=m, in_=m, compare_op=ALU.is_ge, fill=0.0, base=-1,
                                                 pattern=[[1, n], [-1, n]], channel_multiplier=0))
                link(nc.gpsimd.affine_select(out=K["tri"][:], in_=K["tri"][:], compare_op=ALU.is_ge, fill=0.0,
                                             base=-1, pattern=[[1, T]], channel_multiplier=-1))


def normalise(nc, K, name, XN, XT, affine=None, quant=False):
    X = K["X"]
    rounds = 2 if affine else 1
    with Scope(nc, name) as s:
        st, mv, rs = s.sb("stats", [T, B, 6]), s.sb("meanvar", [T, B, 2]), s.sb("rstd", [T, B])
        bc = s.sb("affine", [T, 2, D]) if affine else None
        q = quant_buffers(s, T, B * D) if quant else None
        xt_ps = s.banks("xt", 2)
        ld, var_ready, rstd_ready = s.sem("affine_loaded"), s.sem("var_ready"), s.sem("rstd_ready")
        order, pool_order = s.sem("dve_order"), s.sem("pool_order")
        xn_ready, xt_full, xt_done = s.sem("xn_ready"), s.sem("xt_full"), s.sem("xt_done")
        with nc.Block() as block:

            @block.sync
            def _(sp):
                if affine:
                    for n in range(2):
                        sp.dma_start(bc[:, n, :], bcast_rows(affine[n], T, D)).then_inc(ld, 16)

            @block.vector
            def _(dve):
                link = Link(dve, order)
                for r in range(rounds):
                    src = X if r == 0 else XN
                    for b in range(B):
                        i = nc.vector.bn_stats(st[:, b, :], src[:, b, :])
                        i.then_inc(order, 1)
                        link.n += 1
                    dve.wait_ge(order, link.n)
                    for b in range(B):
                        i = nc.vector.bn_aggr(mv[:, b, :], st[:, b, :])
                        i.then_inc(var_ready, 1)
                    dve.wait_ge(rstd_ready, r + 1)
                    for b in range(B):
                        i = nc.vector.tensor_scalar(XN[:, b, :], src[:, b, :], mv[:, b, 0:1], rs[:, b:b + 1],
                                                    ALU.subtract, ALU.mult)
                        i.then_inc(order, 1)
                        link.n += 1
                    dve.wait_ge(order, link.n)
                if affine:
                    dve.wait_ge(ld, 32)
                    for n, op in ((0, ALU.mult), (1, ALU.add)):
                        link(nc.vector.tensor_tensor(XN[:], XN[:], bc[:, n:n + 1, :].broadcast_to([T, B, D]), op))
                if quant:
                    flat = XN[:].rearrange("p b d -> p (b d)")
                    fp4_round(nc, link, q, flat, flat)
                nc.vector.memset(mv[:, 0, 0:1], 0.0).then_inc(xn_ready, 1)

            @block.gpsimd
            def _(pool):
                for r in range(rounds):
                    pool.wait_ge(var_ready, B * (r + 1))
                    nc.gpsimd.tensor_scalar(rs[:], mv[:, :, 1], EPS, None, ALU.add).then_inc(pool_order, 1)
                    pool.wait_ge(pool_order, r + 1)
                    nc.gpsimd.tensor_tensor(rs[:], rs[:], K["mhalf"][0:T, 0:B], ALU.pow).then_inc(rstd_ready, 1)

            @block.tensor
            def _(pe):
                pe.wait_ge(xn_ready, 1)
                for b in range(B):
                    i = nc.tensor.transpose(xt_ps[b // 4][:, (b % 4) * T:(b % 4 + 1) * T], XN[:, b, :],
                                            K["ident"][0:T, 0:T])
                    if b % 4 == 3:
                        i.then_inc(xt_full, 1)

            @block.scalar
            def _(act):
                for n in range(2):
                    act.wait_ge(xt_full, n + 1)
                    nc.scalar.copy(XT[:, n * 4 * T:(n + 1) * 4 * T], xt_ps[n][:, 0:4 * T]).then_inc(xt_done, 1)


def quant_buffers(s, rows, n):
    nb = n // 16
    return {"a": s.sb("q_abs", [rows, n]), "q": s.sb("q_code", [rows, n]), "sc": s.sb("q_scale", [rows, nb]),
            "rc": s.sb("q_rscale", [rows, nb])}


def fp4_round(nc, link, buf, out, src, rows=None):
    n = src.shape[-1]
    r = src.shape[0]
    a, q = buf["a"][0:r, 0:n], buf["q"][0:r, 0:n]
    sc, rc = buf["sc"][0:r, 0:n // 16], buf["rc"][0:r, 0:n // 16]
    blk = lambda ap: ap.rearrange("p (n k) -> p n k", k=16)
    wide = lambda ap: ap.rearrange("p (n k) -> p n k", k=1).broadcast_to([r, n // 16, 16])
    v = nc.vector
    link(v.tensor_reduce(sc, blk(src), AX.X, ALU.max, apply_absolute_value=True))
    link(v.tensor_scalar(sc, sc, 1.0 / 6.0, 1e-12, ALU.mult, ALU.max))
    link(v.reciprocal(rc, sc))
    link(v.tensor_tensor(blk(a), blk(src), wide(rc), ALU.mult))
    link(v.tensor_scalar(a.bitcast(U32), a.bitcast(U32), 0x7FFFFFFF, None, ALU.bitwise_and))
    link(v.tensor_scalar(q, a, 5.0, 2.0, ALU.is_gt, ALU.mult))
    for mid in (3.5, 2.5):
        link(v.scalar_tensor_tensor(out=q, in0=a, scalar=mid, in1=q, op0=ALU.is_gt, op1=ALU.add))
    link(v.tensor_scalar(q, q, 2.0, None, ALU.mult))
    for mid in (1.75, 1.25, 0.75, 0.25):
        link(v.scalar_tensor_tensor(out=q, in0=a, scalar=mid, in1=q, op0=ALU.is_gt, op1=ALU.add))
    link(v.tensor_scalar(sc, sc, 0.5, None, ALU.mult))
    link(v.scalar_tensor_tensor(out=q.bitcast(I32), in0=src.bitcast(I32), scalar=-2 ** 31, in1=q.bitcast(I32),
                                op0=ALU.bitwise_and, op1=ALU.bitwise_or))
    link(v.tensor_tensor(blk(out), blk(q), wide(sc), ALU.mult))


def transposes(nc, K, name, jobs, loads=(), quants=(), unused=(), before=None):
    NB = 4
    with Scope(nc, name) as s:
        q = quant_buffers(s, P, max(a.shape[-1] for a in quants)) if quants else None
        ps = s.banks("t", NB)
        ld, order, full = s.sem("loaded"), s.sem("dve_order"), s.sem("bank_full")
        act_done, dve_done, qd = s.sem("act_emptied"), s.sem("dve_emptied"), s.sem("quantised")
        with nc.Block() as block:

            @block.sync
            def _(sp):
                for to, src in loads:
                    sp.dma_start(to, src).then_inc(ld, 16)

            @block.tensor
            def _(pe):
                if loads:
                    pe.wait_ge(ld, 16 * len(loads))
                if before:
                    pe.wait_ge(*before)
                if quants:
                    pe.wait_ge(qd, 1)
                for n, (to, src) in enumerate(jobs):
                    if n >= NB:
                        pe.wait_ge(dve_done if n % 2 else act_done, (n - NB) // 2 + 1)
                    r, c = src.shape
                    nc.tensor.transpose(ps[n % NB][0:c, 0:r], src, K["ident"][0:r, 0:r]).then_inc(full, 1)

            def empty(eng, copy, par, done):
                for n in range(par, len(jobs), 2):
                    to, src = jobs[n]
                    r, c = src.shape
                    eng.wait_ge(full, n + 1)
                    copy(to, ps[n % NB][0:c, 0:r]).then_inc(done, 1)

            @block.scalar
            def _(act):
                empty(act, nc.scalar.copy, 0, act_done)

            @block.vector
            def _(dve):
                if quants:
                    link = Link(dve, order)
                    for m in unused:
                        link(nc.vector.memset(m, 0.0))
                    if loads:
                        dve.wait_ge(ld, 16 * len(loads))
                    if before:
                        dve.wait_ge(*before)
                    for m in quants:
                        fp4_round(nc, link, q, m, m)
                    nc.vector.memset(q["rc"][:, 0:1], 0.0).then_inc(qd, 1)
                empty(dve, nc.vector.tensor_copy, 1, dve_done)


class Ring:

    def __init__(self, jobs, start=None, banks=2):
        self.jobs, self.banks = list(jobs), banks
        self.index = {name: n for n, (name, _) in enumerate(self.jobs)}
        self.total = {e: sum(x == e for _, x in self.jobs) for e in "av"}
        self.start = start or {"a": 0, "v": 0, "full": 0}

    def after(self):
        return {"a": self.start["a"] + self.total["a"], "v": self.start["v"] + self.total["v"],
                "full": self.start["full"] + len(self.jobs)}

    def bank(self, name):
        return self.index[name] % self.banks

    def engine(self, name):
        return self.jobs[self.index[name]][1]

    def full(self, step, name):
        return step * len(self.jobs) + (self.start["full"] + self.index[name] + 1)

    def emptied(self, step, name, engine):
        n = sum(e == engine for _, e in self.jobs[:self.index[name] + 1])
        return step * self.total[engine] + (self.start[engine] + n)

    def before(self, step, engine):
        return step * (len(self.jobs) if engine == "full" else self.total[engine]) + self.start[engine]


LAGS = (3, 2, 3)


def attention(nc, K, kind, W, ins, ctxT_dram):
    H, G, GW = NH, NH // 4, 4
    keys = S2 + T if kind == 0 else S2
    NCH = NC_CTX + (kind == 0)
    widths = [386] * 4 if kind == 0 else [482, 482, 480]
    U = len(widths)
    at = [sum(widths[:u]) for u in range(U)]
    SPLIT = kind in (1, 2)
    SB, NR = 3, 3 if kind == 0 else 4
    NP = 4
    job_chunks = [list(range(4 * k, 4 * k + 4)) for k in range(3)]
    if kind == 0:
        job_chunks[2].append(NC_CTX)
    X = K["X"]
    gate = K["gate"][0:T, kind:kind + 1]

    if kind == 0:
        part_a = [("C0", "a"), ("C1", "a"), ("C2", "a")]
        part_b = [("X0", "v"), ("X1", "a"), ("X2", "v"), ("Q0", "a"), ("Q1", "v"), ("Q2", "a"), ("Q3", "v")]
    else:
        part_a = [("K0", "a"), ("K1", "a"), ("K2", "a")]
        part_b = [("V0", "v"), ("V1", "v"), ("V2", "v")]
        if kind == 1:
            part_b = [("V0", "v"), ("G0", "a"), ("V1", "v"), ("G1", "a"), ("V2", "v"), ("G2", "a")]

    ROWS, NSPLIT = 9 * (D // NH), 4 * U

    SHIFTED = (2, 6, 10, 14)

    def weighted_after(h):
        return h + 1 + sum(x <= h for x in SHIFTED)

    def t_jobs(n):
        if kind == 1:
            return [((n, k), ("vaa" if n in SHIFTED else "vva")[k]) for k in range(3)]
        return [((n, k), "v" if k == 1 else "a") for k in range(3)]

    LAG = LAGS[kind]
    steps = range(LAG, H + LAG)
    plan = {s: [] for s in steps}
    if kind == 0:
        for x, s in zip(part_a, (4, 5, 7)):
            plan[s].append(x)
        for x, s in zip(part_b, (13, 14, 15, 8, 9, 11, 12)):
            plan[s].append(x)
    else:
        for k, x in enumerate(part_a):
            plan[3 + k].append(x)
        for k, x in enumerate(part_b):
            plan[7 + k].append(x)

    def group_at(s):
        if s == H + LAG - 1:
            return G - 1
        j, r = divmod(s - LAG, 4)
        return j - 1 if r == 0 and j > 0 else None

    body = []
    for s in steps:
        body += t_jobs(s - LAG)
        if (kind == 0 or group_at(s) == G - 1) and group_at(s) is not None:
            body.append((f"R{group_at(s)}", "a"))
        body += plan[s]
    if kind != 0:
        body.append(("O", "v"))
    first = Ring(part_a + part_b, banks=NR)
    ring = Ring(body, first.after(), banks=NR)

    with Scope(nc, f"attn{kind}") as s_:
        sb, sem = s_.sb, s_.sem
        if SPLIT:
            kT = [sb("k", [P, S2])] * 2
            kp = sb("kparts", [P, 3, S2], BF16)
            stack = [sb(f"stack{i}", [ROWS, 4, S2], BF16) for i in range(2)]
            Qs = [sb(f"Q{i}", [ROWS, H, T], BF16) for i in range(2)]
        else:
            kT = [sb(f"kT{i}", [P, keys]) for i in range(2)]
            Qs = [sb(f"Q{i}", [P, H, T]) for i in range(2)]
        V = [sb(f"V{i}", [KC, NCH, D]) for i in range(2)]
        bias = [sb(f"bias{i}", [T, keys]) for i in range(2)]
        prob = sb("prob", [T, NP, keys])
        pT = sb("pT", [KC, 2, NCH, GW, T])
        mpart, nmax = sb("mpart", [T, 2, H, U]), sb("nmax", [T, 2, H])
        RW = 32 if kind in (1, 2) else 1
        den, rden = sb("den", [T, 2, H]), sb("rden", [T, 2, H * RW])
        R = sb("R", [P, GW * T])
        Y = [sb(f"Y{i}", [P, GW * T]) for i in range(2)]
        upd = sb("upd", [T, D])
        if kind == 0:
            cn = sb("ctx", [KC, NC_CTX, D])
            stage = sb("ctxT", [P, S2])
            keep = sb("keep", [T, S2], U8)
            st, mv, rs = sb("st", [KC, NC_CTX, 6]), sb("mv", [KC, NC_CTX, 2]), sb("rs", [KC, NC_CTX])
        else:
            ctxT = sb("ctxT", [P, S2])
        if kind == 1:
            mask = sb("mask", [T, S2], I32)
            Gp = sb("group", [T, S2])
            GT = [sb(f"GT{i}", [KC, NC_CTX, T]) for i in range(2)]
        if kind == 2:
            pad = sb("pad", [T, S2], U8)
            attn = sb("attn", [T, S2])
        s_ps, r_ps = s_.banks("score", SB), s_.banks("ring", NR)
        o_ps = s_.banks("av", 1)[0]
        if kind == 0:
            out_ps = s_.banks("out", 1)[0]

        ready = sem("ready")
        ld_ctx, ld_mask, ld_g = sem("ctx_loaded"), sem("mask_loaded"), sem("group_loaded")
        ld_const, stored = sem("const_loaded"), sem("ctxT_stored")
        bias_ready = sem("bias_ready")
        side_ready = sem("pool_ready")
        score_full = sem("score_full")
        score_used = sem("score_used")
        max_ready = sem("max_ready")
        prob_ready = sem("prob_ready")
        rden_ready = sem("rden_ready")
        ring_full, act_out, dve_out = sem("ring_full"), sem("act_emptied"), sem("dve_emptied")
        av_full = sem("av_full")
        y_ready = sem("y_ready")
        folded = sem("y_used")
        upd_ready, x_done = sem("update_ready"), sem("x_done")
        ln, var_ready, rstd_ready, rs_order, xn_ready = (sem("ln"), sem("var_ready"), sem("rstd_ready"),
                                                         sem("rs_order"), sem("xn_ready"))
        out_of = {"a": act_out, "v": dve_out}
        NSIDE = 2 if kind == 0 else 1
        k_split, kp_stored = sem("k_split"), sem("kparts_stored")
        q_loaded = sem("q_loaded")
        weighted = sem("weighted")
        rden_order = sem("rden_order")
        stack_loaded = [sem(f"stack{i}_loaded") for i in range(2)]

        def split_keys(eng, g, rg, step, load_no, first_op, last_op):
            for done in range(first_op, last_op):
                u, op = done // 4, done % 4
                if done == 0 and not isinstance(load_no, int):
                    wait_apart(eng, ready, kp_stored, load_no * 16)
                if op == 0:
                    wait_apart(eng, ready, act_out, rg.emptied(step, f"K{u}", "a"))
                if done:
                    wait_apart(eng, ready, k_split, load_no * NSPLIT + done)
                x = kT[0][:, at[u]:at[u] + widths[u]]
                parts = [kp[:, m, at[u]:at[u] + widths[u]] for m in range(3)]
                if op % 2 == 0:
                    i_ = g.tensor_copy(parts[op // 2], x)
                else:
                    i_ = g.tensor_tensor(x if op == 1 else parts[2], x, parts[op // 2], ALU.subtract)
                i_.then_inc(k_split, 1)

        with nc.Block() as block:

            @block.sync
            def _(sp):
                if kind == 2:
                    sp.dma_start(attn[:], ins["fside_SxS2_0"]).then_inc(ld_const, 16)

                def load(step, b):
                    if kind == 0:
                        n = (NC_CTX - 1) * KC
                        sp.dma_start(cn[:, 0:NC_CTX - 1, :],
                                     ins["ctx_1024"][b, 0:n, :].rearrange("(c p) d -> p c d", p=KC)).then_inc(ld_ctx, 16)
                        sp.dma_start(cn[0:LAST, NC_CTX - 1, :], ins["ctx_1024"][b, n:S2, :]).then_inc(ld_ctx, 16)
                        sp.dma_start(keep[:], bcast_rows(ins["mask_BxS2_bk0"][b, :], T, S2)).then_inc(ld_mask, 16)
                    else:
                        sp.dma_start(ctxT[:], ctxT_dram[b]).then_inc(ld_ctx, 16)
                    if kind == 1:
                        sp.dma_start(mask[:], ins["mask_BxSxS2_ik1"][b]).then_inc(ld_mask, 16)
                        sp.dma_start(Gp[:], ins["fside_BxSxS2_0"][b]).then_inc(ld_g, 16)
                    if kind == 2:
                        sp.dma_start(pad[:], bcast_rows(ins["mask_BxS2_bf0"][b, :], T, S2)).then_inc(ld_mask, 16)

                def store(rg, step, b):
                    wait_apart(sp, ready, act_out, rg.emptied(step, "C2", "a"))
                    sp.dma_start(ctxT_dram[b], stage[:]).then_inc(stored, 16)

                def used(rg, step, load_no):
                    last = max((x for x, _ in part_a + part_b if x[0] != "Q"), key=lambda x: rg.index[x])
                    wait_apart(sp, ready, ring_full, rg.full(step, last))
                    if kind == 0:
                        wait_apart(sp, ready, ln, load_no * 25 + 24)
                    wait_apart(sp, ready, bias_ready, load_no + 1)

                def load_q(b, nxt):
                    sp.dma_start(Qs[nxt][:].rearrange("r h t -> r (h t)"), W["q_dram"][b]).then_inc(q_loaded, 16)

                def store_parts(load_no, nxt):
                    wait_apart(sp, ready, k_split, (load_no + 1) * NSPLIT)
                    sp.dma_start(W["k_dram"][nxt].rearrange("a p s -> p a s"), kp[:]).then_inc(kp_stored, 16)

                def load_group(load_no, nxt, j):
                    wait_apart(sp, ready, kp_stored, (load_no + 1) * 16)
                    src = W["k_dram"][nxt].rearrange("a (d j n) s -> j (a d) (n s)", d=8, j=4)[j]
                    for a in range(3):
                        sp.dma_start(stack[j % 2][24 * a:24 * a + 24].rearrange("r n s -> r (n s)"),
                                     src).then_inc(stack_loaded[j % 2], 16)

                if kind == 0:
                    sp.wait_ge(ready, 1)
                load(0, 0)
                if kind == 0:
                    store(first, 0, 0)
                if SPLIT:
                    load_q(0, 0)
                    store_parts(0, 0)
                    load_group(0, 0, 0)
                    load_group(0, 0, 1)
                used(first, 0, 0)
                load(1, 1)
                with sp.Fori(0, B // 2) as i:
                    for par in range(2):
                        n = i * 2 + par
                        b1, b2 = sp.snap((n + 1) % B), sp.snap((n + 2) % B)
                        if kind == 0:
                            store(ring, n, b1)
                        if SPLIT:
                            wait_apart(sp, ready, score_full, n * (H * U) + 1)
                            load_q(b1, 1 - par)
                            wait_apart(sp, ready, score_full, n * (H * U) + 4 * U)
                            load_group(n, par, 2)
                            wait_apart(sp, ready, score_full, n * (H * U) + 8 * U)
                            load_group(n, par, 3)
                            store_parts(n + 1, 1 - par)
                        used(ring, n, n + 1)
                        load(n + 2, b2)
                        if SPLIT:
                            wait_apart(sp, ready, score_full, n * (H * U) + 12 * U)
                            load_group(n + 1, 1 - par, 0)
                            wait_apart(sp, ready, score_full, n * (H * U) + 16 * U)
                            load_group(n + 1, 1 - par, 1)
                if kind == 0:
                    sp.wait_ge(stored, 16 * (B + 1))
                if SPLIT:
                    sp.wait_ge(q_loaded, (B + 1) * 16)
                    for x in stack_loaded:
                        sp.wait_ge(x, (2 * B + 1) * 48)
                sp.wait_ge(ld_ctx, (B + 2) * (32 if kind == 0 else 16))
                sp.wait_ge(ld_mask, (B + 2) * 16)
                if kind == 1:
                    sp.wait_ge(ld_g, (B + 2) * 16)

            @block.gpsimd
            def _(pool):
                def side(step, b, nxt):
                    if kind == 0:
                        wait_apart(pool, ready, var_ready, (step + 1) * NC_CTX)
                        nc.gpsimd.tensor_scalar(rs[:], mv[:, :, 1], EPS, None, ALU.add).then_inc(rs_order, 1)
                        pool.wait_ge(rs_order, step + 1)
                        nc.gpsimd.tensor_tensor(rs[:], rs[:], K["mhalf"][0:KC, 0:NC_CTX], ALU.pow).then_inc(rstd_ready, 1)
                        nc.gpsimd.tensor_copy(V[nxt][0:T, NC_CTX, :], W["lat"][:, b, :]).then_inc(side_ready, 1)
                        nc.gpsimd.tensor_copy(kT[nxt][:, S2:keys], W["latT"][:, bass.ds(b * T, T)]).then_inc(side_ready, 1)

                def weight(step, par, h):
                    for name, e in t_jobs(h):
                        if e == "a":
                            pool.wait_ge(act_out, ring.emptied(step, name, "a"))
                            ch = job_chunks[name[1]]
                            x = pT[:, (h // 4) % 2, ch[0]:ch[0] + len(ch), h % 4, :]
                            nc.gpsimd.tensor_tensor(x, x, GT[par][:, ch[0]:ch[0] + len(ch), :], ALU.mult).then_inc(weighted, 1)

                pool.wait_ge(ready, 1)
                if not SPLIT:
                    side(0, 0, 0)
                with pool.Fori(0, B // 2) as i:
                    for par in range(2):
                        n = i * 2 + par
                        if SPLIT:
                            for s in steps:
                                if kind == 1:
                                    weight(n, par, s - LAG)
                                if 5 <= s < 5 + NSPLIT // 2:
                                    split_keys(pool, nc.gpsimd, ring, n, n + 1, 2 * (s - 5), 2 * (s - 5) + 2)
                        else:
                            b = pool.snap((n + 1) % B)
                            wait_apart(pool, ready, score_full, n * (H * U) + ((LAG * U if kind == 0 else 0) + 1))
                            side(n + 1, b, 1 - par)

            @block.tensor
            def _(pe):
                ident = K["ident"]

                def job(rg, step, name):
                    n = rg.index[name]
                    if n >= NR:
                        prev, e = rg.jobs[n - NR]
                        pe.wait_ge(out_of[e], rg.emptied(step, prev, e))
                    elif n == 0 and rg is ring:
                        for e in "av":
                            pe.wait_ge(out_of[e], rg.before(step, e))
                    return r_ps[n % NR]

                def scores(step, par, h, u):
                    m = h * U + u
                    if m >= SB or not isinstance(step, int):
                        pe.wait_ge(score_used, step * (H * U) + (m - SB + 1))
                    if SPLIT:
                        j = h // 4
                        if h % 4 == 0 and u == 0:
                            pe.wait_ge(stack_loaded[j % 2], step * 96 + (j // 2 + 1) * 48)
                        k = stack[j % 2][:, h % 4, at[u]:at[u] + widths[u]]
                    else:
                        k = kT[par][:, at[u]:at[u] + widths[u]]
                    i_ = nc.tensor.matmul(s_ps[m % SB][0:T, 0:widths[u]], Qs[par][:, h, :], k, start=True, stop=True)
                    i_.then_inc(score_full, 1)

                def turn(step, par, h, k):
                    if k == 0:
                        pe.wait_ge(prob_ready, step * H + (h + 1))
                    slot = (h + par * H) % NP
                    ps = job(ring, step, (h, k))
                    for x, c in enumerate(job_chunks[k]):
                        kc, c0 = chunk_rows(c), chunk_at(c)
                        i_ = nc.tensor.transpose(ps[0:kc, x * T:(x + 1) * T], prob[:, slot, c0:c0 + kc],
                                                 ident[0:T, 0:T])
                    i_.then_inc(ring_full, 1)

                def spread(step, par, j):
                    name = f"R{j}"
                    ps = job(ring, step, name)
                    pe.wait_ge(rden_ready, step * (G if kind == 0 else 1) + ((j if kind == 0 else 0) + 1))
                    for x in range(GW):
                        if kind == 0:
                            r = rden[:, par, 4 * j + x:4 * j + x + 1].broadcast_to([T, P])
                        else:
                            r = rden[:, par, P * x:P * x + P]
                        i_ = nc.tensor.transpose(ps[:, x * T:(x + 1) * T], r, ident[0:T, 0:T])
                    i_.then_inc(ring_full, 1)

                def values(step, par, j):
                    last = GW * (j + 1) - 1
                    for e in "av":
                        if any(x == e for _, x in t_jobs(last)):
                            pe.wait_ge(out_of[e], ring.emptied(step, (last, 2), e))
                    if kind == 1:
                        pe.wait_ge(weighted, step * weighted_after(H - 1) + weighted_after(4 * j + 3))
                    if kind == 0 and j:
                        pe.wait_ge(y_ready, step * G + j)
                    slot = j % 2
                    for c in range(NCH):
                        kc = chunk_rows(c)
                        flags = {"start": c == 0, "stop": c == NCH - 1}
                        if kind == 0:
                            i_ = nc.tensor.matmul(o_ps[:, 0:GW * T], V[par][0:kc, c, :],
                                                  pT[0:kc, slot, c, :, :].rearrange("p g t -> p (g t)"), **flags)
                        else:
                            for g in range(4):
                                i_ = nc.tensor.matmul(o_ps[32 * g:32 * g + 32, j * T:(j + 1) * T],
                                                      V[par][0:kc, c, 32 * g:32 * g + 32],
                                                      pT[0:kc, slot, c, g, :], **flags)
                    i_.then_inc(av_full, 1)

                def output(step, j):
                    pe.wait_ge(y_ready, step * (G if kind == 0 else 1) + ((j if kind == 0 else 0) + 1))
                    ps = out_ps if kind == 0 else job(ring, step, "O")
                    for x in range(GW):
                        if kind == 0:
                            n, w, y = 4 * j + x, W["vo"][:, 4 * x + j, :], Y[j % 2]
                        else:
                            n, w, y = x, W["o"][:, x, :], Y[0]
                        i_ = nc.tensor.matmul(ps[0:T, 0:D], y[:, x * T:(x + 1) * T], w, start=(n == 0),
                                              stop=(n == (H if kind == 0 else GW) - 1))
                    i_.then_inc(folded if kind == 0 else ring_full, 1)

                def project(rg, step, load_no, nxt, b, name):
                    what, k = name[0], int(name[1])
                    chunks = range(4 * k, 4 * k + 4)
                    if name == "C0" or name == "K0":
                        pe.wait_ge(ld_ctx, (load_no + 1) * (32 if kind == 0 else 16))
                    if name == "X0":
                        pe.wait_ge(xn_ready, load_no + 1)
                    if name == "G0":
                        pe.wait_ge(ld_g, (load_no + 1) * 16)
                    ps = job(rg, step, name)
                    if what in "CX":
                        for x, c in enumerate(chunks):
                            kc = chunk_rows(c)
                            src = (cn if what == "C" else V[nxt])[0:kc, c, :]
                            i_ = nc.tensor.transpose(ps[:, x * KC:x * KC + kc], src, ident[0:kc, 0:kc])
                    elif what == "Q":
                        for g in range(4):
                            i_ = nc.tensor.matmul(ps[:, g * T:(g + 1) * T], W["qk"][:, 4 * g + k, :],
                                                  W["latT"][:, bass.ds(b * T, T)], start=True, stop=True)
                    elif what == "K":
                        i_ = nc.tensor.matmul(ps[:, 0:widths[k]], W["k"][:], ctxT[:, at[k]:at[k] + widths[k]],
                                              start=True, stop=True)
                    else:
                        for x, c in enumerate(chunks):
                            kc, c0 = chunk_rows(c), chunk_at(c)
                            if what == "V":
                                i_ = nc.tensor.matmul(ps[0:kc, x * D:(x + 1) * D], ctxT[:, c0:c0 + kc], W["v"][:],
                                                      start=True, stop=True)
                            else:
                                i_ = nc.tensor.transpose(ps[0:kc, x * T:(x + 1) * T], Gp[:, c0:c0 + kc],
                                                         ident[0:T, 0:T])
                    i_.then_inc(ring_full, 1)

                def operands(rg, step, load_no):
                    for e in "av":
                        names = [x for x, who in part_a + part_b if who == e]
                        last = max(names, key=lambda x: rg.index[x])
                        pe.wait_ge(out_of[e], rg.emptied(step, last, e))
                    if SPLIT:
                        pe.wait_ge(q_loaded, (load_no + 1) * 16)
                    else:
                        pe.wait_ge(side_ready, (load_no + 1) * NSIDE)

                pe.wait_ge(ready, 1)
                for name, _ in part_a + part_b:
                    project(first, 0, 0, 0, 0, name)
                operands(first, 0, 0)
                for h in range(LAG):
                    for u in range(U):
                        scores(0, 0, h, u)
                with pe.Fori(0, B // 2) as i:
                    for par in range(2):
                        n = i * 2 + par
                        b = pe.snap((n + 1) % B)
                        for s in steps:
                            if s == H:
                                operands(ring, n, n + 1)
                            for u in range(U):
                                scores(n + s // H, par ^ (s // H), s % H, u)
                                if u < 3:
                                    turn(n, par, s - LAG, u)
                            j = group_at(s)
                            if j is not None:
                                if kind == 0 or j == G - 1:
                                    spread(n, par, j)
                                values(n, par, j)
                            for name, _ in plan[s]:
                                project(ring, n, n + 1, 1 - par, b, name)
                            if kind == 0 and s in (LAG + 6, LAG + 10):
                                output(n, (s - LAG - 6) // 4)
                        if kind == 0:
                            output(n, G - 2)
                        output(n, G - 1)

            @block.scalar
            def _(act):
                def out(rg, step, name):
                    act.wait_ge(ring_full, rg.full(step, name))
                    return r_ps[rg.bank(name)]

                def turned(step, par, h):
                    for (name, e) in t_jobs(h):
                        if e != "a":
                            continue
                        ch = job_chunks[name[1]]
                        j, g = h // 4, h % 4
                        slot = j % 2
                        ps = out(ring, step, name)
                        if j >= 2 and h % 4 < 2:
                            act.wait_ge(av_full, step * G + (j - 1))
                        nc.scalar.copy(pT[:, slot, ch[0]:ch[0] + len(ch), g, :],
                                       ps[0:KC, 0:len(ch) * T].rearrange("p (c t) -> p c t", t=T)).then_inc(act_out, 1)

                def expo(step, par, h):
                    act.wait_ge(max_ready, step * H + (h + 1))
                    p = prob[:, (h + par * H) % NP, :]
                    nc.scalar.activation(p, p, ACT.Exp, bias=nmax[:, par, h:h + 1],
                                         accum_out=den[:, par, h:h + 1]).then_inc(prob_ready, 1)

                def spread(step, j):
                    ps = out(ring, step, f"R{j}")
                    if kind == 0 and j:
                        act.wait_ge(y_ready, step * G + j)
                    nc.scalar.copy(R[:], ps[:, 0:GW * T]).then_inc(act_out, 1)

                def projected(rg, step, load_no, nxt, part):
                    for name, e in part:
                        if e != "a":
                            continue
                        k = int(name[1])
                        ps = out(rg, step, name)
                        if name[0] == "C":
                            if k == 0 and rg is ring:
                                act.wait_ge(stored, load_no * 16)
                            w = min(4 * KC, S2 - 4 * k * KC)
                            i_ = nc.scalar.copy(stage[:, 4 * k * KC:4 * k * KC + w], ps[:, 0:w])
                        elif name[0] == "X":
                            w = min(4 * KC, S2 - 4 * k * KC)
                            i_ = nc.scalar.copy(kT[nxt][:, 4 * k * KC:4 * k * KC + w], ps[:, 0:w])
                        elif name[0] == "Q":
                            i_ = nc.scalar.copy(Qs[nxt][:, 4 * k:4 * k + 4, :],
                                                ps[:, 0:4 * T].rearrange("p (g t) -> p g t", t=T))
                        elif name[0] == "K":
                            if SPLIT and rg is ring:
                                act.wait_ge(k_split, load_no * NSPLIT)
                            i_ = nc.scalar.activation(kT[nxt][:, at[k]:at[k] + widths[k]], ps[:, 0:widths[k]],
                                                      ACT.Identity, bias=W["bk"][:, 0:1])
                        else:
                            if k == 0 and rg is ring:
                                act.wait_ge(weighted, step * weighted_after(H - 1) + weighted_after(3))
                            i_ = nc.scalar.copy(GT[nxt][:, 4 * k:4 * k + 4, :],
                                                ps[0:KC, 0:4 * T].rearrange("p (c t) -> p c t", t=T))
                        i_.then_inc(act_out, 1)

                act.wait_ge(ready, 1)
                projected(first, 0, 0, 0, part_a + part_b)
                for h in range(LAG):
                    expo(0, 0, h)
                with act.Fori(0, B // 2) as i:
                    for par in range(2):
                        n = i * 2 + par
                        for s in steps:
                            turned(n, par, s - LAG)
                            j = group_at(s)
                            if j is not None and (kind == 0 or j == G - 1):
                                spread(n, j)
                            projected(ring, n, n + 1, 1 - par, plan[s])
                            expo(n + s // H, par ^ (s // H), s % H)

            @block.vector
            def _(dve):
                v = nc.vector


                def masked(step, par, h, between, last=None):
                    if h == 0:
                        dve.wait_ge(bias_ready, step + 1)
                    if last is not None:
                        dve.wait_ge(ring_full, ring.full(*last))
                    slot = (h + par * H) % NP
                    for u in range(U):
                        m = h * U + u
                        wait_apart(dve, ready, score_full, step * (H * U) + (m + 1))
                        i_ = v.tensor_tensor_reduce(prob[:, slot, at[u]:at[u] + widths[u]], s_ps[m % SB][0:T, 0:widths[u]],
                                                    bias[par][:, at[u]:at[u] + widths[u]], 1.0, -FLT_MAX,
                                                    ALU.add, ALU.max, mpart[:, par, h, u:u + 1])
                        i_.then_inc(score_used, 1)
                        between(u)
                    dve.wait_ge(score_used, step * (H * U) + (h + 1) * U)
                    v.tensor_reduce(nmax[:, par, h:h + 1], mpart[:, par, h, :], AX.X, ALU.max,
                                    negate=True).then_inc(max_ready, 1)

                def out(rg, step, name):
                    dve.wait_ge(ring_full, rg.full(step, name))
                    return r_ps[rg.bank(name)]

                def turned(step, par, h, only=(0, 1, 2)):
                    for (name, e) in t_jobs(h):
                        if e != "v" or name[1] not in only:
                            continue
                        ch = job_chunks[name[1]]
                        j, g = h // 4, h % 4
                        slot = j % 2
                        ps = out(ring, step, name)
                        if j >= 2 and h % 4 < 2:
                            dve.wait_ge(av_full, step * G + (j - 1))
                        to = pT[:, slot, ch[0]:ch[0] + len(ch), g, :]
                        src = ps[0:KC, 0:len(ch) * T].rearrange("p (c t) -> p c t", t=T)
                        if kind == 1:
                            if h == 0 and name[1] == 0:
                                dve.wait_ge(act_out, ring.before(step, "a"))
                            i_ = v.tensor_tensor(to, src, GT[par][:, ch[0]:ch[0] + len(ch), :], ALU.mult)
                        else:
                            i_ = v.tensor_copy(to, src)
                        i_.then_inc(dve_out, 1)

                def recip(step, par, j):
                    n = 4 * (j + 1) if kind == 0 else H
                    dve.wait_ge(prob_ready, step * H + n)
                    lo = n - 4 if kind == 0 else 0
                    if RW == 1:
                        v.reciprocal(rden[:, par, lo:n], den[:, par, lo:n]).then_inc(rden_ready, 1)
                    else:
                        v.reciprocal(den[:, par, lo:n], den[:, par, lo:n]).then_inc(rden_order, 1)
                        dve.wait_ge(rden_order, step + 1)
                        v.tensor_copy(rden[:, par, :].rearrange("t (h r) -> t h r", r=RW),
                                      den[:, par, :].rearrange("t (h r) -> t h r", r=1).broadcast_to([T, H, RW])
                                      ).then_inc(rden_ready, 1)

                def divide(step, j):
                    dve.wait_ge(act_out, ring.emptied(step, f"R{j}", "a"))
                    dve.wait_ge(av_full, step * G + (j + 1))
                    if kind == 0 and j >= 2:
                        dve.wait_ge(folded, step * G + (j - 1))
                    v.tensor_tensor(Y[j % 2 if kind == 0 else 0][:], o_ps[:, 0:GW * T], R[:], ALU.mult).then_inc(y_ready, 1)

                def projected(rg, step, load_no, nxt, part):
                    for name, e in part:
                        if e != "v":
                            continue
                        k = int(name[1])
                        ps = out(rg, step, name)
                        if name[0] == "X":
                            w = min(4 * KC, S2 - 4 * k * KC)
                            i_ = v.tensor_copy(kT[nxt][:, 4 * k * KC:4 * k * KC + w], ps[:, 0:w])
                        elif name[0] == "Q":
                            i_ = v.tensor_copy(Qs[nxt][:, 4 * k:4 * k + 4, :],
                                               ps[:, 0:4 * T].rearrange("p (g t) -> p g t", t=T))
                        elif name[0] == "K":
                            if SPLIT and rg is ring:
                                dve.wait_ge(k_split, load_no * NSPLIT)
                            i_ = v.tensor_scalar(kT[nxt][:, at[k]:at[k] + widths[k]], ps[:, 0:widths[k]],
                                                 W["bk"][:, 0:1], None, ALU.add)
                        else:
                            bv = W["bv"][0:KC, :].rearrange("p (a d) -> p a d", a=1).broadcast_to([KC, 4, D])
                            i_ = v.tensor_tensor(V[nxt][:, 4 * k:4 * k + 4, :],
                                                 ps[0:KC, 0:4 * D].rearrange("p (c d) -> p c d", d=D), bv, ALU.add)
                        i_.then_inc(dve_out, 1)

                def build_bias(load_no, nxt):
                    dve.wait_ge(ld_mask, (load_no + 1) * 16)
                    b = bias[nxt][:, 0:S2]
                    if kind == 0:
                        i_ = v.tensor_scalar(b, keep[:], FLT_MAX, -FLT_MAX, ALU.mult, ALU.add)
                    elif kind == 1:
                        i_ = v.tensor_scalar(b, mask[:], NEG_MASK, -NEG_MASK, ALU.mult, ALU.add)
                    else:
                        i_ = v.scalar_tensor_tensor(out=b, in0=pad[:], scalar=-FLT_MAX, in1=attn[:],
                                                    op0=ALU.mult, op1=ALU.add)
                    i_.then_inc(bias_ready, 1)

                def ln_stats(load_no, c):
                    if c == 0:
                        dve.wait_ge(ld_ctx, (load_no + 1) * 32)
                    v.bn_stats(st[:, c, :], cn[:, c, :]).then_inc(ln, 1)

                def ln_var(load_no, c):
                    wait_apart(dve, ready, ln, load_no * 25 + (c + 1))
                    v.bn_aggr(mv[:, c, :], st[:, c, :]).then_inc(var_ready, 1)

                def ln_apply(load_no, nxt, c):
                    if c == 0:
                        dve.wait_ge(rstd_ready, load_no + 1)
                    v.tensor_scalar(V[nxt][:, c, :], cn[:, c, :], mv[:, c, 0:1], rs[:, c:c + 1],
                                    ALU.subtract, ALU.mult).then_inc(ln, 1)

                def ln_affine(load_no, nxt):
                    x = V[nxt][:, 0:NC_CTX, :]
                    g1, b1 = (W[k][0:KC, :].rearrange("p (a d) -> p a d", a=1).broadcast_to([KC, NC_CTX, D])
                              for k in ("g1", "b1"))
                    dve.wait_ge(ln, load_no * 25 + 24)
                    v.tensor_tensor(x, x, g1, ALU.mult).then_inc(ln, 1)
                    dve.wait_ge(ln, load_no * 25 + 25)
                    v.tensor_tensor(x, x, b1, ALU.add).then_inc(xn_ready, 1)

                for n, t in enumerate(r_ps):
                    v.memset(t[:], 0.0).then_inc(x_done, 1)
                extra = NR
                if kind == 0:
                    v.memset(cn[96:KC, NC_CTX - 1, :], 0.0).then_inc(x_done, 1)
                    for t in bias:
                        v.memset(t[:, S2:keys], 0.0).then_inc(x_done, 1)
                    extra += 3
                dve.wait_ge(x_done, extra)
                if kind == 2:
                    dve.wait_ge(ld_const, 16)
                v.memset(upd[:], 0.0).then_inc(ready, 1)

                if kind == 0:
                    for c in range(NC_CTX):
                        ln_stats(0, c)
                    for c in range(NC_CTX):
                        ln_var(0, c)
                    for c in range(NC_CTX):
                        ln_apply(0, 0, c)
                    ln_affine(0, 0)
                build_bias(0, 0)
                if SPLIT:
                    split_keys(dve, v, first, 0, 0, 0, NSPLIT)
                projected(first, 0, 0, 0, part_a + part_b)
                for h in range(LAG):
                    masked(0, 0, h, lambda u: None)
                with dve.Fori(0, B // 2) as i:
                    for par in range(2):
                        n = i * 2 + par
                        for s in steps:
                            last = (n, (s - NP, 2)) if s >= NP else None
                            masked(n + s // H, par ^ (s // H), s % H, lambda u: turned(n, par, s - LAG, (u,)), last)
                            if kind == 0:
                                if s % 4 == 0:
                                    recip(n, par, s // 4 - 1)
                                if group_at(s - 1) is not None and s > LAG:
                                    divide(n, group_at(s - 1))
                                if 3 <= s <= 6:
                                    for c in range(3 * (s - 3), 3 * (s - 2)):
                                        ln_stats(n + 1, c)
                                if 7 <= s <= 8:
                                    for c in range(6 * (s - 7), 6 * (s - 6)):
                                        ln_var(n + 1, c)
                                if 9 <= s <= 10:
                                    for c in range(6 * (s - 9), 6 * (s - 8)):
                                        ln_apply(n + 1, 1 - par, c)
                                if s == 11:
                                    ln_affine(n + 1, 1 - par)
                            if s == 7:
                                build_bias(n + 1, 1 - par)
                            if s == H and kind in (1, 2):
                                recip(n, par, G - 1)
                            projected(ring, n, n + 1, 1 - par, plan[s])
                        divide(n, G - 1)
                        if kind == 0:
                            dve.wait_ge(folded, (n + 1) * G)
                            src = out_ps[0:T, 0:D]
                        else:
                            v.tensor_tensor(upd[:], out(ring, n, "O")[0:T, 0:D], W["bo"][0:T, :], ALU.add).then_inc(dve_out, 1)
                            dve.wait_ge(dve_out, ring.emptied(n, "O", "v"))
                            src = upd[:]
                        v.scalar_tensor_tensor(out=X[:, n, :], in0=src, scalar=gate, in1=X[:, n, :],
                                               op0=ALU.mult, op1=ALU.add).then_inc(x_done, 1)


def queries(nc, K, name, w, bias_col, scale, XT, q, q_dram=None):
    with Scope(nc, name) as s:
        ps = s.banks("q", 2)
        parts = [s.sb(f"part{m}", [P, B * T], BF16) for m in range(3)] if q_dram is not None else []
        full, done, stored = s.sem("full"), s.sem("done"), s.sem("stored")
        with nc.Block() as block:

            @block.tensor
            def _(pe):
                for n in range(2):
                    nc.tensor.matmul(ps[n][:, 0:4 * T], w, XT[:, n * 4 * T:(n + 1) * 4 * T], start=True,
                                     stop=True).then_inc(full, 1)

            @block.vector
            def _(dve):
                for n in range(2):
                    dve.wait_ge(full, n + 1)
                    nc.vector.tensor_scalar(q[:, n * 4 * T:(n + 1) * 4 * T], ps[n][:, 0:4 * T], bias_col, scale,
                                            ALU.add, ALU.mult).then_inc(done, 1)
                if parts:
                    dve.wait_ge(done, 2)
                    link = Link(dve, done, 2)
                    link(nc.vector.tensor_copy(parts[0][:], q[:]))
                    link(nc.vector.tensor_tensor(q[:], q[:], parts[0][:], ALU.subtract))
                    link(nc.vector.tensor_copy(parts[1][:], q[:]))
                    link(nc.vector.tensor_tensor(parts[2][:], q[:], parts[1][:], ALU.subtract))

            @block.sync
            def _(sp):
                for a in range(3 if parts else 0):
                    sp.wait_ge(done, (3, 5, 6)[a])
                    for c in range(3):
                        to = q_dram[:, 24 * a + 8 * c:24 * a + 8 * c + 8, :].rearrange("b d (n t) -> (d n) b t", t=T)
                        sp.dma_start(to, parts[a][:].rearrange("p (b t) -> p b t", t=T)).then_inc(stored, 16)
                if parts:
                    sp.wait_ge(stored, 144)


def prefetch(nc, s, name, loads):
    ld = s.sem(f"{name}_prefetched")
    with nc.Block() as block:

        @block.sync
        def _(sp):
            for to, src in loads:
                sp.dma_start(to, src).then_inc(ld, 16)

    return ld, 16 * len(loads)


def arrived(nc, before):
    with nc.Block() as block:

        @block.sync
        def _(sp):
            sp.wait_ge(*before)


def load(nc, name, loads):
    with Scope(nc, name) as s:
        ld = s.sem("loaded")
        with nc.Block() as block:

            @block.sync
            def _(sp):
                for to, src in loads:
                    sp.dma_start(to, src).then_inc(ld, 16)
                sp.wait_ge(ld, 16 * len(loads))


def col(ap):
    return ap.rearrange("(p a) -> p a", a=1)


def fold_heads(nc, K, W, wqT, wkT, wvT, wout):
    jobs = [(W["qk"], wqT, wkT, 0.125), (W["vo"], wvT, wout, 1.0)]
    with Scope(nc, "fold") as s:
        ps = s.banks("f", 4)
        full, done = s.sem("full"), s.sem("done")
        with nc.Block() as block:

            @block.tensor
            def _(pe):
                n = 0
                for to, left, right, _ in jobs:
                    for h8 in range(0, NH, 8):
                        for odd in range(2):
                            if n >= 4:
                                pe.wait_ge(done, n - 3)
                            if n:
                                pe.wait_ge(full, n)
                            r = slice(64 * odd, 64 * odd + 64)
                            for x in range(4):
                                i_ = nc.tensor.matmul(ps[n % 4][:, x * D:(x + 1) * D], left[r, h8 // 2 + x, :],
                                                      right[r, h8 // 2 + x, :], start=True, stop=True)
                            i_.then_inc(full, 1)
                            n += 1

            @block.vector
            def _(dve):
                n = 0
                for to, _, _, scale in jobs:
                    for h8 in range(0, NH, 8):
                        for odd in range(2):
                            dve.wait_ge(full, n + 1)
                            to2 = to[:].rearrange("p (h o) d -> p h o d", o=2)[:, h8 // 2:h8 // 2 + 4, odd, :]
                            nc.vector.tensor_scalar(to2, ps[n % 4][:].rearrange("p (h d) -> p h d", d=D),
                                                    scale, None, ALU.mult).then_inc(done, 1)
                            n += 1


def head_outputs(nc, K, name, wo, to, by_dim):
    with Scope(nc, name) as s:
        done = s.sem("done")
        with nc.Block() as block:

            @block.vector
            def _(dve):
                for j in range(4):
                    nc.vector.tensor_scalar(to[:, j, :], wo, K["jm"][:, j:j + 1], None, ALU.mult).then_inc(done, 1)
                for a, b, _ in by_dim:
                    for j in range(4):
                        nc.vector.tensor_copy(a.rearrange("p (d j g) -> p j g d", j=4, g=4)[:, j],
                                              b.rearrange("p (g j d) -> p j g d", j=4, g=4)[:, j]).then_inc(done, 1)
                link = Link(dve, done, 4 + 4 * len(by_dim))
                dve.wait_ge(done, link.base)
                for a, _, column in by_dim:
                    if column is not None:
                        link(nc.vector.tensor_tensor(a, a, K["ident"][:], ALU.mult))
                        link(nc.vector.tensor_reduce(column, a, AX.X, ALU.add))


def route(nc, K, kind, XT, wr, gates, gate_bias=None):
    E = wr.shape[-1]
    with Scope(nc, f"route{kind}") as s:
        lg_ps, cnt_ps = s.banks("lg", 1)[0], s.banks("cnt", 1)[0]
        sc, ch, sel = s.sb("scores", [T, B, E]), s.sb("choice", [T, B, E]), s.sb("chosen", [T, B, E])
        top = s.sb("top", [T, B, 8])
        r1 = s.sb("r1", [T, B])
        full, act_done, order, cnt = s.sem("full"), s.sem("act_done"), s.sem("dve_order"), s.sem("counted")
        sel_ready = s.sem("chosen_ready")
        v = nc.vector

        def per_token(ap):
            return ap.rearrange("t (b a) -> t b a", a=1).broadcast_to([T, B, E])

        def rank_below(link, x, lt, n, groups, k, out, cmp, eq):
            a = x.rearrange("t (b g a) -> t b g a", g=n, a=1).broadcast_to([T, groups, n, n])
            b_ = x.rearrange("t (b a j) -> t b a j", a=1, j=n).broadcast_to([T, groups, n, n])
            m = lt.rearrange("t (a g) j -> t a g j", a=1).broadcast_to([T, groups, n, n])
            link(v.tensor_tensor(cmp, b_, a, ALU.is_gt))
            link(v.tensor_tensor(eq, b_, a, ALU.is_equal))
            link(v.tensor_tensor(eq, eq, m, ALU.mult))
            link(v.tensor_tensor(cmp, cmp, eq, ALU.add))
            link(v.tensor_reduce(out, cmp, AX.X, ALU.add))
            link(v.tensor_scalar(out, out, k - 0.5, None, ALU.is_lt))

        if kind == 2:
            top2 = s.sb("top2", [T, B, 4, 8])
            gs, gm = s.sb("group_score", [T, B * 4]), s.sb("group_mask", [T, B * 4])
            cmp, eq = s.sb("cmp", [T, B, 4, 4]), s.sb("eq", [T, B, 4, 4])
            mrep = s.sb("replaced", [T, B, E])
        if kind == 3:
            cmp, eq = s.sb("cmp", [T, B, E, E]), s.sb("eq", [T, B, E, E])
            before = s.sb("before", [T, B, E])
        with nc.Block() as block:

            @block.tensor
            def _(pe):
                for b in range(B):
                    i_ = nc.tensor.matmul(lg_ps[0:T, b * E:(b + 1) * E], XT[:, b * T:(b + 1) * T], wr, start=True,
                                          stop=True)
                i_.then_inc(full, 1)
                if kind == 3:
                    pe.wait_ge(sel_ready, 1)
                    nc.tensor.matmul(cnt_ps[0:T, 0:B * E], K["tri"][:], sel[:].rearrange("t b e -> t (b e)"),
                                     start=True, stop=False)
                    nc.tensor.matmul(cnt_ps[0:T, 0:B * E], K["ones"][:], before[:].rearrange("t b e -> t (b e)"),
                                     start=False, stop=True).then_inc(cnt, 1)

            @block.scalar
            def _(act):
                if kind == 2:
                    act.wait_ge(full, 1)
                    nc.scalar.activation(sc[:].rearrange("t b e -> t (b e)"), lg_ps[0:T, 0:B * E],
                                         ACT.Sigmoid).then_inc(act_done, 1)
                elif kind == 3:
                    act.wait_ge(order, 2)
                    nc.scalar.activation(ch[:], ch[:], ACT.Exp).then_inc(act_done, 1)
                else:
                    act.wait_ge(order, B + 1 + 1)
                    nc.scalar.activation(r1[:], r1[:], ACT.Exp).then_inc(act_done, 1)

            @block.vector
            def _(dve):
                link = Link(dve, order)
                lg = lg_ps[0:T, 0:B * E].rearrange("t (b e) -> t b e", e=E)
                if kind == 0:
                    dve.wait_ge(full, 1)
                    link(v.tensor_copy(sc[:], lg))
                    for b in range(B):
                        link(v.max(top[:, b, :], sc[:, b, :]))
                    link(v.tensor_tensor(r1[:], top[:, :, 1], top[:, :, 0], ALU.subtract))
                    dve.wait_ge(act_done, 1)
                    link(v.tensor_scalar(r1[:], r1[:], 1.0, None, ALU.add))
                    link(v.reciprocal(r1[:], r1[:]))
                    link(v.tensor_scalar(r1[:], r1[:], 1.0, None, ALU.is_ge))
                    link(v.tensor_tensor(sel[:], sc[:], top[:, :, 0:1].broadcast_to([T, B, E]), ALU.is_ge))
                    link(v.tensor_tensor(gates[:], sel[:], per_token(r1[:]), ALU.mult))
                if kind == 2:
                    dve.wait_ge(act_done, 1)
                    gb = gate_bias.rearrange("t (a e) -> t a e", a=1).broadcast_to([T, B, E])
                    link(v.tensor_tensor(ch[:], sc[:], gb, ALU.add))
                    for b in range(B):
                        for g in range(4):
                            i_ = v.max(top2[:, b, g, :], ch[:, b, 8 * g:8 * g + 8])
                            i_.then_inc(order, 1)
                            link.n += 1
                    dve.wait_ge(order, link.n)
                    link(v.tensor_tensor(gs[:].rearrange("t (b g) -> t b g", g=4), top2[:, :, :, 0],
                                         top2[:, :, :, 1], ALU.add))
                    rank_below(link, gs[:], K["lt4"][0:T], 4, B, 2, gm[:].rearrange("t (b g) -> t b g", g=4),
                               cmp[:], eq[:])
                    link(v.tensor_tensor(ch[:].rearrange("t b (g e) -> t (b g) e", e=8),
                                         ch[:].rearrange("t b (g e) -> t (b g) e", e=8),
                                         gm[:].rearrange("t (g a) -> t g a", a=1).broadcast_to([T, B * 4, 8]), ALU.mult))
                    for b in range(B):
                        link(v.max(top[:, b, :], ch[:, b, :]))
                        link(v.match_replace(out=mrep[:, b, :], in_to_replace=top[:, b, :], in_values=ch[:, b, :],
                                             imm_value=-1e30))
                    link(v.tensor_tensor(sel[:], mrep[:], ch[:], ALU.not_equal))
                    link(v.tensor_tensor(sc[:], sc[:], sel[:], ALU.mult))
                    link(v.tensor_reduce(r1[:], sc[:], AX.X, ALU.add))
                    link(v.tensor_scalar(r1[:], r1[:], 1e-20, None, ALU.add))
                    link(v.reciprocal(r1[:], r1[:]))
                    link(v.tensor_scalar(r1[:], r1[:], 2.5, None, ALU.mult))
                    link(v.tensor_tensor(gates[:], sc[:], per_token(r1[:]), ALU.mult))
                if kind == 3:
                    dve.wait_ge(full, 1)
                    link(v.tensor_reduce(r1[:], lg, AX.X, ALU.max))
                    link(v.tensor_tensor(ch[:], lg, per_token(r1[:]), ALU.subtract))
                    dve.wait_ge(act_done, 1)
                    link(v.tensor_reduce(r1[:], ch[:], AX.X, ALU.add))
                    link(v.reciprocal(r1[:], r1[:]))
                    link(v.tensor_tensor(sc[:], ch[:], per_token(r1[:]), ALU.mult))
                    rank_below(link, sc[:].rearrange("t b e -> t (b e)"), K["lt8"][0:T], 8, B, 2, sel[:], cmp[:], eq[:])
                    link(v.memset(before[:, 0, :], 0.0))
                    for b in range(1, B):
                        link(v.tensor_tensor(before[:, b, :], before[:, b - 1, :], sel[:, b - 1, :], ALU.add))
                    v.memset(ch[:], 0.0).then_inc(sel_ready, 1)
                    link(v.tensor_tensor(sc[:], sc[:], sel[:], ALU.mult))
                    dve.wait_ge(cnt, 1)
                    link(v.tensor_scalar(sel[:].rearrange("t b e -> t (b e)"), cnt_ps[0:T, 0:B * E], 511.5, None, ALU.is_lt))
                    link(v.tensor_tensor(gates[:], sc[:], sel[:], ALU.mult))


def ffn(nc, K, kind, XT, units, width, rows, down, gates=None):
    NU, NCK = len(units), len(rows)
    X = K["X"]
    gate = K["gate"][0:T, 4 + kind:5 + kind]
    act_fn = ACT.Relu if kind == 0 else ACT.Silu
    NG = sum(u[4] is not None for u in units)
    groups = [list(range(c, min(c + 4, NCK))) for c in range(0, NCK, 4)]
    ring = Ring([(k, "v" if len(groups) == 1 or k % 2 else "a") for k in range(len(groups))])
    NQ = 16
    with Scope(nc, f"ffn{kind}") as s:
        xT = [s.sb(f"xT{i}", [P, T]) for i in range(2)]
        h = [s.sb(f"h{i}", [T, width]) for i in range(2)]
        hT = s.sb("hT", [P, NCK, T])
        sg = [s.sb(f"act{i}", [T, 512]) for i in range(2)]
        q = quant_buffers(s, T, width) if kind == 1 else None
        a_ps, g_ps = s.banks("a", 2), s.banks("g", 2)
        t_ps, out_ps = s.banks("t", 2), s.banks("o", 1)[0]
        ready = s.sem("ready")
        x_ready = s.sem("x_ready")
        up_full = s.sem("up_full")
        act_ready = s.sem("act_ready")
        h_ready = s.sem("h_ready")
        h_gated = s.sem("h_gated")
        h_round = s.sem("h_rounded")
        ring_full, act_out, dve_out = s.sem("ring_full"), s.sem("act_emptied"), s.sem("dve_emptied")
        out_full, x_done = s.sem("out_full"), s.sem("x_done")
        out_of = {"a": act_out, "v": dve_out}
        with nc.Block() as block:

            @block.tensor
            def _(pe):
                def up(load_no, nxt):
                    pe.wait_ge(x_ready, load_no + 1)
                    for u, (wa, wg, _, n, _) in enumerate(units):
                        if u >= 2:
                            pe.wait_ge(h_ready, load_no * NU + (u - 1))
                        elif not isinstance(load_no, int):
                            pe.wait_ge(h_ready, load_no * NU)
                        i_ = nc.tensor.matmul(a_ps[u % 2][0:T, 0:n], xT[nxt][:], wa, start=True, stop=True)
                        if wg is not None:
                            i_ = nc.tensor.matmul(g_ps[u % 2][0:T, 0:n], xT[nxt][:], wg, start=True, stop=True)
                        i_.then_inc(up_full, 1)

                pe.wait_ge(ready, 1)
                up(0, 0)
                with pe.Fori(0, B // 2) as i:
                    for par in range(2):
                        n = i * 2 + par
                        up(n + 1, 1 - par)
                        pe.wait_ge(h_ready, (n + 1) * NU)
                        if NG:
                            pe.wait_ge(h_gated, (n + 1) * NG)
                        if kind == 1:
                            pe.wait_ge(h_round, (n + 1) * NQ)
                        for k, ch in enumerate(groups):
                            if k >= 2:
                                prev, e = ring.jobs[k - 2]
                                pe.wait_ge(out_of[e], ring.emptied(n, prev, e))
                            for x, c in enumerate(ch):
                                i_ = nc.tensor.transpose(t_ps[k % 2][0:rows[c], x * T:(x + 1) * T],
                                                         h[par][:, sum(rows[:c]):sum(rows[:c + 1])], K["ident"][0:T, 0:T])
                            i_.then_inc(ring_full, 1)
                        for k, ch in enumerate(groups):
                            pe.wait_ge(out_of[ring.engine(k)], ring.emptied(n, k, ring.engine(k)))
                            if k == 0:
                                pe.wait_ge(x_done, n + len(t_ps))
                            for c in ch:
                                i_ = nc.tensor.matmul(out_ps[0:T, 0:D], hT[0:rows[c], c, :], down[0:rows[c], c, :],
                                                      start=(c == 0), stop=(c == NCK - 1))
                        i_.then_inc(out_full, 1)

            def empty(eng, copy, n, e, done):
                for k, ch in enumerate(groups):
                    if ring.engine(k) == e:
                        eng.wait_ge(ring_full, ring.full(n, k))
                        copy(hT[:, ch[0]:ch[0] + len(ch), :],
                             t_ps[k % 2][:, 0:len(ch) * T].rearrange("p (c t) -> p c t", t=T)).then_inc(done, 1)

            @block.scalar
            def _(act):
                def first_half(load_no, b, nxt):
                    nc.scalar.copy(xT[nxt][:], XT[:, bass.ds(b * T, T)]).then_inc(x_ready, 1)
                    for u, (_, _, _, n, _) in enumerate(units):
                        act.wait_ge(up_full, load_no * NU + (u + 1))
                        if u >= 2:
                            act.wait_ge(h_ready, load_no * NU + (u - 1))
                        elif not isinstance(load_no, int):
                            act.wait_ge(h_ready, load_no * NU)
                        nc.scalar.activation(sg[u % 2][:, 0:n], a_ps[u % 2][0:T, 0:n], act_fn).then_inc(act_ready, 1)

                act.wait_ge(ready, 1)
                first_half(0, 0, 0)
                with act.Fori(0, B // 2) as i:
                    for par in range(2):
                        n = i * 2 + par
                        first_half(n + 1, (n + 1) % B, 1 - par)
                        empty(act, nc.scalar.copy, n, "a", act_out)

            @block.vector
            def _(dve):
                v = nc.vector

                def products(load_no, b, nxt):
                    gated = 0
                    for u, (_, wg, c0, n, e) in enumerate(units):
                        dve.wait_ge(act_ready, load_no * NU + (u + 1))
                        hu = h[nxt][:, c0:c0 + n]
                        v.tensor_tensor(hu, sg[u % 2][:, 0:n], sg[u % 2][:, 0:n] if wg is None else g_ps[u % 2][0:T, 0:n],
                                        ALU.mult).then_inc(h_ready, 1)
                        if e is not None:
                            dve.wait_ge(h_ready, load_no * NU + (u + 1))
                            ne = e[1] - e[0]
                            w = gates[:, b, e[0]:e[1]].rearrange("t (e a) -> t e a", a=1).broadcast_to([T, ne, n // ne])
                            hv = hu.rearrange("t (e f) -> t e f", e=ne)
                            v.tensor_tensor(hv, hv, w, ALU.mult).then_inc(h_gated, 1)
                    if kind == 1:
                        dve.wait_ge(h_ready, (load_no + 1) * NU)
                        link = Link(dve, h_round, load_no * NQ)
                        fp4_round(nc, link, q, h[nxt][:], h[nxt][:])
                        assert link.n == NQ

                for n, t in enumerate(t_ps):
                    v.memset(t[:], 0.0).then_inc(x_done, 1)
                dve.wait_ge(x_done, 2)
                v.memset(sg[0][:, 0:1], 0.0).then_inc(ready, 1)
                products(0, 0, 0)
                with dve.Fori(0, B // 2) as i:
                    for par in range(2):
                        n = i * 2 + par
                        products(n + 1, (n + 1) % B, 1 - par)
                        empty(dve, v.tensor_copy, n, "v", dve_out)
                        dve.wait_ge(out_full, n + 1)
                        v.scalar_tensor_tensor(out=X[:, n, :], in0=out_ps[0:T, 0:D], scalar=gate, in1=X[:, n, :],
                                               op0=ALU.mult, op1=ALU.add).then_inc(x_done, 1)


def layer0(nc, K, ins, ctxT_dram):
    with Scope(nc, "L0f") as s:
        up, down, wr = s.sb("up", [P, 576]), s.sb("down", [P, 5, D]), s.sb("wr", [P, 8])
        weights = [
            (up[:, 0:512].rearrange("d (e f) -> d e f", e=8), ins["L0_ffn_W1"].rearrange("e d f -> d e f")),
            (up[:, 512:576], ins["L0_ffn_Ws1"]), (wr[:], ins["L0_ffn_Wr"]),
            (down[:, 0:4, :], ins["L0_ffn_W2"].rearrange("e f d -> (e f) d").rearrange("(c p) d -> p c d", p=P)),
            (down[0:64, 4, :], ins["L0_ffn_Ws2"])]
        layer0_attention(nc, K, ins, ctxT_dram, lambda: prefetch(nc, s, "ffn", weights))
        XN, XT, gates = s.sb("XN", [T, B, D]), s.sb("XT", [P, B * T]), s.sb("gates", [T, B, 8])
        normalise(nc, K, "ln0f", XN, XT)
        route(nc, K, 0, XT, wr[:], gates)
        ffn(nc, K, 0, XT, [(up[:, 0:512], None, 0, 512, (0, 8)), (up[:, 512:576], None, 512, 64, None)], 576,
            [P] * 4 + [64], down, gates)


def layer0_attention(nc, K, ins, ctxT_dram, start_prefetch):
    with Scope(nc, "L0a") as s:
        W = {"qk": s.sb("qk", [P, NH, D]), "vo": s.sb("vo", [P, NH, D]), "g1": s.sb("g1", [P, D]),
             "b1": s.sb("b1", [P, D]), "lat": s.sb("lat", [T, B, D]), "latT": s.sb("latT", [P, B * T])}
        with Scope(nc, "L0w") as w:
            wq, wkv, wout = w.sb("wq", [P, 1024]), w.sb("wkv", [P, 2048]), w.sb("wout", [P, 8, D])
            wqT, wkT, wvT = w.sb("wqT", [P, 8, D]), w.sb("wkT", [P, 8, D]), w.sb("wvT", [P, 8, D])
            jobs = []
            for n in range(8):
                jobs.append((wqT[:, n, :], wq[:, n * D:(n + 1) * D]))
                jobs.append((wkT[:, n, :], wkv[:, n * D:(n + 1) * D]))
                jobs.append((wvT[:, n, :], wkv[:, 1024 + n * D:1024 + (n + 1) * D]))
            transposes(nc, K, "L0t", jobs, [
                (wq[:], ins["L0_xattn_Wq"]), (wkv[:], ins["L0_xattn_Wkv"]),
                (wout[:], ins["L0_xattn_Wout"].rearrange("(n p) d -> p n d", p=P)),
                (W["g1"][:], bcast_rows(ins["L0_xattn_g1"], P, D)), (W["b1"][:], bcast_rows(ins["L0_xattn_b1"], P, D))])
            fold_heads(nc, K, W, wqT, wkT, wvT, wout)
        normalise(nc, K, "ln0a", W["lat"], W["latT"], affine=(ins["L0_xattn_g2"], ins["L0_xattn_b2"]))
        before = start_prefetch()
        attention(nc, K, 0, W, ins, ctxT_dram)
        arrived(nc, before)


def plain_attention(nc, K, kind, ins, ctxT_dram, names, turned):
    wq_n, wk_n, wv_n, wo_n, bq_n, bk_n, bv_n, bo_n = names
    with Scope(nc, f"L{kind}a") as s:
        wq, wk, wv, wo = (s.sb(n, [P, D]) for n in ("wq", "wk", "wv", "wo"))
        W = {"k": wk, "v": wv, "bk": s.sb("bk", [P, 1]), "bv": s.sb("bv", [P, D]), "bo": s.sb("bo", [P, D]),
             "q": s.sb("q", [P, B * T]), "o": s.sb("o", [P, 4, D])}
        bq = s.sb("bq", [P, 1])
        rows = {t: s.sb(f"{t}_row", [P, D]) for t in ("bq", "bk")}
        small = [(rows["bq"][:], bcast_rows(ins[bq_n], P, D)), (rows["bk"][:], bcast_rows(ins[bk_n], P, D)),
                 (W["bv"][:], bcast_rows(ins[bv_n], P, D)),
                 (W["bo"][:], bcast_rows(ins[bo_n], P, D))]
        if turned:
            with Scope(nc, f"L{kind}aw") as w:
                raw = [w.sb(n, [P, D]) for n in ("q", "k", "v", "o")]
                to = [wq[:], wk[:], wv[:], wo[:]]
                transposes(nc, K, f"L{kind}at", [(t, r[:]) for t, r in zip(to, raw)],
                           [(r[:], ins[n]) for r, n in zip(raw, (wq_n, wk_n, wv_n, wo_n))] + small)
        else:
            load(nc, f"L{kind}l", [(t[:], ins[n]) for t, n in zip((wq, wk, wv, wo), (wq_n, wk_n, wv_n, wo_n))] + small)
        wqd, wkd = s.sb("wqd", [P, D]), s.sb("wkd", [P, D])
        head_outputs(nc, K, f"ho{kind}", wo[:], W["o"],
                     [(wqd[:], wq[:], None), (wkd[:], wk[:], None),
                      (s.sb("bq_by", [P, D])[:], rows["bq"][:], bq[:]), (s.sb("bk_by", [P, D])[:], rows["bk"][:], W["bk"][:])])
        W["k"], wq = wkd, wqd
        W["q_dram"] = nc.dram_tensor(f"q{kind}", [B, 72, NH * T], BF16, kind="Internal").ap()
        W["k_dram"] = nc.dram_tensor(f"k{kind}", [2, 3, P, S2], BF16, kind="Internal").ap()
        with Scope(nc, f"L{kind}an") as n_:
            XN, XT = n_.sb("XN", [T, B, D]), n_.sb("XT", [P, B * T])
            normalise(nc, K, f"ln{kind}a", XN, XT)
            queries(nc, K, f"q{kind}", wq[:], bq[:, 0:1], float(D // NH) ** -0.5, XT, W["q"],
                    W["q_dram"])
        attention(nc, K, kind, W, ins, ctxT_dram)


def layer3_attention(nc, K, ins, ctxT_dram):
    widths, at = [482, 482, 480], [0, 482, 964]
    ident, X, gate = K["ident"], K["X"], K["gate"][0:T, 3:4]
    with Scope(nc, "L3a") as s:
        wqT, woT, wvo = s.sb("wqT", [P, D]), s.sb("woT", [P, D]), s.sb("wvo", [P, D])
        raw = [s.sb(f"{n}_raw", [P, D]) for n in ("q", "k", "v", "o")]
        bq, bv, bo, q = s.sb("bq", [P, 1]), s.sb("bv", [P, 1]), s.sb("bo", [P, D]), s.sb("q", [P, B * T])
        transposes(nc, K, "L3at", [(wqT[:], raw[0][:]), (woT[:], raw[3][:])],
                   [(r[:], ins[f"L3_xattn_W{n}"]) for r, n in zip(raw, "qkvo")]
                   + [(bq[:], col(ins["L3_xattn_bq"])), (bv[:], col(ins["L3_xattn_bv"])),
                      (bo[:], bcast_rows(ins["L3_xattn_bo"], P, D))])
        with Scope(nc, "L3an") as n_:
            XN, XT, qe = n_.sb("XN", [T, B, D]), n_.sb("XT", [P, B * T]), n_.sb("qe", [P, B * T])
            normalise(nc, K, "ln3a", XN, XT)
            queries(nc, K, "q3", wqT[:], bq[:, 0:1], float(D) ** -0.5, XT, qe)
            f_ps = n_.banks("f", 4)
            full, done = n_.sem("full"), n_.sem("done")
            with nc.Block() as block:

                @block.tensor
                def _(pe):
                    for n in range(2):
                        nc.tensor.matmul(f_ps[n][:, 0:4 * T], raw[1][:], qe[:, n * 4 * T:(n + 1) * 4 * T],
                                         start=True, stop=True).then_inc(full, 1)
                    nc.tensor.matmul(f_ps[2][:, 0:D], raw[2][:], woT[:], start=True, stop=True).then_inc(full, 1)
                    nc.tensor.matmul(f_ps[3][:, 0:D], bv[:, 0:1].broadcast_to([P, P]), woT[:], start=True,
                                     stop=True).then_inc(full, 1)

                @block.vector
                def _(dve):
                    for n in range(2):
                        dve.wait_ge(full, n + 1)
                        nc.vector.tensor_copy(q[:, n * 4 * T:(n + 1) * 4 * T], f_ps[n][:, 0:4 * T]).then_inc(done, 1)
                    dve.wait_ge(full, 3)
                    nc.vector.tensor_copy(wvo[:], f_ps[2][:, 0:D]).then_inc(done, 1)
                    dve.wait_ge(full, 4)
                    nc.vector.tensor_tensor(bo[:], bo[:], f_ps[3][:, 0:D], ALU.add).then_inc(done, 1)

        with Scope(nc, "attn3") as s_:
            sb, sem = s_.sb, s_.sem
            kT = [sb(f"kT{i}", [P, S2]) for i in range(2)]
            V = [sb(f"V{i}", [KC, NC_CTX, D]) for i in range(2)]
            qb = [sb(f"q{i}", [P, T]) for i in range(2)]
            prob = [sb(f"prob{i}", [T, S2]) for i in range(2)]
            pT = [sb(f"pT{i}", [KC, NC_CTX, T]) for i in range(2)]
            mpart, dparts, nmax = sb("mpart", [T, 2, 3]), sb("dparts", [T, 2, 3]), sb("nmax", [T, 2])
            den, rden, y, yT, upd = (sb("den", [T, 2]), sb("rden", [T, 2]), sb("y", [T, D]), sb("yT", [P, T]),
                                     sb("upd", [T, D]))
            s_ps, t_ps = s_.banks("score", 3), s_.banks("t", 3)
            av_ps, o_ps = s_.banks("av", 1)[0], s_.banks("out", 1)[0]
            before = sb("before", [P, 2])
            ready = sem("ready")
            k_loaded = [sem(f"k_loaded{i}") for i in range(2)]
            v_loaded = [sem(f"v_loaded{i}") for i in range(2)]
            q_ready = sem("q_ready")
            score_full, score_out = sem("score_full"), sem("max_parts")
            max_ready, prob_ready = sem("max_ready"), sem("prob_ready")
            t_full, act_out, dve_out = sem("t_full"), sem("act_emptied"), sem("dve_emptied")
            av_full, y_ready, yT_full, yT_ready = sem("av_full"), sem("y_ready"), sem("yT_full"), sem("yT_ready")
            out_full, upd_ready, x_done, rden_ready = (sem("out_full"), sem("update_ready"), sem("x_done"),
                                                       sem("rden_ready"))
            with nc.Block() as block:

                @block.sync
                def _(sp):
                    def load_k(b, k):
                        sp.dma_start(kT[k][:], ctxT_dram[b]).then_inc(k_loaded[k], 16)

                    def load_v(b, k):
                        n = (NC_CTX - 1) * KC
                        sp.dma_start(V[k][:, 0:NC_CTX - 1, :],
                                     ins["ctx_1024"][b, 0:n, :].rearrange("(c p) d -> p c d", p=KC)).then_inc(v_loaded[k], 16)
                        sp.dma_start(V[k][0:LAST, NC_CTX - 1, :], ins["ctx_1024"][b, n:S2, :]).then_inc(v_loaded[k], 16)

                    for k in range(2):
                        load_k(k, k)
                    for k in range(2):
                        load_v(k, k)
                    with sp.Fori(0, B // 2) as i:
                        for par in range(2):
                            n = i * 2 + par
                            b2 = sp.snap((n + 2) % B)
                            wait_apart(sp, q_ready, score_full, n * 3 + 3)
                            load_k(b2, par)
                            wait_apart(sp, q_ready, av_full, n + 1)
                            load_v(b2, par)
                    for k in range(2):
                        sp.wait_ge(k_loaded[k], (B // 2 + 1) * 16)
                        sp.wait_ge(v_loaded[k], (B // 2 + 1) * 32)

                @block.tensor
                def _(pe):
                    def scores(i, par, step):
                        pe.wait_ge(k_loaded[par], i * 16 + 16)
                        pe.wait_ge(q_ready, step + 1)
                        for u in range(3):
                            if not isinstance(step, int):
                                pe.wait_ge(prob_ready, step * 3 + (u - 2))
                            nc.tensor.matmul(s_ps[u][0:T, 0:widths[u]], qb[par][:], kT[par][:, at[u]:at[u] + widths[u]],
                                             start=True, stop=True).then_inc(score_full, 1)

                    pe.wait_ge(ready, 1)
                    scores(0, 0, 0)
                    with pe.Fori(0, B // 2) as i:
                        for par in range(2):
                            n = i * 2 + par
                            scores(i + par, 1 - par, n + 1)
                            pe.wait_ge(prob_ready, n * 3 + 3)
                            for k in range(3):
                                pe.wait_ge(dve_out if k == 1 else act_out, n * (1 if k == 1 else 2) + (k // 2 + 1))
                                for x, c in enumerate(range(4 * k, 4 * k + 4)):
                                    kc, c0 = chunk_rows(c), chunk_at(c)
                                    i_ = nc.tensor.transpose(t_ps[k][0:kc, x * T:(x + 1) * T], prob[par][:, c0:c0 + kc],
                                                             ident[0:T, 0:T])
                                i_.then_inc(t_full, 1)
                            for k in range(3):
                                pe.wait_ge(dve_out if k == 1 else act_out, n * (1 if k == 1 else 2) + (2 if k == 1 else 3 + k // 2))
                                if k == 0:
                                    pe.wait_ge(v_loaded[par], i * 32 + 32)
                                    pe.wait_ge(y_ready, n + 1)
                                for c in range(4 * k, 4 * k + 4):
                                    kc = chunk_rows(c)
                                    i_ = nc.tensor.matmul(av_ps[0:T, 0:D], pT[par][0:kc, c, :], V[par][0:kc, c, :],
                                                          start=(c == 0), stop=(c == NC_CTX - 1))
                            i_.then_inc(av_full, 1)
                            pe.wait_ge(y_ready, n + 2)
                            pe.wait_ge(x_done, n + 1)
                            nc.tensor.transpose(o_ps[:, 0:T], y[:], ident[0:T, 0:T]).then_inc(yT_full, 1)
                            pe.wait_ge(yT_ready, n + 1)
                            nc.tensor.matmul(o_ps[0:T, P:P + D], yT[:], wvo[:], start=True, stop=True).then_inc(out_full, 1)

                @block.scalar
                def _(act):
                    def query(b, k, step):
                        if not isinstance(step, int):
                            act.wait_ge(score_full, step * 3 + 1)
                        nc.scalar.copy(qb[k][:], q[:, bass.ds(b * T, T)]).then_inc(q_ready, 1)

                    def expo(step, k):
                        act.wait_ge(max_ready, step + 1)
                        for u in range(3):
                            nc.scalar.activation(prob[k][:, at[u]:at[u] + widths[u]], s_ps[u][0:T, 0:widths[u]],
                                                 ACT.Exp, bias=nmax[:, k:k + 1],
                                                 accum_out=dparts[:, k, u:u + 1]).then_inc(prob_ready, 1)

                    act.wait_ge(ready, 1)
                    for _n in range(2):
                        nc.scalar.copy(before[:, _n:_n + 1], ident[:, 0:1]).then_inc(act_out, 1)
                    query(0, 0, 0)
                    expo(0, 0)
                    with act.Fori(0, B // 2) as i:
                        for par in range(2):
                            n = i * 2 + par
                            query((n + 1) % B, 1 - par, n)
                            for k in (0, 2):
                                act.wait_ge(t_full, n * 3 + (k + 1))
                                nc.scalar.copy(pT[par][:, 4 * k:4 * k + 4, :],
                                               t_ps[k][0:KC, 0:4 * T].rearrange("p (c t) -> p c t", t=T)).then_inc(act_out, 1)
                            expo(n + 1, 1 - par)

                @block.vector
                def _(dve):
                    v = nc.vector

                    def masked(step, k):
                        for u in range(3):
                            dve.wait_ge(score_full, step * 3 + (u + 1))
                            v.tensor_reduce(mpart[:, k, u:u + 1], s_ps[u][0:T, 0:widths[u]], AX.X,
                                            ALU.max).then_inc(score_out, 1)
                        dve.wait_ge(score_out, step * 3 + 3)
                        v.tensor_reduce(nmax[:, k:k + 1], mpart[:, k, :], AX.X, ALU.max, negate=True).then_inc(max_ready, 1)

                    for t in t_ps:
                        v.memset(t[:], 0.0).then_inc(rden_ready, 1)
                    dve.wait_ge(rden_ready, 3)
                    v.memset(upd[:, 3:4], 0.0).then_inc(ready, 1)
                    v.memset(upd[:, 0:1], 0.0).then_inc(dve_out, 1)
                    v.memset(upd[:, 1:2], 0.0).then_inc(y_ready, 1)
                    v.memset(upd[:, 2:3], 0.0).then_inc(x_done, 1)
                    masked(0, 0)
                    with dve.Fori(0, B // 2) as i:
                        for par in range(2):
                            n = i * 2 + par
                            masked(n + 1, 1 - par)
                            dve.wait_ge(t_full, n * 3 + 2)
                            v.tensor_copy(pT[par][:, 4:8, :],
                                          t_ps[1][0:KC, 0:4 * T].rearrange("p (c t) -> p c t", t=T)).then_inc(dve_out, 1)
                            dve.wait_ge(prob_ready, n * 3 + 3)
                            v.tensor_reduce(den[:, par:par + 1], dparts[:, par, :], AX.X, ALU.add).then_inc(rden_ready, 1)
                            dve.wait_ge(rden_ready, n * 2 + 4)
                            v.reciprocal(rden[:, par:par + 1], den[:, par:par + 1]).then_inc(rden_ready, 1)
                            dve.wait_ge(rden_ready, n * 2 + 5)
                            dve.wait_ge(av_full, n + 1)
                            v.tensor_scalar(y[:], av_ps[0:T, 0:D], rden[:, par:par + 1], None, ALU.mult).then_inc(y_ready, 1)
                            dve.wait_ge(yT_full, n + 1)
                            v.tensor_copy(yT[:], o_ps[:, 0:T]).then_inc(yT_ready, 1)
                            dve.wait_ge(out_full, n + 1)
                            v.tensor_tensor(upd[:], o_ps[0:T, P:P + D], bo[0:T, :], ALU.add).then_inc(upd_ready, 1)
                            dve.wait_ge(upd_ready, n + 1)
                            v.scalar_tensor_tensor(out=X[:, n, :], in0=upd[:], scalar=gate, in1=X[:, n, :],
                                                   op0=ALU.mult, op1=ALU.add).then_inc(x_done, 1)


def layer1(nc, K, ins, ctxT_dram, names):
    I = 352
    rows = [128, 128, 96]
    with Scope(nc, "L1f") as s:
        raw, rawd = s.sb("raw", [P, 6, D]), s.sb("rawd", [P, I])
        loads = [(rawd[:], ins["L1_ffn_w_down"])]
        for m, name in enumerate(("L1_ffn_w_gate", "L1_ffn_w_up")):
            loads += [(raw[0:r, 3 * m + c, :], ins[name][c * P:c * P + r, :]) for c, r in enumerate(rows)]
        before = prefetch(nc, s, "ffn", loads)
        plain_attention(nc, K, 1, ins, ctxT_dram, names, False)
        up, down = s.sb("up", [P, 2, I]), s.sb("down", [P, 3, D])
        XN, XT = s.sb("XN", [T, B, D]), s.sb("XT", [P, B * T])
        jobs = [(up[:, m, c * P:c * P + r], raw[0:r, 3 * m + c, :]) for m in range(2) for c, r in enumerate(rows)]
        jobs += [(down[0:r, c, :], rawd[:, c * P:c * P + r]) for c, r in enumerate(rows)]
        transposes(nc, K, "L1t", jobs, (), [raw[:].rearrange("p c d -> p (c d)"), rawd[:]],
                   [raw[96:P, c, :] for c in (2, 5)], before)
        normalise(nc, K, "ln1f", XN, XT, quant=True)
        ffn(nc, K, 1, XT, [(up[:, 0, :], up[:, 1, :], 0, I, None)], I, rows, down)


def layer2(nc, K, ins, ctxT_dram, names):
    E, I = 32, 64
    N = E * I // P
    with Scope(nc, "L2w") as w:
        rg, ru, rd, rr = w.sb("rg", [P, N + 1, D]), w.sb("ru", [P, N + 1, D]), w.sb("rd", [P, N + 1, P]), w.sb("rr", [E, D])
        gb = w.sb("gb", [T, E])
        loads = [(rr[:], ins["L2_ffn_gate_w"]), (gb[:], bcast_rows(ins["L2_ffn_gate_bias"], T, E))]
        for raw, a in ((rg, "gate"), (ru, "up")):
            loads.append((raw[:, 0:N, :], ins[f"L2_ffn_expert_{a}"].rearrange("e i h -> (e i) h")
                          .rearrange("(c p) h -> p c h", p=P)))
            loads.append((raw[:, N, :], ins[f"L2_ffn_shared_{a}"]))
        loads.append((rd[:, 0:N, :].rearrange("h c (e i) -> h (c e) i", i=I),
                      ins["L2_ffn_expert_down"].rearrange("e h i -> h e i")))
        loads.append((rd[:, N, :], ins["L2_ffn_shared_down"]))
        before = prefetch(nc, w, "ffn", loads)
        plain_attention(nc, K, 2, ins, ctxT_dram, names, True)
        with Scope(nc, "L2f") as s:
            wg, wu = s.sb("wg", [P, N + 1, P]), s.sb("wu", [P, N + 1, P])
            down, wr = s.sb("down", [P, N + 1, D]), s.sb("wr", [P, E])
            gates, XT = s.sb("gates", [T, B, E]), s.sb("XT", [P, B * T])
            jobs = [(to[:, c, :], raw[:, c, :]) for to, raw in ((wg, rg), (wu, ru), (down, rd)) for c in range(N + 1)]
            jobs.append((wr[:], rr[:]))
            transposes(nc, K, "L2t", jobs, before=before)
            with Scope(nc, "L2n") as n_:
                XN = n_.sb("XN", [T, B, D])
                normalise(nc, K, "ln2f", XN, XT)
            route(nc, K, 2, XT, wr[:], gates, gb[:])
            flat = lambda t, c, n: t[:, c:c + n, :].rearrange("p c f -> p (c f)")
            units = [(flat(wg, 4 * k, 4), flat(wu, 4 * k, 4), 512 * k, 512, (8 * k, 8 * k + 8)) for k in range(4)]
            units.append((flat(wg, N, 1), flat(wu, N, 1), N * P, P, None))
            ffn(nc, K, 2, XT, units, (N + 1) * P, [P] * (N + 1), down, gates)


def layer3(nc, K, ins, ctxT_dram):
    E, F = 8, 192
    with Scope(nc, "L3f") as s:
        fc, down, wr = s.sb("fc", [P, E, 2 * F]), s.sb("down", [P, E * F // P, D]), s.sb("wr", [P, E])
        before = prefetch(nc, s, "ffn", [
            (fc[:], ins["L3_ffn_c_fc"].rearrange("e d f -> d e f")), (wr[:], ins["L3_ffn_w_gate"]),
            (down[:], ins["L3_ffn_c_proj"].rearrange("e f d -> (e f) d").rearrange("(c p) d -> p c d", p=P))])
        layer3_attention(nc, K, ins, ctxT_dram)
        arrived(nc, before)
        gates, XT, XN = s.sb("gates", [T, B, E]), s.sb("XT", [P, B * T]), s.sb("XN", [T, B, D])
        normalise(nc, K, "ln3f", XN, XT)
        route(nc, K, 3, XT, wr[:], gates)
        units = [(fc[:, 2 * k:2 * k + 2, 0:F], fc[:, 2 * k:2 * k + 2, F:2 * F], 2 * k * F, 2 * F, (2 * k, 2 * k + 2))
                 for k in range(E // 2)]
        ffn(nc, K, 3, XT, units, E * F, [P] * (E * F // P), down, gates)


def flamingo(nc, ins, out):
    with Scope(nc, "k") as s:
        K = {"X": s.sb("X", [T, B, D]), "gate": s.sb("gate", [P, 8]), "ident": s.sb("ident", [P, P]),
             "hm": s.sb("hm", [P, NH]), "jm": s.sb("jm", [P, 4]), "lt4": s.sb("lt4", [P, 4, 4]),
             "lt8": s.sb("lt8", [P, 8, 8]), "tri": s.sb("tri", [T, T]), "ones": s.sb("ones", [T, T]),
             "mhalf": s.sb("mhalf", [P, 16])}
        ctxT_dram = nc.dram_tensor("ctxT", [B, P, S2], F32, kind="Internal").ap()
        constants(nc, K, ins)
        load(nc, "x", [(K["X"][:], ins["x"].rearrange("b t d -> t b d"))])
        layer0(nc, K, ins, ctxT_dram)
        give_back(nc, Scope.used)
        n1 = [f"L1_xattn_{n}" for n in ("wq_k", "wk_k", "wv_k", "wo_k", "wq_b", "wk_b", "wv_b", "wo_b")]
        n2 = [f"L2_xattn_{n}" for n in ("Wq", "Wk", "Wv", "Wo", "bq", "bk", "bv", "bo")]
        layer1(nc, K, ins, ctxT_dram, n1)
        give_back(nc, Scope.used)
        layer2(nc, K, ins, ctxT_dram, n2)
        give_back(nc, Scope.used)
        layer3(nc, K, ins, ctxT_dram)
        load(nc, "y", [(out.rearrange("b t d -> t b d"), K["X"][:])])


_SKIP = ("fside_Bx16xSxS2_0",)


def kernel(**inputs):
    import concourse.bacc as bacc
    from concourse.bass_utils import run_bass_kernel_spmd

    nc = bacc.Bacc("TRN2", target_bir_lowering=False, num_devices=1)
    arrays, ins = {}, {}
    for name, a in inputs.items():
        if name in _SKIP:
            continue
        a = np.ascontiguousarray(a)
        arrays[f"in_{name}"] = a
        ins[name] = nc.dram_tensor(f"in_{name}", a.shape, mybir.dt.from_np(a.dtype), kind="ExternalInput").ap()
    out = nc.dram_tensor("out", [B, T, D], F32, kind="ExternalOutput").ap()
    flamingo(nc, ins, out)
    r = run_bass_kernel_spmd(nc, [arrays], core_ids=[0])
    return r.results[0]["out"]
```
